# Optimizing a Trainium2 kernel written in Bass

```python
import numpy as np
import jax
import jax.numpy as jnp

def _softmax(x, axis=-1):
    return jax.nn.softmax(x, axis=axis)

def _gelu(x):
    return jax.nn.gelu(x, approximate=True)

def _silu(x):
    return jax.nn.silu(x)

def _sigmoid(x):
    return jax.nn.sigmoid(x)

def _layernorm(x, axis=-1, eps=1e-05):
    m = jnp.mean(x, axis=axis, keepdims=True)
    v = jnp.var(x, axis=axis, keepdims=True)
    return (x - m) / jnp.sqrt(v + eps)

def _scatter_add(tgt, idx, src, axis=0):
    return tgt.at[idx].add(src)

def _segment_sum(src, seg, n):
    return jax.ops.segment_sum(src, seg, n)
kernel_name = 'mk_early_fusion_d1_tok_img2048_r4_0b6e7c'

def setup_inputs(seed: int=0):
    np.random.seed(seed)
    _w = jnp.asarray

    def _rec_inputs():
        import jax
        import jax.numpy as jnp
        _rk = jax.random.key(seed)
        x = -0.00340659 + 1.00146 * jax.random.normal(jax.random.fold_in(_rk, 1), (8, 256, 64, 2), jnp.float32)
        txt = 0.000411298 + 0.588087 * jax.random.normal(jax.random.fold_in(_rk, 2), (8, 128, 512), jnp.float32)
        return (x, txt)
    x, txt = _rec_inputs()

    def _L0_tok_setup():
        import jax, jax.numpy as jnp
        import numpy as np
        CH, H, N, N_SSM, SEQ_L = (1, 256, 64, 256, 512)

        def _kernel(C_ri, log_dt, B_ri, inv_A_real, A_imag, L):
            C = C_ri[..., 0] + 1j * C_ri[..., 1]
            B = B_ri[..., 0] + 1j * B_ri[..., 1]
            A = -jnp.exp(inv_A_real) + 1j * A_imag
            rep = log_dt.shape[0] // inv_A_real.shape[0]
            B = jnp.tile(B, (rep, 1))
            A = jnp.tile(A, (rep, 1))
            dt = jnp.exp(log_dt)
            dtA = A * dt[:, None]
            Ct = B[None] * C / (1.0 - dtA / 2) * dt[:, None]
            dA = (1.0 + dtA / 2) / (1.0 - dtA / 2)
            dA_log = jnp.log(dA)
            l = jnp.arange(L, dtype=jnp.float32)
            V = jnp.exp(dA_log[:, :, None] * l)
            K = 2.0 * jnp.einsum('chn,hnl->chl', Ct, V).real
            return K
        key = jax.random.key(seed)
        ks = jax.random.split(key, 5)
        return {'C_ri': jax.random.normal(ks[0], (CH, H, N, 2), dtype=jnp.float32), 'log_dt': jax.random.normal(ks[1], (H,), dtype=jnp.float32), 'B_ri': jax.random.normal(ks[2], (N_SSM, N, 2), dtype=jnp.float32), 'inv_A_real': jax.random.normal(ks[3], (N_SSM, N), dtype=jnp.float32), 'A_imag': jax.random.normal(ks[4], (N_SSM, N), dtype=jnp.float32), 'L': SEQ_L}
    _L0_tok_all = _L0_tok_setup()
    _L0_tok_in = {k: v for k, v in _L0_tok_all.items() if k in ('log_dt', 'B_ri', 'inv_A_real', 'A_imag')}
    del _L0_tok_all

    def _L0_attn_setup():
        import jax, jax.numpy as jnp
        import numpy as np
        B, S, H = (16, 128, 512)
        NH, NKV = (16, 4)
        HD = H // NH

        def _rope_tables(seq_len, dim, dtype):
            inv_freq = 1.0 / 10000.0 ** (jnp.arange(0, dim, 2, dtype=jnp.float32) / dim)
            t = jnp.arange(seq_len, dtype=jnp.float32)
            freqs = jnp.einsum('i,j->ij', t, inv_freq)
            emb = jnp.concatenate([freqs, freqs], axis=-1)
            cos = jnp.cos(emb)[None, None].astype(dtype)
            sin = jnp.sin(emb)[None, None].astype(dtype)
            return (cos, sin)

        def _rotate_half(x):
            x1, x2 = jnp.split(x, 2, axis=-1)
            return jnp.concatenate([-x2, x1], axis=-1)
        key = jax.random.key(seed)
        kx, kq, kk, kv, ko = jax.random.split(key, 5)
        x = jax.random.normal(kx, (B, S, H), dtype=jnp.float32)
        s = 0.02
        Wq = jax.random.normal(kq, (H, H), dtype=jnp.float32) * s
        Wk = jax.random.normal(kk, (NKV * HD, H), dtype=jnp.float32) * s
        Wv = jax.random.normal(kv, (NKV * HD, H), dtype=jnp.float32) * s
        Wo = jax.random.normal(ko, (H, H), dtype=jnp.float32) * s
        return {'x': x, 'Wq': Wq, 'Wk': Wk, 'Wv': Wv, 'Wo': Wo}
    _L0_attn_all = _L0_attn_setup()
    _L0_attn_in = {k: v for k, v in _L0_attn_all.items() if k in ('Wq', 'Wk', 'Wv', 'Wo')}
    del _L0_attn_all

    def _L0_ffn_setup():
        import jax, jax.numpy as jnp
        import numpy as np
        E, K, H, I = (64, 6, 512, 352)
        NS = 2
        IS = NS * I
        CAP = 64
        T_TOKENS = (1, 256)
        SCALE = 0.02

        def _moe_infer(x, gate_w, w_gate, w_up, w_down):
            T = x.shape[0]
            TK = T * K
            logits = x @ gate_w.T
            scores = jax.nn.softmax(logits, axis=-1)
            topk_w, topk_i = jax.lax.top_k(scores, K)
            flat_i = topk_i.reshape(-1)
            flat_w = topk_w.reshape(-1)
            token_ids = jnp.arange(TK, dtype=jnp.int32) // K
            order = jnp.argsort(flat_i)
            sorted_e = flat_i[order]
            counts = jnp.bincount(flat_i, length=E)
            starts = jnp.concatenate([jnp.zeros((1,), counts.dtype), jnp.cumsum(counts)[:-1]])
            pos_sorted = jnp.arange(TK) - starts[sorted_e]
            pos = jnp.zeros((TK,), jnp.int32).at[order].set(pos_sorted.astype(jnp.int32))
            valid = pos < CAP
            slot = jnp.where(valid, pos, CAP)
            buf = jnp.zeros((E, CAP + 1, H), x.dtype).at[flat_i, slot].set(x[token_ids])
            g = jnp.einsum('ech,ehi->eci', buf, w_gate)
            u = jnp.einsum('ech,ehi->eci', buf, w_up)
            y = jnp.einsum('eci,eih->ech', jax.nn.silu(g) * u, w_down)
            out_slots = y[flat_i, slot] * (flat_w * valid)[:, None]
            return out_slots.reshape(T, K, H).sum(axis=1)
        key = jax.random.key(seed)
        ks = jax.random.split(key, 8)
        f32 = jnp.float32
        return {'hidden_states': jax.random.normal(ks[0], (*T_TOKENS, H), f32), 'gate_w': jax.random.normal(ks[1], (E, H), f32) * SCALE, 'w_gate': jax.random.normal(ks[2], (E, H, I), f32) * SCALE, 'w_up': jax.random.normal(ks[3], (E, H, I), f32) * SCALE, 'w_down': jax.random.normal(ks[4], (E, I, H), f32) * SCALE, 'sw_gate': jax.random.normal(ks[5], (H, IS), f32) * SCALE, 'sw_up': jax.random.normal(ks[6], (H, IS), f32) * SCALE, 'sw_down': jax.random.normal(ks[7], (IS, H), f32) * SCALE}
    _L0_ffn_all = _L0_ffn_setup()
    _L0_ffn_in = {k: v for k, v in _L0_ffn_all.items() if k in ('gate_w', 'w_gate', 'w_up', 'w_down', 'sw_gate', 'sw_up', 'sw_down')}
    del _L0_ffn_all
    return {'x': x, 'txt': txt, 'L0_tok_log_dt': _L0_tok_in['log_dt'], 'L0_tok_B_ri': _L0_tok_in['B_ri'], 'L0_tok_inv_A_real': _L0_tok_in['inv_A_real'], 'L0_tok_A_imag': _L0_tok_in['A_imag'], 'L0_attn_Wq': _L0_attn_in['Wq'], 'L0_attn_Wk': _L0_attn_in['Wk'], 'L0_attn_Wv': _L0_attn_in['Wv'], 'L0_attn_Wo': _L0_attn_in['Wo'], 'L0_ffn_gate_w': _L0_ffn_in['gate_w'], 'L0_ffn_w_gate': _L0_ffn_in['w_gate'], 'L0_ffn_w_up': _L0_ffn_in['w_up'], 'L0_ffn_w_down': _L0_ffn_in['w_down'], 'L0_ffn_sw_gate': _L0_ffn_in['sw_gate'], 'L0_ffn_sw_up': _L0_ffn_in['sw_up'], 'L0_ffn_sw_down': _L0_ffn_in['sw_down']}

def reference(x, txt, L0_tok_log_dt, L0_tok_B_ri, L0_tok_inv_A_real, L0_tok_A_imag, L0_attn_Wq, L0_attn_Wk, L0_attn_Wv, L0_attn_Wo, L0_ffn_gate_w, L0_ffn_w_gate, L0_ffn_w_up, L0_ffn_w_down, L0_ffn_sw_gate, L0_ffn_sw_up, L0_ffn_sw_down):
    import jax
    import jax.numpy as jnp

    def _L0_tok_ref(C_ri, log_dt, B_ri, inv_A_real, A_imag, L):
        import jax, jax.numpy as jnp
        import numpy as np
        CH, H, N, N_SSM, SEQ_L = (1, 256, 64, 256, 512)

        def _kernel(C_ri, log_dt, B_ri, inv_A_real, A_imag, L):
            C = C_ri[..., 0] + 1j * C_ri[..., 1]
            B = B_ri[..., 0] + 1j * B_ri[..., 1]
            A = -jnp.exp(inv_A_real) + 1j * A_imag
            rep = log_dt.shape[0] // inv_A_real.shape[0]
            B = jnp.tile(B, (rep, 1))
            A = jnp.tile(A, (rep, 1))
            dt = jnp.exp(log_dt)
            dtA = A * dt[:, None]
            Ct = B[None] * C / (1.0 - dtA / 2) * dt[:, None]
            dA = (1.0 + dtA / 2) / (1.0 - dtA / 2)
            dA_log = jnp.log(dA)
            l = jnp.arange(L, dtype=jnp.float32)
            V = jnp.exp(dA_log[:, :, None] * l)
            K = 2.0 * jnp.einsum('chn,hnl->chl', Ct, V).real
            return K
        return _kernel(C_ri, log_dt, B_ri, inv_A_real, A_imag, L)

    def _L0_attn_ref(x, Wq, Wk, Wv, Wo):
        import jax, jax.numpy as jnp
        import numpy as np
        B, S, H = (16, 128, 512)
        NH, NKV = (16, 4)
        HD = H // NH

        def _rope_tables(seq_len, dim, dtype):
            inv_freq = 1.0 / 10000.0 ** (jnp.arange(0, dim, 2, dtype=jnp.float32) / dim)
            t = jnp.arange(seq_len, dtype=jnp.float32)
            freqs = jnp.einsum('i,j->ij', t, inv_freq)
            emb = jnp.concatenate([freqs, freqs], axis=-1)
            cos = jnp.cos(emb)[None, None].astype(dtype)
            sin = jnp.sin(emb)[None, None].astype(dtype)
            return (cos, sin)

        def _rotate_half(x):
            x1, x2 = jnp.split(x, 2, axis=-1)
            return jnp.concatenate([-x2, x1], axis=-1)
        b, s, _ = x.shape
        scaling = HD ** (-0.5)
        q = jnp.einsum('bsh,oh->bso', x, Wq).reshape(b, s, NH, HD).transpose(0, 2, 1, 3)
        k = jnp.einsum('bsh,oh->bso', x, Wk).reshape(b, s, NKV, HD).transpose(0, 2, 1, 3)
        v = jnp.einsum('bsh,oh->bso', x, Wv).reshape(b, s, NKV, HD).transpose(0, 2, 1, 3)
        cos, sin = _rope_tables(s, HD, x.dtype)
        q = q * cos + _rotate_half(q) * sin
        k = k * cos + _rotate_half(k) * sin
        rep = NH // NKV
        k = jnp.repeat(k, rep, axis=1)
        v = jnp.repeat(v, rep, axis=1)
        scores = jnp.einsum('bhqd,bhkd->bhqk', q, k) * scaling
        attn = jax.nn.softmax(scores, axis=-1)
        out = jnp.einsum('bhqk,bhkd->bhqd', attn, v)
        out = out.transpose(0, 2, 1, 3).reshape(b, s, H)
        return jnp.einsum('bsh,oh->bso', out, Wo)

    def _L0_ffn_ref(hidden_states, gate_w, w_gate, w_up, w_down, sw_gate, sw_up, sw_down):
        import jax, jax.numpy as jnp
        import numpy as np
        E, K, H, I = (64, 6, 512, 352)
        NS = 2
        IS = NS * I
        CAP = 64
        T_TOKENS = (1, 256)
        SCALE = 0.02

        def _moe_infer(x, gate_w, w_gate, w_up, w_down):
            T = x.shape[0]
            TK = T * K
            logits = x @ gate_w.T
            scores = jax.nn.softmax(logits, axis=-1)
            topk_w, topk_i = jax.lax.top_k(scores, K)
            flat_i = topk_i.reshape(-1)
            flat_w = topk_w.reshape(-1)
            token_ids = jnp.arange(TK, dtype=jnp.int32) // K
            order = jnp.argsort(flat_i)
            sorted_e = flat_i[order]
            counts = jnp.bincount(flat_i, length=E)
            starts = jnp.concatenate([jnp.zeros((1,), counts.dtype), jnp.cumsum(counts)[:-1]])
            pos_sorted = jnp.arange(TK) - starts[sorted_e]
            pos = jnp.zeros((TK,), jnp.int32).at[order].set(pos_sorted.astype(jnp.int32))
            valid = pos < CAP
            slot = jnp.where(valid, pos, CAP)
            buf = jnp.zeros((E, CAP + 1, H), x.dtype).at[flat_i, slot].set(x[token_ids])
            g = jnp.einsum('ech,ehi->eci', buf, w_gate)
            u = jnp.einsum('ech,ehi->eci', buf, w_up)
            y = jnp.einsum('eci,eih->ech', jax.nn.silu(g) * u, w_down)
            out_slots = y[flat_i, slot] * (flat_w * valid)[:, None]
            return out_slots.reshape(T, K, H).sum(axis=1)
        orig_shape = hidden_states.shape
        x = hidden_states.reshape(-1, orig_shape[-1])
        y = _moe_infer(x, gate_w, w_gate, w_up, w_down).reshape(orig_shape)
        shared = jax.nn.silu(hidden_states @ sw_gate) * (hidden_states @ sw_up) @ sw_down
        return y + shared
    h = _L0_tok_ref(x, L0_tok_log_dt, L0_tok_B_ri, L0_tok_inv_A_real, L0_tok_A_imag, 512)
    h = jnp.concatenate([h, txt], axis=1)
    h = h + _L0_attn_ref(_layernorm(h, axis=-1), L0_attn_Wq, L0_attn_Wk, L0_attn_Wv, L0_attn_Wo)
    h = h + _L0_ffn_ref(_layernorm(h, axis=-1), L0_ffn_gate_w, L0_ffn_w_gate, L0_ffn_w_up, L0_ffn_w_down, L0_ffn_sw_gate, L0_ffn_sw_up, L0_ffn_sw_down)
    return h

_drawn_inputs = setup_inputs


def setup_inputs(seed=0):
    import zlib

    import numpy as np

    out = dict(_drawn_inputs(seed))
    spreads = {}
    factors = {'L0_attn_Wq': 7.508,
     'L0_attn_Wk': 7.078,
     'L0_attn_Wv': 4.386,
     'L0_attn_Wo': 4.374,
     'L0_ffn_gate_w': 8.0,
     'L0_ffn_w_gate': 8.0,
     'L0_ffn_w_up': 8.0,
     'L0_ffn_w_down': 8.0,
     'L0_ffn_sw_gate': 8.0,
     'L0_ffn_sw_up': 8.0,
     'L0_ffn_sw_down': 8.0}
    for name, (base, spread) in spreads.items():
        noise = np.random.default_rng([zlib.crc32(name.encode()), seed]).standard_normal(out[name].shape)
        drawn = base * np.exp(spread * noise) if base else spread * noise
        out[name] = jnp.asarray(drawn.astype(out[name].dtype))
    for name, factor in factors.items():
        out[name] = (out[name] * factor).astype(out[name].dtype)
    return out
```

```python
from contextlib import ExitStack

import numpy as np

import concourse.bass as bass
from concourse import mybir

F32 = mybir.dt.float32
F32R = mybir.dt.float32r
BF16 = mybir.dt.bfloat16
U32 = mybir.dt.uint32
ALU = mybir.AluOpType
ACT = mybir.ActivationFunctionType
AX = mybir.AxisListType
P = 128


def state_space_phase(nc, x, log_dt, B_ri, inv_A_real, A_imag, ident_in, h_dram):
    CH, H, N, _ = x.shape
    L = h_dram.shape[2]
    STEP = 64
    NA = L // STEP
    HALF = H // 2
    CHUNK = 32
    NCHUNK = HALF // CHUNK
    CA = CH * NA
    with ExitStack() as ctx:
        def sb(name, shape, dt=F32):
            return ctx.enter_context(nc.sbuf_tensor(name, shape, dt))

        def ps(name, shape, dt=F32):
            return ctx.enter_context(nc.psum_tensor(name, shape, dt))

        def sem(name):
            return ctx.enter_context(nc.semaphore(name))

        C = sb("ss_C", [P, CH, 2, N, 2])
        Bn = sb("ss_B", [P, 2, N, 2])
        ar = sb("ss_ar", [P, 2, N])
        ai = sb("ss_ai", [P, 2, N])
        dt = sb("ss_dt", [P, 2])
        ident = sb("ss_ident", [P, P])
        xr = sb("ss_xr", [P, 2, N])
        xi = sb("ss_xi", [P, 2, N])
        dr = sb("ss_dr", [P, 2, N])
        inv = sb("ss_inv", [P, 2, N])
        t1 = sb("ss_t1", [P, 2, N])
        t2 = sb("ss_t2", [P, 2, N])
        t3 = sb("ss_t3", [P, 2, N])
        zg = sb("ss_zg", [P, 4, 2, N])
        zgT = sb("ss_zgT", [P, 4, HALF])
        E = sb("ss_E", [P, 2, CH, HALF])
        e1 = sb("ss_e1", [P, CH, HALF])
        e2 = sb("ss_e2", [P, CH, HALF])
        zp = sb("ss_zp", [P, 2, 7, HALF])
        Za = sb("ss_Za", [P, 2, NA, HALF])
        sq = sb("ss_sq", [P, 2, NA, HALF])
        Pm = sb("ss_P", [P, 2, 2, CHUNK, CA])
        Qm = sb("ss_Q", [P, 2, 2, CHUNK, STEP])
        tp = sb("ss_tp", [P, 2, CHUNK, NA])
        tq = sb("ss_tq", [P, 2, CHUNK * STEP // 2])
        out = sb("ss_out", [P, 2, CHUNK, STEP])
        psT = ps("ss_psT", [P, 5, 4, P])
        psK = ps("ss_psK", [P, 2, 512])

        loaded = sem("ss_loaded")
        exps = sem("ss_exps")
        zg_ready = sem("ss_zg_ready")
        turned = sem("ss_turned")
        powers = sem("ss_powers")
        p_ready = sem("ss_p_ready")
        q_ready = sem("ss_q_ready")
        multiplied = sem("ss_multiplied")
        evacuated = sem("ss_evacuated")
        stored = [sem(f"ss_stored{j}") for j in range(2)]
        dve_step = sem("ss_dve_step")
        pool_step = sem("ss_pool_step")
        block = ctx.enter_context(nc.Block())
        HPB = 512 // STEP
        NBANK = CHUNK // HPB

        @block.sync
        def _(sp):
            sp.dma_start(ar[:], inv_A_real.rearrange("(s p) n -> p s n", p=P)).then_inc(loaded, 16)
            sp.dma_start(ai[:], A_imag.rearrange("(s p) n -> p s n", p=P)).then_inc(loaded, 16)
            with nc.allow_non_contiguous_dma(reason="256 values of log_dt"):
                sp.dma_start(dt[:], log_dt.rearrange("(s p) -> p s", p=P)).then_inc(loaded, 16)
            sp.dma_start(Bn[:].rearrange("p s n r -> p s (n r)"),
                         B_ri.rearrange("(s p) n r -> p s (n r)", p=P)).then_inc(loaded, 16)
            sp.dma_start(ident[:], ident_in).then_inc(loaded, 16)
            for s in range(2):
                sp.dma_start(C[:, :, s].rearrange("p c n r -> p c (n r)"),
                             x[:, s * P:(s + 1) * P].rearrange("c p n r -> p c (n r)")).then_inc(loaded, 16)
            for k in range(NCHUNK):
                sp.wait_ge(evacuated, NBANK * (k + 1))
                for s in range(2):
                    h0 = s * HALF + k * CHUNK
                    for c in range(CH):
                        q0 = s * CA + c * NA
                        sp.dma_start(h_dram[c, h0:h0 + CHUNK, :].rearrange("h (a b) -> a h b", b=STEP),
                                     out[q0:q0 + NA, k % 2]).then_inc(stored[k % 2], 16)
            for j in range(2):
                sp.wait_ge(stored[j], 16 * 2 * CH * NCHUNK // 2)

        @block.scalar
        def _(act):
            act.wait_ge(loaded, 16 * 7)
            nc.scalar.activation(ar[:], ar[:], ACT.Exp).then_inc(exps, 1)
            nc.scalar.activation(dt[:], dt[:], ACT.Exp).then_inc(exps, 1)
            for k in range(NCHUNK):
                if k >= 2:
                    act.wait_ge(stored[k % 2], 16 * 2 * CH * (k // 2))
                for j in range(NBANK):
                    n = k * NBANK + j
                    act.wait_ge(multiplied, n + 1)
                    nc.scalar.activation(out[:, k % 2, j * HPB:(j + 1) * HPB, :].rearrange("p h b -> p (h b)"),
                                         psK[:, n % 2, :], ACT.Copy).then_inc(evacuated, 1)

        @block.vector
        def _(dve):
            chain = [0]

            def link(ins):
                chain[0] += 1
                ins.then_inc(dve_step, 1)
                dve.wait_ge(dve_step, chain[0])

            dve.wait_ge(exps, 2)
            V = nc.vector
            for s in range(2):
                V.tensor_scalar(xr[:, s], ar[:, s], dt[:, s:s + 1], -0.5, ALU.mult, ALU.mult)
                link(V.tensor_scalar(xi[:, s], ai[:, s], dt[:, s:s + 1], 0.5, ALU.mult, ALU.mult))
            V.tensor_scalar(dr[:], xr[:], -1.0, 1.0, ALU.mult, ALU.add)
            V.tensor_tensor(t1[:], xr[:], xr[:], ALU.mult)
            link(V.tensor_tensor(t2[:], xi[:], xi[:], ALU.mult))
            link(V.tensor_tensor(inv[:], dr[:], dr[:], ALU.mult))
            link(V.tensor_tensor(inv[:], inv[:], t2[:], ALU.add))
            link(V.reciprocal(inv[:], inv[:]))
            link(V.tensor_tensor(t1[:], t1[:], t2[:], ALU.add))
            link(V.tensor_scalar(t1[:], t1[:], -1.0, 1.0, ALU.mult, ALU.add))
            V.tensor_tensor(zg[:, 0], t1[:], inv[:], ALU.mult)
            link(V.scalar_tensor_tensor(out=zg[:, 1], in0=xi[:], scalar=2.0, in1=inv[:], op0=ALU.mult, op1=ALU.mult))
            for s in range(2):
                link(V.tensor_scalar(inv[:, s], inv[:, s], dt[:, s:s + 1], 2.0, ALU.mult, ALU.mult))
            V.tensor_tensor(t1[:], Bn[:, :, :, 0], dr[:], ALU.mult)
            V.tensor_tensor(t2[:], Bn[:, :, :, 1], xi[:], ALU.mult)
            V.tensor_tensor(t3[:], Bn[:, :, :, 0], xi[:], ALU.mult)
            link(V.tensor_tensor(xr[:], Bn[:, :, :, 1], dr[:], ALU.mult))
            V.tensor_tensor(t1[:], t1[:], t2[:], ALU.subtract)
            link(V.tensor_tensor(t3[:], t3[:], xr[:], ALU.add))
            V.tensor_tensor(zg[:, 2], t1[:], inv[:], ALU.mult)
            V.tensor_tensor(zg[:, 3], t3[:], inv[:], ALU.mult).then_inc(zg_ready, 1)

            dve.wait_ge(turned, 1)
            link(V.tensor_copy(zgT[:], psT[:, 0]))
            dve.wait_ge(turned, 2)
            Cr = psT[:, 1:3].rearrange("p u v h -> p (u v) h")
            Ci = psT[:, 3:5].rearrange("p u v h -> p (u v) h")
            g = [zgT[:, 2 + r:3 + r, :].to_broadcast([P, CH, HALF]) for r in range(2)]
            V.tensor_tensor(e1[:], Cr, g[0], ALU.mult)
            link(V.tensor_tensor(e2[:], Ci, g[1], ALU.mult))
            link(V.tensor_tensor(E[:, 0], e1[:], e2[:], ALU.subtract))
            V.tensor_tensor(e1[:], Cr, g[1], ALU.mult)
            link(V.tensor_tensor(e2[:], Ci, g[0], ALU.mult))
            V.tensor_tensor(E[:, 1], e1[:], e2[:], ALU.add)

            link(V.tensor_copy(zp[:, :, 0, :], zgT[:, 0:2, :]))
            for k in range(6):
                a, b = zp[:, 0, k], zp[:, 1, k]
                V.tensor_tensor(sq[:, 0, 0], a, a, ALU.mult)
                V.tensor_tensor(sq[:, 0, 1], b, b, ALU.mult)
                link(V.tensor_tensor(sq[:, 0, 2], a, b, ALU.mult))
                V.tensor_tensor(zp[:, 0, k + 1], sq[:, 0, 0], sq[:, 0, 1], ALU.subtract)
                link(V.tensor_scalar(zp[:, 1, k + 1], sq[:, 0, 2], 2.0, None, ALU.mult))
            V.memset(Za[:, 0, 0], 1.0)
            V.memset(Za[:, 1, 0], 0.0)
            link(V.tensor_copy(Za[:, :, 1, :], zp[:, :, 6, :]))
            n = 2
            while n < NA:
                a, b = Za[:, 0, n // 2], Za[:, 1, n // 2]
                V.tensor_tensor(sq[:, 0, 0], a, a, ALU.mult)
                V.tensor_tensor(sq[:, 0, 1], b, b, ALU.mult)
                link(V.tensor_tensor(sq[:, 0, 2], a, b, ALU.mult))
                V.tensor_tensor(Za[:, 0, n], sq[:, 0, 0], sq[:, 0, 1], ALU.subtract)
                link(V.tensor_scalar(Za[:, 1, n], sq[:, 0, 2], 2.0, None, ALU.mult))
                m = n - 1
                u = [Za[:, r, n:n + 1, :].to_broadcast([P, m, HALF]) for r in range(2)]
                v = [Za[:, r, 1:n, :] for r in range(2)]
                V.tensor_tensor(Za[:, 0, n + 1:2 * n], u[0], v[0], ALU.mult)
                link(V.tensor_tensor(sq[:, 0, 0:m], u[1], v[1], ALU.mult))
                V.tensor_tensor(Za[:, 1, n + 1:2 * n], u[0], v[1], ALU.mult)
                link(V.tensor_tensor(sq[:, 1, 0:m], u[1], v[0], ALU.mult))
                V.tensor_tensor(Za[:, 0, n + 1:2 * n], Za[:, 0, n + 1:2 * n], sq[:, 0, 0:m], ALU.subtract)
                link(V.tensor_tensor(Za[:, 1, n + 1:2 * n], Za[:, 1, n + 1:2 * n], sq[:, 1, 0:m], ALU.add))
                n *= 2
            dve.sem_inc(powers, 1)

            for k in range(NCHUNK):
                hs = slice(k * CHUNK, (k + 1) * CHUNK)
                if k >= 2:
                    dve.wait_ge(multiplied, NBANK * (k - 1))
                za = [Za[:, r, :, hs].rearrange("p a h -> p h a") for r in range(2)]
                for c in range(CH):
                    pr = Pm[:, k % 2, 0, :, c * NA:(c + 1) * NA]
                    pi = Pm[:, k % 2, 1, :, c * NA:(c + 1) * NA]
                    er = E[:, 0, c, hs].rearrange("p (h a) -> p h a", a=1).to_broadcast([P, CHUNK, NA])
                    ei = E[:, 1, c, hs].rearrange("p (h a) -> p h a", a=1).to_broadcast([P, CHUNK, NA])
                    V.tensor_tensor(pr, er, za[0], ALU.mult)
                    V.tensor_tensor(tp[:, 0], ei, za[1], ALU.mult)
                    V.tensor_tensor(tp[:, 1], er, za[1], ALU.mult)
                    link(V.scalar_tensor_tensor(out=pi, in0=ei, scalar=-1.0, in1=za[0], op0=ALU.mult, op1=ALU.mult))
                    V.tensor_tensor(pr, pr, tp[:, 0], ALU.subtract)
                    link(V.tensor_tensor(pi, pi, tp[:, 1], ALU.subtract))
                dve.sem_inc(p_ready, 1)

        @block.gpsimd
        def _(pool):
            chain = [0]

            def link(ins):
                chain[0] += 1
                ins.then_inc(pool_step, 1)
                pool.wait_ge(pool_step, chain[0])

            G = nc.gpsimd
            pool.wait_ge(powers, 1)
            for k in range(NCHUNK):
                hs = slice(k * CHUNK, (k + 1) * CHUNK)
                if k >= 2:
                    pool.wait_ge(multiplied, NBANK * (k - 1))
                q = [Qm[:, k % 2, r] for r in range(2)]
                G.memset(q[0][:, :, 0:1], 1.0)
                G.memset(q[1][:, :, 0:1], 0.0)
                for r in range(2):
                    link(G.tensor_copy(q[r][:, :, 1], zp[:, r, 0, hs]))
                n = 2
                lev = 1
                while n < STEP:
                    z = [zp[:, r, lev, hs].rearrange("p (h a) -> p h a", a=1).to_broadcast([P, CHUNK, n]) for r in range(2)]
                    t = [tq[:, r, 0:CHUNK * n].rearrange("p (h a) -> p h a", a=n) for r in range(2)]
                    G.tensor_tensor(q[0][:, :, n:2 * n], q[0][:, :, 0:n], z[0], ALU.mult)
                    G.tensor_tensor(t[0], q[1][:, :, 0:n], z[1], ALU.mult)
                    G.tensor_tensor(q[1][:, :, n:2 * n], q[0][:, :, 0:n], z[1], ALU.mult)
                    link(G.tensor_tensor(t[1], q[1][:, :, 0:n], z[0], ALU.mult))
                    G.tensor_tensor(q[0][:, :, n:2 * n], q[0][:, :, n:2 * n], t[0], ALU.subtract)
                    link(G.tensor_tensor(q[1][:, :, n:2 * n], q[1][:, :, n:2 * n], t[1], ALU.add))
                    n *= 2
                    lev += 1
                pool.sem_inc(q_ready, 1)

        @block.tensor
        def _(pe):
            T = nc.tensor
            pe.wait_ge(loaded, 16 * 7)
            for r in range(2):
                for c in range(CH):
                    T.transpose(psT[:, 1 + 2 * r + c // 4, c % 4, :], C[:, c, :, :, r].rearrange("p s n -> p (s n)"), ident[:])
            pe.wait_ge(zg_ready, 1)
            for j in range(4):
                m = T.transpose(psT[:, 0, j, :], zg[:, j].rearrange("p s n -> p (s n)"), ident[:])
            m.then_inc(turned, 2)
            for k in range(NCHUNK):
                pe.wait_ge(p_ready, k + 1)
                pe.wait_ge(q_ready, k + 1)
                for j in range(NBANK):
                    n = k * NBANK + j
                    if n >= 2:
                        pe.wait_ge(evacuated, n - 1)
                    for i in range(HPB):
                        h = j * HPB + i
                        for r in range(2):
                            for s in range(2):
                                m = T.matmul(psK[64 * s:64 * s + 64, n % 2, i * STEP:(i + 1) * STEP],
                                             Pm[64 * s:64 * s + 64, k % 2, r, h, :],
                                             Qm[64 * s:64 * s + 64, k % 2, r, h, :],
                                             start=(r == 0), stop=(r == 1))
                    m.then_inc(multiplied, 1)
DVE_STEPS = 80


def shape_constants(B, SEQ, E, CAP):
    HD = 32
    NT = SEQ // P
    inv = (np.float32(1.0) / np.float32(10000.0) ** (np.arange(0, HD, 2, dtype=np.float32) / np.float32(HD))).astype(np.float32)
    f = np.arange(SEQ, dtype=np.float32)[:, None] * inv[None]
    emb = np.concatenate([f, f], axis=-1)
    sign = np.where(np.arange(HD) < HD // 2, -1.0, 1.0).astype(np.float32)
    tiles = lambda a: np.ascontiguousarray(a.reshape(NT, P, HD).transpose(1, 0, 2))
    t = np.arange(P)
    return {
        "cos": tiles(np.cos(emb).astype(np.float32)),
        "sin": tiles(np.sin(emb).astype(np.float32) * sign),
        "ident": np.eye(P, dtype=np.float32),
        "upper": np.stack([(t[:, None] < t[None]).astype(np.float32), np.ones((P, P), np.float32)], axis=1),
        "tok": (t[:, None] + P * np.arange(NT)[None]).astype(np.float32),
        "slot": np.stack([np.broadcast_to(np.arange(E, dtype=np.float32), (P, E)),
                          np.broadcast_to(CAP * np.arange(E, dtype=np.float32), (P, E))]),
        "empty": (B * SEQ + np.arange(E * CAP) % CAP).astype(np.uint32)[:, None],
    }


def wait(engine, semaphore, value):
    if type(value) is int and value <= 0:
        return
    engine.wait_ge(semaphore, value)


def wait_apart(engine, semaphore, value, carrier):
    if type(value) is int and value <= 0:
        return
    engine.wait_ge(semaphore, value)
    engine.sem_inc(carrier, 1)


def transposed_weights_phase(nc, Wq, Wk, Wv, Wo, gate_w, ident_in, WxT, WoT, gwT):
    D = Wq.shape[1]
    KC = D // P
    OQ, OK = Wq.shape[0] // P, Wk.shape[0] // P
    NE = gate_w.shape[0]
    blocks = [(Wq, o) for o in range(OQ)] + [(Wk, o) for o in range(OK)] + [(Wv, o) for o in range(OK)] \
        + [(Wo, o) for o in range(OQ)]
    NB = len(blocks)
    NX = OQ + 2 * OK
    with ExitStack() as ctx:
        rows = ctx.enter_context(nc.sbuf_tensor("w_rows", [P, NB, D], F32))
        grow = ctx.enter_context(nc.sbuf_tensor("w_gate_rows", [NE, D], F32))
        ident = ctx.enter_context(nc.sbuf_tensor("w_ident", [P, P], F32))
        ps = ctx.enter_context(nc.psum_tensor("w_ps", [P, 8, 512], F32))
        loaded = ctx.enter_context(nc.semaphore("w_loaded"))
        turned = ctx.enter_context(nc.semaphore("w_turned"))
        hi_done = ctx.enter_context(nc.semaphore("w_hi_done"))
        lo_done = ctx.enter_context(nc.semaphore("w_lo_done"))
        block = ctx.enter_context(nc.Block())

        def halves(n):
            if n < NX:
                return [WxT[:, r, :, n * P:(n + 1) * P] for r in range(2)]
            return [WoT[:, r, :, (n - NX) * P:(n - NX + 1) * P] for r in range(2)]

        @block.sync
        def _(sp):
            sp.dma_start(ident[:], ident_in).then_inc(loaded, 16)
            sp.dma_start(grow[:], gate_w).then_inc(loaded, 16)
            for n, (w, o) in enumerate(blocks):
                sp.dma_start(rows[:, n], w[o * P:(o + 1) * P, :]).then_inc(loaded, 16)

        @block.tensor
        def _(pe):
            pe.wait_ge(loaded, 16 * (NB + 2))
            for n in range(NB + 1):
                if n >= 8:
                    pe.wait_ge(lo_done, n - 7)
                for k in range(KC):
                    if n < NB:
                        m = nc.tensor.transpose(ps[:, n % 8, k * P:(k + 1) * P], rows[:, n, k * P:(k + 1) * P], ident[:])
                    else:
                        m = nc.tensor.transpose(ps[:, n % 8, k * NE:(k + 1) * NE], grow[:, k * P:(k + 1) * P],
                                                ident[0:NE, 0:NE])
                m.then_inc(turned, 1)

        @block.scalar
        def _(act):
            for n in range(NB):
                act.wait_ge(turned, n + 1)
                nc.scalar.activation(halves(n)[0], ps[:, n % 8].rearrange("p (k o) -> p k o", k=KC),
                                     ACT.Copy).then_inc(hi_done, 1)

        @block.vector
        def _(dve):
            for n in range(NB):
                dve.wait_ge(hi_done, n + 1)
                hi, lo = halves(n)
                nc.vector.tensor_tensor(lo, ps[:, n % 8].rearrange("p (k o) -> p k o", k=KC),
                                        hi.bitcast(F32), ALU.subtract).then_inc(lo_done, 1)
            dve.wait_ge(turned, NB + 1)
            nc.vector.tensor_copy(gwT[:], ps[:, NB % 8, 0:KC * NE].rearrange("p (k e) -> p k e", k=KC))\
                .then_inc(lo_done, 1)


def attention_phase(nc, h_dram, txt, tabs, WxT, WoT, gwT, acc, xrow, x2T_dram, slot_table, consts):
    (cos_in, sin_in, ident_in, upper_in, tok_in, slot_in) = tabs
    B, S0, D = h_dram.shape
    SEQ = S0 + txt.shape[1]
    NT = SEQ // P
    KC = D // P
    NH, NKV, HD = 16, 4, 32
    HT = NH + NKV
    REP = NH // NKV
    E, TOPK, CAP = 64, 6, 64
    SPLIT = 3 * HD
    QR = SPLIT + 1
    NSLOT = E * CAP
    RING = 2 * REP
    EPS = 1e-5
    with ExitStack() as ctx:
        def sb(name, shape, dt=F32):
            return ctx.enter_context(nc.sbuf_tensor(name, shape, dt))

        def sem(name):
            return ctx.enter_context(nc.semaphore(name))

        ident = sb("at_ident", [P, P])
        identb = sb("at_identb", [P, P], BF16)
        ones = sb("at_ones", [P, HD])
        upper = sb("at_upper", [P, 2, P], BF16)
        upf = sb("at_upf", [P, 2, P])
        cos = sb("at_cos", [P, NT, HD])
        sin = sb("at_sin", [P, NT, HD])
        mhalf = sb("at_mhalf", [P, NT])
        ht = [sb(f"at_h{j}", [P, NT, D]) for j in range(2)]
        rows = sb("at_rows", [P, NT * D])
        xn = rows[:, :].rearrange("p (s d) -> p s d", s=NT)
        x2T = rows[:, :].rearrange("p (k t) -> p k t", k=KC)
        bn = sb("at_bn", [P, NT, 6])
        mv = sb("at_mv", [P, NT, 2])
        ve = sb("at_ve", [P, NT])
        rstd = sb("at_rstd", [P, NT])
        xT = sb("at_xT", [P, 2, KC, SEQ], F32R)
        oTs = xT
        r1 = sb("at_r1", [P, NT, HT, HD])
        r2 = sb("at_r2", [P, NT, HT, HD])
        Q3 = sb("at_Q3", [P, NT, HT, QR])
        qb = sb("at_qb", [P, NT, 5, P], BF16)
        qbT = sb("at_qbT", [P, NT, 5, P], BF16)
        vv = sb("at_v", [P, NT, NKV * HD])
        QT = sb("at_QT", [QR, HT, SEQ], F32R)
        PT = sb("at_PT", [P, RING, NT, SEQ])
        rS = sb("at_rS", [P, SEQ])
        oT = sb("at_oT", [P, 2, SEQ])
        x2 = sb("at_x2", [P, NT, D + E])
        lg = sb("at_lg", [P, NT, E])
        mx = sb("at_mx", [P, NT, 8])
        mi = sb("at_mi", [P, NT, 8], U32)
        mf = sb("at_mf", [P, NT, 8])
        nm = sb("at_nm", [P, NT])
        es = sb("at_es", [P, NT, E])
        ssum = sb("at_ssum", [P, NT])
        rsum = sb("at_rsum", [P, NT])
        iota = sb("at_iota", [P, E])
        slot0 = sb("at_slot0", [P, E])
        hot = sb("at_hot", [P, NT * TOPK, E], BF16)
        mask = sb("at_mask", [P, NT, E], BF16)
        base = sb("at_base", [P, E])
        pos = sb("at_pos", [P, NT, E])
        over = sb("at_over", [P, NT, E])
        hv = r2[:].rearrange("p s h d -> p (s h d)")[:, 0:NT * TOPK * E].rearrange("p (n e) -> p n e", e=E)
        sf = sb("at_sf", [P, NT * TOPK])
        si = [sb(f"at_si{j}", [P, NT * TOPK], U32) for j in range(2)]
        tokf = sb("at_tokf", [P, NT])
        toki = [sb(f"at_toki{j}", [P, NT], U32) for j in range(2)]
        ps = ctx.enter_context(nc.psum_tensor("at_ps", [P, 8, 512], F32))

        consts_in = sem("at_consts_in")
        consts_ok = sem("at_consts_ok")
        ones_ok = sem("at_ones_ok")
        h_in = [sem(f"at_h_in{j}") for j in range(2)]
        var_ready = sem("at_var_ready")
        rstd_ready = sem("at_rstd_ready")
        xn_ready = sem("at_xn_ready")
        x_turned = sem("at_x_turned")
        xhi_ready = sem("at_xhi_ready")
        xlo_ready = sem("at_xlo_ready")
        qkv_ready = sem("at_qkv_ready")
        v_copied = sem("at_v_copied")
        rope_mul = sem("at_rope_mul")
        rope_add = sem("at_rope_add")
        q_hi = sem("at_q_hi")
        q_lo = sem("at_q_lo")
        qb_ready = sem("at_qb_ready")
        qb_turned = sem("at_qb_turned")
        qbT_ready = sem("at_qbT_ready")
        raw_scores = sem("at_raw_scores")
        max_ready = sem("at_max_ready")
        q_turned = sem("at_q_turned")
        qT_by_act = sem("at_qT_by_act")
        qT_by_dve = sem("at_qT_by_dve")
        scores_ready = sem("at_scores_ready")
        probs_ready = sem("at_probs_ready")
        pv_done = sem("at_pv_done")
        o_ready = sem("at_o_ready")
        ohi_ready = sem("at_ohi_ready")
        olo_ready = sem("at_olo_ready")
        proj_done = sem("at_proj_done")
        h2_ready = sem("at_h2_ready")
        var2_ready = sem("at_var2_ready")
        rstd2_ready = sem("at_rstd2_ready")
        x2_ready = sem("at_x2_ready")
        x2_turned = sem("at_x2_turned")
        x2T_by_act = sem("at_x2T_by_act")
        x2T_by_dve = sem("at_x2T_by_dve")
        logits_ready = sem("at_logits_ready")
        gmax_ready = sem("at_gmax_ready")
        gexp_ready = sem("at_gexp_ready")
        mask_ready = sem("at_mask_ready")
        pos_ready = sem("at_pos_ready")
        pos_read = sem("at_pos_read")
        score_rows = sem("at_score_rows")
        slots_ready = sem("at_slots_ready")
        h2_stored = [sem(f"at_h2_stored{j}") for j in range(2)]
        x2_stored = sem("at_x2_stored")
        x2T_stored = sem("at_x2T_stored")
        scattered = sem("at_scattered")
        table_set = sem("at_table_set")
        dve_step = sem("at_dve_step")
        carried_dve = sem("at_carried_dve")
        carried_pool = sem("at_carried_pool")
        pool_step = sem("at_pool_step")
        block = ctx.enter_context(nc.Block())
        NIT = B // 2

        @block.sync
        def _(sp):
            for dst, src in ((ident, ident_in), (cos, cos_in), (sin, sin_in), (upf, upper_in), (tokf, tok_in),
                             (iota, slot_in[0]), (slot0, slot_in[1])):
                sp.dma_start(dst[:], src).then_inc(consts_in, 16)
            def pair(i):
                for j in range(2):
                    b = 2 * i + j
                    wait(sp, h2_stored[j], 16 * i)
                    sp.dma_start(ht[j][:, 0:S0 // P, :], h_dram[b].rearrange("(s p) d -> p s d", p=P))\
                        .then_inc(h_in[j], 16)
                    sp.dma_start(ht[j][:, S0 // P:NT, :], txt[b].rearrange("(s p) d -> p s d", p=P))\
                        .then_inc(h_in[j], 16)
                    wait(sp, h2_ready, NT * (b + 1))
                    sp.dma_start(acc[bass.ds(b * SEQ, SEQ), :].rearrange("(s p) d -> p s d", p=P), ht[j][:])\
                        .then_inc(h2_stored[j], 16)
                    wait(sp, x2T_by_act, 2 * (b + 1))
                    wait(sp, x2T_by_dve, 2 * (b + 1))
                    sp.dma_start(x2T_dram[b], x2T).then_inc(x2T_stored, 16)
                    wait(sp, score_rows, b + 1)
                    sp.dma_start(xrow[bass.ds(b * SEQ, SEQ), :].rearrange("(s p) d -> p s d", p=P), x2[:])\
                        .then_inc(x2_stored, 16)

            pair(0)
            with sp.Fori(1, NIT) as i:
                pair(i)
            for j in range(2):
                wait(sp, h2_stored[j], 16 * NIT)
            wait(sp, x2_stored, 16 * B)
            wait(sp, x2T_stored, 16 * B)

        @block.tensor
        def _(pe):
            T = nc.tensor
            wait(pe, consts_in, 16 * 7)
            wait(pe, consts_ok, 1)
            wait(pe, ones_ok, 1)

            def sequence(b):
                wait(pe, xn_ready, NT * (b + 1))
                wait(pe, pos_read, b)
                for k in range(KC):
                    for s in range(NT):
                        m = T.transpose(ps[:, k, s * P:(s + 1) * P], xn[:, s, k * P:(k + 1) * P], ident[:])
                    m.then_inc(x_turned, 1)
                wait(pe, xhi_ready, KC * (b + 1))
                wait(pe, xlo_ready, KC * (b + 1))
                for s in range(NT):
                    if s == 2:
                        wait(pe, rope_mul, NT * b + 1)
                        wait(pe, v_copied, NT * b + 1)
                    u = 4 + 2 * (s % 2)
                    for c0, c1, bank in ((0, 512, u), (512, 768, u + 1)):
                        n = 0
                        for k in range(KC):
                            for xa, wa in ((0, 0), (0, 1), (1, 0)):
                                m = T.matmul(ps[:, bank, 0:c1 - c0], xT[:, xa, k, s * P:(s + 1) * P],
                                             WxT[:, wa, k, c0:c1], start=(n == 0), stop=(n == 3 * KC - 1))
                                n += 1
                    m.then_inc(qkv_ready, 1)
                for s in range(NT):
                    wait(pe, qb_ready, NT * b + s + 1)
                    for r in range(5):
                        m = T.transpose(ps[:, s].bitcast(BF16)[:, r * P:(r + 1) * P], qb[:, s, r, :], identb[:])
                    m.then_inc(qb_turned, 1)
                wait(pe, qbT_ready, NT * (b + 1))
                wait(pe, rope_mul, NT * (b + 1))
                wait(pe, v_copied, NT * (b + 1))
                for s in range(NT):
                    for r in range(REP):
                        n = s * REP + r
                        if n >= 2:
                            wait(pe, max_ready, NT * REP * b + n - 1)
                        for g in range(NKV):
                            rows = slice(HD * g, HD * (g + 1))
                            m = T.matmul(ps[:, 4 * (n % 2) + g, 0:SEQ], qbT[rows, s, r, :],
                                         qbT[rows, :, 4, :], start=True, stop=True)
                        m.then_inc(raw_scores, 1)
                wait(pe, max_ready, NT * REP * (b + 1))
                wait(pe, q_hi, 3 * NT * (b + 1))
                wait(pe, q_lo, NT * (b + 1))
                for n in range(HT):
                    if n >= 8:
                        wait(pe, qT_by_act if n % 2 == 0 else qT_by_dve, HT // 2 * b + (n - 8) // 2 + 1)
                    for s in range(NT):
                        m = T.transpose(ps[0:QR, n % 8, s * P:(s + 1) * P], Q3[:, s, n, :], ident[:])
                    m.then_inc(q_turned, 1)
                wait(pe, qT_by_act, HT // 2 * (b + 1))
                wait(pe, qT_by_dve, HT // 2 * (b + 1))

                def scores(g):
                    for h in range(REP * g, REP * (g + 1)):
                        if h >= 2:
                            wait(pe, probs_ready, NH * b + h - 1)
                        for kt in range(NT):
                            m = T.matmul(ps[:, 3 * (h % 2) + kt, 0:SEQ], QT[:, NH + g, kt * P:(kt + 1) * P],
                                         QT[:, h, :], start=True, stop=True)
                        m.then_inc(scores_ready, 1)

                def values(g):
                    wait(pe, probs_ready, NH * b + REP * (g + 1))
                    wait(pe, o_ready, NKV * b + g)
                    for lhs, bank in ((None, 6), (ones, 7)):
                        for kt in range(NT):
                            for jj in range(REP):
                                w = ones[:, :] if lhs is not None else vv[:, kt, HD * g:HD * (g + 1)]
                                m = T.matmul(ps[HD * jj:HD * (jj + 1), bank, 0:SEQ], w,
                                             PT[:, (REP * g + jj) % RING, kt, :],
                                             start=(kt == 0), stop=(kt == NT - 1))
                    m.then_inc(pv_done, 1)

                scores(0)
                for g in range(NKV):
                    if g + 1 < NKV:
                        scores(g + 1)
                    values(g)
                wait(pe, ohi_ready, NKV * (b + 1))
                wait(pe, olo_ready, NKV * (b + 1))
                for s in range(NT):
                    n = 0
                    for k in range(KC):
                        for xa, wa in ((0, 0), (0, 1), (1, 0)):
                            m = T.matmul(ps[:, s, :], oTs[:, xa, k, s * P:(s + 1) * P], WoT[:, wa, k, :],
                                         start=(n == 0), stop=(n == 3 * KC - 1))
                            n += 1
                    m.then_inc(proj_done, 1)
                wait(pe, x2_ready, NT * (b + 1))
                for k in range(KC):
                    for s in range(NT):
                        m = T.transpose(ps[:, 3 + k, s * P:(s + 1) * P], x2[:, s, k * P:(k + 1) * P], ident[:])
                    m.then_inc(x2_turned, 1)
                wait(pe, x2T_by_act, 2 * (b + 1))
                wait(pe, x2T_by_dve, 2 * (b + 1))
                for s in range(NT):
                    for k in range(KC):
                        m = T.matmul(ps[:, 7, s * E:(s + 1) * E], x2T[:, k, s * P:(s + 1) * P], gwT[:, k, :],
                                     start=(k == 0), stop=(k == KC - 1))
                m.then_inc(logits_ready, 1)
                wait(pe, mask_ready, b + 1)
                for s in range(NT + 1):
                    for q in range(min(s, NT - 1) + 1):
                        m = T.matmul(ps[:, 6, s * E:(s + 1) * E], upper[:, 0 if q == s else 1, :], mask[:, q, :],
                                     start=(q == 0), stop=(q == min(s, NT - 1)))
                m.then_inc(pos_ready, 1)

            sequence(0)
            with pe.Fori(1, B) as b:
                sequence(b)

        @block.scalar
        def _(act):
            A = nc.scalar
            wait(act, consts_in, 16 * 7)
            A.activation(identb[:], ident[:], ACT.Copy)
            A.activation(upper[:], upf[:], ACT.Copy).then_inc(consts_ok, 1)

            def sequence(b):
                for k in range(KC):
                    wait(act, x_turned, KC * b + k + 1)
                    A.activation(xT[:, 0, k, :], ps[:, k, 0:SEQ], ACT.Copy).then_inc(xhi_ready, 1)
                for s in range(NT):
                    wait(act, qkv_ready, NT * b + s + 1)
                    u = 4 + 2 * (s % 2)
                    wait(act, rope_mul, NT * b + s + 1)
                    A.activation(vv[:, s, :], ps[:, u + 1, P:2 * P], ACT.Copy).then_inc(v_copied, 1)
                    wait(act, rope_add, NT * b + s + 1)
                    qk = r1[:, s]
                    A.activation(Q3[:, s, :, 0:HD].bitcast(F32R), qk, ACT.Copy).then_inc(q_hi, 1)
                    A.activation(qb[:, s, 0:4, :].rearrange("p r (g d) -> p g r d", g=NKV),
                                 qk[:, 0:NH, :].rearrange("p (g r) d -> p g r d", g=NKV), ACT.Copy)
                    A.activation(qb[:, s, 4, :].rearrange("p (g d) -> p g d", g=NKV), qk[:, NH:HT, :], ACT.Copy)\
                        .then_inc(qb_ready, 1)
                    wait(act, q_hi, 3 * (NT * b + s) + 1)
                    A.activation(Q3[:, s, 0:NH, 2 * HD:3 * HD], Q3[:, s, 0:NH, 0:HD], ACT.Copy).then_inc(q_hi, 1)
                    A.activation(Q3[:, s, NH:HT, HD:2 * HD], Q3[:, s, NH:HT, 0:HD], ACT.Copy).then_inc(q_hi, 1)
                for s in range(NT):
                    wait(act, qb_turned, NT * b + s + 1)
                    A.activation(qbT[:, s], ps[:, s].bitcast(BF16)[:, 0:5 * P].rearrange("p (r t) -> p r t", r=5),
                                 ACT.Copy).then_inc(qbT_ready, 1)
                for n in range(0, HT, 2):
                    wait(act, q_turned, HT * b + n + 1)
                    A.activation(QT[:, n, :], ps[0:QR, n % 8, 0:SEQ], ACT.Copy).then_inc(qT_by_act, 1)
                for h in range(NH):
                    wait(act, scores_ready, NH * b + h + 1)
                    if h >= RING:
                        wait(act, pv_done, NKV * b + (h - RING) // REP + 1)
                    u = 3 * (h % 2)
                    A.activation(PT[:, h % RING], ps[:, u:u + 3, 0:SEQ], ACT.Exp, scale=float(HD) ** -0.5)\
                        .then_inc(probs_ready, 1)
                    if h % REP == REP - 1 and h // REP >= 1:
                        out_hi(b, h // REP - 1)
                out_hi(b, NKV - 1)
                for k in range(0, KC, 2):
                    wait(act, x2_turned, KC * b + k + 1)
                    wait(act, x2T_stored, 16 * b)
                    A.activation(x2T[:, k, :], ps[:, 3 + k, 0:SEQ], ACT.Copy).then_inc(x2T_by_act, 1)
                wait(act, gmax_ready, b + 1)
                for s in range(NT):
                    A.activation(es[:, s, :], lg[:, s, :], ACT.Exp, bias=nm[:, s:s + 1],
                                 accum_out=ssum[:, s:s + 1]).then_inc(gexp_ready, 1)

            def out_hi(b, g):
                wait(act, o_ready, NKV * b + g + 1)
                A.activation(oTs[:, 0, g, :], oT[:, g % 2, :], ACT.Copy).then_inc(ohi_ready, 1)

            sequence(0)
            with act.Fori(1, B) as b:
                sequence(b)

        @block.vector
        def _(dve):
            V = nc.vector
            V.memset(mhalf[:], -0.5)
            V.memset(base[:], 0.0)
            V.memset(ones[:], 1.0)
            V.memset(Q3[:, :, NH:HT, SPLIT:QR], 1.0).then_inc(ones_ok, 1)
            wait(dve, consts_in, 16 * 7)

            def pair(i):
                steps = [0]
                total = DVE_STEPS

                def link(ins, apart=False):
                    steps[0] += 1
                    ins.then_inc(dve_step, 1)
                    if apart:
                        wait_apart(dve, dve_step, i * total + steps[0], carried_dve)
                    else:
                        wait(dve, dve_step, i * total + steps[0])

                def stats(src, done):
                    for s in range(NT):
                        link(V.bn_stats(bn[:, s, :], src(s)), apart=True)
                        link(V.bn_aggr(mv[:, s, :], bn[:, s, :]))
                    V.tensor_scalar(ve[:], mv[:, :, 1], EPS, None, ALU.add).then_inc(done, 1)

                for j in range(2):
                    b = 2 * i + j
                    wait(dve, h_in[j], 32 * (i + 1))
                    stats(lambda s: ht[j][:, s, :], var_ready)
                    wait(dve, rstd_ready, b + 1)
                    wait(dve, x_turned, KC * b)
                    wait(dve, x2T_stored, 16 * b)
                    for s in range(NT):
                        V.tensor_scalar(xn[:, s, :], ht[j][:, s, :], mv[:, s, 0:1], rstd[:, s:s + 1],
                                        ALU.subtract, ALU.mult).then_inc(xn_ready, 1)
                    for k in range(KC):
                        wait(dve, xhi_ready, KC * b + k + 1)
                        V.tensor_tensor(xT[:, 1, k, :], ps[:, k, 0:SEQ], xT[:, 0, k, :].bitcast(F32), ALU.subtract)\
                            .then_inc(xlo_ready, 1)
                    for s in range(NT):
                        wait(dve, qkv_ready, NT * b + s + 1)
                        u = 4 + 2 * (s % 2)
                        qk = ps[:, u:u + 2, :].rearrange("p u c -> p (u c)")[:, 0:HT * HD]\
                            .rearrange("p (h d) -> p h d", d=HD)
                        half = HD // 2
                        V.tensor_tensor(r1[:, s], qk, cos[:, s:s + 1, :].to_broadcast([P, HT, HD]), ALU.mult)
                        V.tensor_tensor(r2[:, s, :, 0:half], qk[:, :, half:HD],
                                        sin[:, s:s + 1, 0:half].to_broadcast([P, HT, half]), ALU.mult)
                        link(V.tensor_tensor(r2[:, s, :, half:HD], qk[:, :, 0:half],
                                             sin[:, s:s + 1, half:HD].to_broadcast([P, HT, half]), ALU.mult))
                        dve.sem_inc(rope_mul, 1)
                    for s in range(NT):
                        for r in range(REP):
                            n = s * REP + r
                            wait(dve, raw_scores, NT * REP * b + n + 1)
                            u = 4 * (n % 2)
                            V.tensor_reduce(Q3[:, s, r:NH:REP, SPLIT:QR], ps[:, u:u + NKV, 0:SEQ], AX.X, ALU.max,
                                            negate=True).then_inc(max_ready, 1)
                    for n in range(1, HT, 2):
                        wait(dve, q_turned, HT * b + n + 1)
                        V.tensor_copy(QT[:, n, :], ps[0:QR, n % 8, 0:SEQ]).then_inc(qT_by_dve, 1)
                    for g in range(NKV):
                        wait(dve, pv_done, NKV * b + g + 1)
                        link(V.reciprocal(rS[:], ps[:, 7, 0:SEQ]))
                        if g >= 2:
                            wait(dve, olo_ready, NKV * b + g - 1)
                        V.tensor_tensor(oT[:, g % 2, :], ps[:, 6, 0:SEQ], rS[:], ALU.mult).then_inc(o_ready, 1)
                    for s in range(NT):
                        wait(dve, proj_done, NT * b + s + 1)
                        link(V.tensor_tensor(ht[j][:, s, :], ht[j][:, s, :], ps[:, s, :], ALU.add))
                        dve.sem_inc(h2_ready, 1)
                    stats(lambda s: ht[j][:, s, :], var2_ready)
                    wait(dve, rstd2_ready, b + 1)
                    wait(dve, x2_stored, 16 * b)
                    for s in range(NT):
                        V.tensor_scalar(x2[:, s, 0:D], ht[j][:, s, :], mv[:, s, 0:1], rstd[:, s:s + 1],
                                        ALU.subtract, ALU.mult).then_inc(x2_ready, 1)
                    for k in range(1, KC, 2):
                        wait(dve, x2_turned, KC * b + k + 1)
                        wait(dve, x2T_stored, 16 * b)
                        V.tensor_copy(x2T[:, k, :], ps[:, 3 + k, 0:SEQ]).then_inc(x2T_by_dve, 1)
                    wait(dve, logits_ready, b + 1)
                    link(V.tensor_copy(lg[:], ps[:, 7, 0:NT * E].rearrange("p (s e) -> p s e", s=NT)), apart=True)
                    for s in range(NT):
                        ins = V.max(mx[:, s, :], lg[:, s, :])
                    link(ins)
                    link(V.tensor_scalar(nm[:], mx[:, :, 0], -1.0, None, ALU.mult))
                    dve.sem_inc(gmax_ready, 1)
                    for s in range(NT):
                        ins = V.max_index(mi[:, s, :], mx[:, s, :], lg[:, s, :])
                    link(ins)
                    link(V.tensor_copy(mf[:], mi[:]))
                    for s in range(NT):
                        ins = V.tensor_tensor(hot[:, s * TOPK:(s + 1) * TOPK, :],
                                        iota[:, :].rearrange("p (a e) -> p a e", a=1).to_broadcast([P, TOPK, E]),
                                        mf[:, s, 0:TOPK].rearrange("p (k a) -> p k a", a=1).to_broadcast([P, TOPK, E]),
                                        ALU.is_equal)
                    link(ins)
                    link(V.tensor_reduce(pos[:], hot[:].rearrange("p (s k) e -> p s e k", s=NT), AX.X, ALU.add))
                    V.tensor_copy(mask[:], pos[:]).then_inc(mask_ready, 1)
                    wait(dve, gexp_ready, NT * (b + 1))
                    link(V.reciprocal(rsum[:], ssum[:]))
                    for s in range(NT):
                        ins = V.tensor_scalar(x2[:, s, D:D + E], es[:, s, :], rsum[:, s:s + 1], None, ALU.mult)
                    link(ins)
                    dve.sem_inc(score_rows, 1)
                    wait(dve, pos_ready, b + 1)
                    pp = ps[:, 6, 0:NT * E].rearrange("p (s e) -> p s e", s=NT)
                    link(V.tensor_tensor(pos[:], pp, base[:, :].rearrange("p (a e) -> p a e", a=1)
                                         .to_broadcast([P, NT, E]), ALU.add))
                    link(V.tensor_tensor(base[:], base[:], ps[:, 6, NT * E:(NT + 1) * E], ALU.add))
                    dve.sem_inc(pos_read, 1)
                    link(V.tensor_scalar(over[:], pos[:], float(CAP), 65536.0, ALU.is_ge, ALU.mult))
                    link(V.tensor_tensor(pos[:], pos[:], over[:], ALU.add))
                    link(V.tensor_tensor(pos[:], pos[:], slot0[:, :].rearrange("p (a e) -> p a e", a=1)
                                         .to_broadcast([P, NT, E]), ALU.add))
                    for s in range(NT):
                        ks = slice(s * TOPK, (s + 1) * TOPK)
                        ins = V.tensor_tensor(hv[:, ks, :], hot[:, ks, :], pos[:, s:s + 1, :].to_broadcast([P, TOPK, E]),
                                              ALU.mult)
                    link(ins)
                    link(V.tensor_reduce(sf[:], hv[:], AX.X, ALU.add))
                    wait(dve, scattered, 16 * NT * TOPK * b)
                    V.tensor_copy(si[j][:], sf[:])
                    link(V.tensor_copy(toki[j][:], tokf[:]))
                    link(V.tensor_scalar(tokf[:], tokf[:], float(SEQ), None, ALU.add))
                    dve.sem_inc(slots_ready, 1)
                assert steps[0] == total, steps[0]

            pair(0)
            with dve.Fori(1, NIT) as i:
                pair(i)

        @block.gpsimd
        def _(pool):
            G = nc.gpsimd
            G.dma_start(slot_table, consts).then_inc(table_set, 16)
            wait(pool, table_set, 16)
            wait(pool, ones_ok, 1)

            def pair(i):
                for j in range(2):
                    b = 2 * i + j
                    wait(pool, var_ready, b + 1)
                    G.tensor_tensor(rstd[:], ve[:], mhalf[:], ALU.pow).then_inc(rstd_ready, 1)
                    for s in range(NT):
                        n = NT * b + s
                        wait(pool, rope_mul, n + 1)
                        G.tensor_tensor(r1[:, s], r1[:, s], r2[:, s], ALU.add).then_inc(rope_add, 1)
                        wait(pool, q_hi, 3 * n + 1)
                        wait(pool, rope_add, n + 1)
                        G.tensor_tensor(Q3[:, s, 0:NH, HD:2 * HD].bitcast(F32R), r1[:, s, 0:NH],
                                        Q3[:, s, 0:NH, 0:HD], ALU.subtract)
                        G.tensor_tensor(Q3[:, s, NH:HT, 2 * HD:3 * HD].bitcast(F32R), r1[:, s, NH:HT],
                                        Q3[:, s, NH:HT, 0:HD], ALU.subtract).then_inc(q_lo, 1)
                    for g in range(NKV):
                        wait(pool, ohi_ready, NKV * b + g + 1)
                        G.tensor_tensor(oTs[:, 1, g, :], oT[:, g % 2, :], oTs[:, 0, g, :].bitcast(F32),
                                        ALU.subtract).then_inc(olo_ready, 1)
                    wait(pool, var2_ready, b + 1)
                    G.tensor_tensor(rstd[:], ve[:], mhalf[:], ALU.pow).then_inc(rstd2_ready, 1)
                    wait_apart(pool, slots_ready, b + 1, carried_pool)
                    for s in range(NT):
                        for k in range(TOPK):
                            n = s * TOPK + k
                            G.indirect_dma_start(
                                slot_table, bass.IndirectOffsetOnAxis(ap=si[j][:, n:n + 1], axis=0),
                                toki[j][:, s:s + 1], None, bounds_check=NSLOT - 1, oob_is_err=False,
                                compute_op=ALU.bypass).then_inc(scattered, 16)

            pair(0)
            with pool.Fori(1, NIT) as i:
                pair(i)
            wait(pool, scattered, 16 * NT * TOPK * B)


def experts_phase(nc, acc, xrow, x2T_dram, slot_table, w_gate, w_up, w_down, sw_gate, sw_up, sw_down, ident_in):
    E, D, I = w_gate.shape
    IS = sw_gate.shape[1]
    NSEQ, _, KC, SEQ = x2T_dram.shape
    CAP = slot_table.shape[0] // E
    T = NSEQ * SEQ
    NT = SEQ // P
    PAIRS = E // 2
    Q = PAIRS // NSEQ
    IC = (I + P - 1) // P
    IW = [min(P, I - c * P) for c in range(IC)]
    SC = (IS + P - 1) // P
    SW = [IS // SC + (1 if c < IS % SC else 0) for c in range(SC)]
    SO = [sum(SW[:c]) for c in range(SC)]
    SM = max(SW)
    assert Q == 4 and SC == 2 * (Q - 1) and NT == 3
    with ExitStack() as ctx:
        def sb(name, shape, dt=F32):
            return ctx.enter_context(nc.sbuf_tensor(name, shape, dt))

        def sem(name):
            return ctx.enter_context(nc.semaphore(name))

        ident = sb("mo_ident", [P, P])
        zeros = sb("mo_zeros", [CAP, D + E])
        gather_all = sb("mo_gather_all", [P, PAIRS], U32)
        scatter_all = sb("mo_scatter_all", [CAP, E], U32)
        gather_ix = sb("mo_gather_ix", [P, Q], U32)
        scatter_ix = sb("mo_scatter_ix", [CAP, Q, 2], U32)
        wgu = sb("mo_wgu", [P, 2, 2, 2, KC, I])
        wd = sb("mo_wd", [P, 2, 2, IC, D])
        sgu = sb("mo_sgu", [P, 2, 2, KC, IS], F32R)
        sd = sb("mo_sd", [SM, 2, SC, D], F32R)
        x2 = sb("mo_x2", [P, KC, SEQ])
        x2s = sb("mo_x2s", [P, 2, KC, SEQ], F32R)
        hs = sb("mo_hs", [SM, 2, SC, SEQ], F32R)
        ssil = sb("mo_ssil", [SM, SEQ])
        sh = sb("mo_sh", [SM, 2, SEQ])
        so = sb("mo_so", [P, NT, D])
        xg = sb("mo_xg", [P, 2, D + E])
        xgT = sb("mo_xgT", [P, KC, P])
        wcol = sb("mo_wcol", [P, 2])
        sil = sb("mo_sil", [P, I])
        hm = sb("mo_hm", [P, I])
        hmT = sb("mo_hmT", [P, IC, P])
        y = sb("mo_y", [CAP, 2, 2, D])
        ps = ctx.enter_context(nc.psum_tensor("mo_ps", [P, 8, 512], F32))

        consts_in = sem("mo_consts_in")
        zeros_set = sem("mo_zeros_set")
        pads_in = sem("mo_pads_in")
        table_in = sem("mo_table_in")
        staged = [sem(f"mo_staged{j}") for j in range(2)]
        shi_done = sem("mo_shi_done")
        slo_done = sem("mo_slo_done")
        w_in = [sem(f"mo_w_in{j}") for j in range(2)]
        x2_in = sem("mo_x2_in")
        x2hi_ready = sem("mo_x2hi_ready")
        x2lo_ready = sem("mo_x2lo_ready")
        gix_ready = sem("mo_gix_ready")
        six_ready = sem("mo_six_ready")
        rows_in = [sem(f"mo_rows_in{j}") for j in range(2)]
        rows_turned = sem("mo_rows_turned")
        rowsT_ready = sem("mo_rowsT_ready")
        wcol_ready = sem("mo_wcol_ready")
        gate_up_done = sem("mo_gate_up_done")
        silu_done = sem("mo_silu_done")
        hidden_ready = sem("mo_hidden_ready")
        hidden_turned = sem("mo_hidden_turned")
        hiddenT_ready = sem("mo_hiddenT_ready")
        down_done = sem("mo_down_done")
        ya_ready = sem("mo_ya_ready")
        yb_ready = sem("mo_yb_ready")
        s_gate_done = sem("mo_s_gate_done")
        s_up_done = sem("mo_s_up_done")
        s_silu_done = sem("mo_s_silu_done")
        s_mult_done = sem("mo_s_mult_done")
        s_hi_done = sem("mo_s_hi_done")
        s_lo_done = sem("mo_s_lo_done")
        s_down_done = sem("mo_s_down_done")
        so_ready = sem("mo_so_ready")
        added = sem("mo_added")
        carried = sem("mo_carried")
        block = ctx.enter_context(nc.Block())

        stage = [wgu[:, j].rearrange("p e g k i -> p (e g k i)")[:, 0:KC * IS] for j in range(2)]
        staged_d = wd[:].rearrange("p b e c d -> p (b e c d)")[0:SM, 0:SC * D]

        def adds_before(i, q):
            return (2 * Q + 1) * i - 2 * (Q - 2) - 1 + 2 * q + (1 if q >= 2 else 0)

        def steps(engine, body):
            body(0)
            with engine.Fori(1, NSEQ) as i:
                body(i)

        @block.sync
        def _(sp):
            sp.dma_start(ident[:], ident_in).then_inc(consts_in, 16)
            for j, w in enumerate((sw_gate, sw_up)):
                sp.dma_start(stage[j].rearrange("p (k i) -> p k i", k=KC), w.rearrange("(k p) i -> p k i", p=P))\
                    .then_inc(staged[0], 16)
            for c in range(SC):
                sp.dma_start(staged_d[0:SW[c], c * D:(c + 1) * D], sw_down[SO[c]:SO[c] + SW[c], :])\
                    .then_inc(staged[1], 16)
            sp.wait_ge(zeros_set, 1)
            sp.dma_start(xrow[T:T + CAP, :], zeros[:]).then_inc(pads_in, 16)
            sp.dma_start(acc[T:T + CAP, :], zeros[:, 0:D]).then_inc(pads_in, 16)
            with nc.allow_non_contiguous_dma(reason="one word for each slot"):
                sp.dma_start(gather_all[:], slot_table.rearrange("(q c) a -> c (q a)", c=P)).then_inc(table_in, 16)
                sp.dma_start(scatter_all[:], slot_table.rearrange("(e c) a -> c (e a)", c=CAP)).then_inc(table_in, 16)

            def body(i):
                for q in range(Q):
                    p = Q * i + q
                    j = q % 2
                    if q == 0:
                        wait(sp, x2hi_ready, i)
                        wait(sp, x2lo_ready, i)
                        sp.dma_start(x2[:], x2T_dram[i]).then_inc(x2_in, 16)
                    if type(p) is int and p < 2:
                        sp.wait_ge(slo_done, 3)
                    wait(sp, gate_up_done, p - 1)
                    for e in range(2):
                        for g, w in enumerate((w_gate, w_up)):
                            sp.dma_start(wgu[:, j, e, g], w[2 * p + e].rearrange("(p k) i -> p k i", k=KC))\
                                .then_inc(w_in[j], 16)
                    wait(sp, down_done, p - 1)
                    for e in range(2):
                        sp.dma_start(wd[:, j, e, 0:IC - 1, :],
                                     w_down[2 * p + e][0:(IC - 1) * P, :].rearrange("(c p) d -> p c d", p=P))\
                            .then_inc(w_in[j], 16)
                        sp.dma_start(wd[0:IW[-1], j, e, IC - 1, :], w_down[2 * p + e][(IC - 1) * P:I, :])\
                            .then_inc(w_in[j], 16)

            steps(sp, body)
            sp.wait_ge(pads_in, 32)

        @block.tensor
        def _(pe):
            M = nc.tensor
            pe.wait_ge(consts_in, 16)
            pe.wait_ge(slo_done, 3)

            def shared_in(i, c, g):
                n = SC * i + c
                if c == 0 and g == 0:
                    pe.wait_ge(x2hi_ready, i + 1)
                    pe.wait_ge(x2lo_ready, i + 1)
                wait(pe, s_mult_done, n)
                k3 = 0
                for k in range(KC):
                    for xa, wa in ((0, 0), (0, 1), (1, 0)):
                        m = M.matmul(ps[0:SW[c], 5 + g, 0:SEQ], sgu[:, wa, g, k, SO[c]:SO[c] + SW[c]],
                                     x2s[:, xa, k, :], start=(k3 == 0), stop=(k3 == 3 * KC - 1))
                        k3 += 1
                m.then_inc((s_gate_done, s_up_done)[g], 1)

            def shared_out(i, s):
                wait(pe, so_ready, NT * i + s)
                if s == 0:
                    pe.wait_ge(s_hi_done, SC * (i + 1))
                    pe.wait_ge(s_lo_done, SC * (i + 1))
                k3 = 0
                for c in range(SC):
                    for xa, wa in ((0, 0), (0, 1), (1, 0)):
                        m = M.matmul(ps[:, 7, :], hs[0:SW[c], xa, c, s * P:(s + 1) * P], sd[0:SW[c], wa, c, :],
                                     start=(k3 == 0), stop=(k3 == 3 * SC - 1))
                        k3 += 1
                m.then_inc(s_down_done, 1)

            def body(i):
                for q in range(Q):
                    p = Q * i + q
                    j = q % 2
                    use = 2 * i + q // 2 + 1
                    pe.wait_ge(rows_in[j], 16 * use)
                    wait(pe, rowsT_ready, p)
                    for k in range(KC):
                        m = M.transpose(ps[:, 0, k * P:(k + 1) * P], xg[:, j, k:D:KC], ident[:])
                    m.then_inc(rows_turned, 1)
                    if q < Q - 1:
                        shared_in(i, 2 * q, 0)
                        shared_in(i, 2 * q, 1)
                    else:
                        shared_out(i, 0)
                    pe.wait_ge(rowsT_ready, p + 1)
                    pe.wait_ge(w_in[j], 16 * 8 * use)
                    wait(pe, hidden_ready, p)
                    for g in range(2):
                        for k in range(KC):
                            for e in range(2):
                                m = M.matmul(ps[CAP * e:CAP * (e + 1), 1 + g, 0:I], xgT[:, k, CAP * e:CAP * (e + 1)],
                                             wgu[:, j, e, g, k, :], start=(k == 0), stop=(k == KC - 1))
                    m.then_inc(gate_up_done, 1)
                    if q < Q - 1:
                        shared_in(i, 2 * q + 1, 0)
                    else:
                        shared_out(i, 1)
                    pe.wait_ge(hidden_ready, p + 1)
                    wait(pe, hiddenT_ready, p)
                    for c in range(IC):
                        m = M.transpose(ps[0:IW[c], 3, c * P:(c + 1) * P], hm[:, c * P:c * P + IW[c]], ident[:])
                    m.then_inc(hidden_turned, 1)
                    if q < Q - 1:
                        shared_in(i, 2 * q + 1, 1)
                    else:
                        shared_out(i, 2)
                    pe.wait_ge(hiddenT_ready, p + 1)
                    wait(pe, ya_ready, p)
                    wait(pe, yb_ready, p)
                    for c in range(IC):
                        for e in range(2):
                            m = M.matmul(ps[CAP * e:CAP * (e + 1), 4, :], hmT[0:IW[c], c, CAP * e:CAP * (e + 1)],
                                         wd[0:IW[c], j, e, c, :], start=(c == 0), stop=(c == IC - 1))
                    m.then_inc(down_done, 1)

            steps(pe, body)

        @block.scalar
        def _(act):
            A = nc.scalar
            act.wait_ge(staged[0], 32)
            for g in range(2):
                A.activation(sgu[:, 0, g].rearrange("p k i -> p (k i)"), stage[g], ACT.Copy).then_inc(shi_done, 1)
            act.wait_ge(staged[1], 16 * SC)
            for c in range(SC):
                m = A.activation(sd[0:SW[c], 0, c], staged_d[0:SW[c], c * D:(c + 1) * D], ACT.Copy)
            m.then_inc(shi_done, 1)

            def split_x2(i):
                act.wait_ge(x2_in, 16 * (i + 1))
                wait(act, s_up_done, SC * i)
                A.activation(x2s[:, 0], x2[:], ACT.Copy).then_inc(x2hi_ready, 1)

            def silu_shared(i, c):
                n = SC * i + c
                act.wait_ge(s_gate_done, n + 1)
                wait(act, s_mult_done, n)
                A.activation(ssil[0:SW[c], :], ps[0:SW[c], 5, 0:SEQ], ACT.Silu).then_inc(s_silu_done, 1)

            def hi_shared(i, c):
                n = SC * i + c
                act.wait_ge(s_mult_done, n + 1)
                if c == 0:
                    wait(act, s_down_done, NT * i)
                A.activation(hs[0:SW[c], 0, c, :], sh[0:SW[c], c % 2, :], ACT.Copy).then_inc(s_hi_done, 1)

            def body(i):
                for q in range(Q):
                    p = Q * i + q
                    if q == 0:
                        split_x2(i)
                    if q < Q - 1:
                        silu_shared(i, 2 * q)
                    act.wait_ge(gate_up_done, p + 1)
                    wait(act, hidden_ready, p)
                    A.activation(sil[:], ps[:, 1, 0:I], ACT.Silu).then_inc(silu_done, 1)
                    if q < Q - 1:
                        hi_shared(i, 2 * q)
                        silu_shared(i, 2 * q + 1)
                        hi_shared(i, 2 * q + 1)
                    act.wait_ge(down_done, p + 1)
                    wait(act, added, 16 * (adds_before(i, q) + 1))
                    A.activation(y[:, q % 2, 0, :], ps[0:CAP, 4, :], ACT.Copy).then_inc(ya_ready, 1)

            steps(act, body)

        @block.vector
        def _(dve):
            V = nc.vector
            V.memset(zeros[:], 0.0).then_inc(zeros_set, 1)
            for g in range(2):
                dve.wait_ge(shi_done, g + 1)
                V.tensor_tensor(sgu[:, 1, g].rearrange("p k i -> p (k i)"), stage[g],
                                sgu[:, 0, g].bitcast(F32).rearrange("p k i -> p (k i)"), ALU.subtract)\
                    .then_inc(slo_done, 1)
            dve.wait_ge(shi_done, 3)
            for c in range(SC):
                m = V.tensor_tensor(sd[0:SW[c], 1, c], staged_d[0:SW[c], c * D:(c + 1) * D],
                                    sd[0:SW[c], 0, c].bitcast(F32), ALU.subtract)
            m.then_inc(slo_done, 1)

            def mult_shared(i, c):
                n = SC * i + c
                dve.wait_ge(s_silu_done, n + 1)
                dve.wait_ge(s_up_done, n + 1)
                wait(dve, s_hi_done, n - 1)
                V.tensor_tensor(sh[0:SW[c], c % 2, :], ssil[0:SW[c], :], ps[0:SW[c], 6, 0:SEQ], ALU.mult)\
                    .then_inc(s_mult_done, 1)

            def lo_shared(i, c):
                n = SC * i + c
                dve.wait_ge(s_hi_done, n + 1)
                V.tensor_tensor(hs[0:SW[c], 1, c, :], sh[0:SW[c], c % 2, :], hs[0:SW[c], 0, c, :].bitcast(F32),
                                ALU.subtract).then_inc(s_lo_done, 1)

            def out_shared(i, s):
                dve.wait_ge(s_down_done, NT * i + s + 1)
                wait(dve, added, 16 * adds_before(i, 2) if type(i) is not int or i > 0 else 0)
                V.tensor_copy(so[:, s, :], ps[:, 7, :]).then_inc(so_ready, 1)

            def body(i):
                for q in range(Q):
                    p = Q * i + q
                    j = q % 2
                    if q == 0:
                        dve.wait_ge(x2hi_ready, i + 1)
                        V.tensor_tensor(x2s[:, 1], x2[:], x2s[:, 0].bitcast(F32), ALU.subtract)\
                            .then_inc(x2lo_ready, 1)
                    dve.wait_ge(rows_turned, p + 1)
                    wait(dve, gate_up_done, p)
                    V.tensor_copy(xgT[:].rearrange("p k t -> p (k t)"), ps[:, 0, :]).then_inc(rowsT_ready, 1)
                    V.tensor_copy(wcol[0:CAP, j:j + 1], xg[0:CAP, j, bass.ds(D + 2 * p, 1)])
                    V.tensor_copy(wcol[CAP:P, j:j + 1], xg[CAP:P, j, bass.ds(D + 2 * p + 1, 1)])\
                        .then_inc(wcol_ready, 1)
                    if q < Q - 1:
                        mult_shared(i, 2 * q)
                    else:
                        out_shared(i, 0)
                    dve.wait_ge(silu_done, p + 1)
                    dve.wait_ge(wcol_ready, p + 1)
                    wait(dve, hidden_turned, p)
                    V.scalar_tensor_tensor(out=hm[:], in0=sil[:], scalar=wcol[:, j:j + 1], in1=ps[:, 2, 0:I],
                                           op0=ALU.mult, op1=ALU.mult).then_inc(hidden_ready, 1)
                    if q == Q - 1:
                        out_shared(i, 1)
                    dve.wait_ge(hidden_turned, p + 1)
                    wait(dve, down_done, p)
                    V.tensor_copy(hmT[:, 0:IC - 1, :], ps[:, 3, 0:(IC - 1) * P].rearrange("p (c t) -> p c t", t=P))
                    V.tensor_copy(hmT[0:IW[-1], IC - 1, :], ps[0:IW[-1], 3, (IC - 1) * P:IC * P])\
                        .then_inc(hiddenT_ready, 1)
                    if q < Q - 1:
                        lo_shared(i, 2 * q)
                        mult_shared(i, 2 * q + 1)
                        lo_shared(i, 2 * q + 1)
                    else:
                        out_shared(i, 2)
                    dve.wait_ge(down_done, p + 1)
                    wait(dve, added, 16 * (adds_before(i, q) + 2))
                    V.tensor_copy(y[:, j, 1, :], ps[CAP:P, 4, :]).then_inc(yb_ready, 1)

            steps(dve, body)

        @block.gpsimd
        def _(pool):
            G = nc.gpsimd
            pool.wait_ge(table_in, 32)
            pool.wait_ge(pads_in, 32)

            def add_pair(n, p, jy, qix):
                for e in range(2):
                    wait(pool, added, 16 * (n + e))
                    wait_apart(pool, (ya_ready, yb_ready)[e], p + 1, carried)
                    G.indirect_dma_start(acc, bass.IndirectOffsetOnAxis(ap=scatter_ix[:, qix, e:e + 1], axis=0),
                                         y[:, jy, e, :], None, compute_op=ALU.add).then_inc(added, 16)

            def add_shared(n, i):
                pool.wait_ge(so_ready, NT * (i + 1))
                pool.wait_ge(added, 16 * n)
                G.dma_start(acc[bass.ds(i * SEQ, SEQ), :].rearrange("(s p) d -> p s d", p=P), so[:],
                            accum_op=ALU.add).then_inc(added, 16)

            def body(i):
                peeled = type(i) is int and i == 0
                for q in range(Q):
                    p = Q * i + q
                    j = q % 2
                    wait(pool, rows_in[j], 16 * (2 * i + q // 2))
                    wait(pool, rows_turned, p - 1)
                    wait(pool, wcol_ready, p - 1)
                    G.tensor_copy(gather_ix[:, q:q + 1], gather_all[:, bass.ds(p, 1)]).then_inc(gix_ready, 1)
                    wait_apart(pool, gix_ready, p + 1, carried)
                    G.indirect_dma_start(xg[:, j, :], None, xrow,
                                         bass.IndirectOffsetOnAxis(ap=gather_ix[:, q:q + 1], axis=0))\
                        .then_inc(rows_in[j], 16)
                    if not (peeled and q < 2):
                        add_pair(adds_before(i, q), p - 2, j, (q + 2) % Q)
                    G.tensor_copy(scatter_ix[:, q, :], scatter_all[:, bass.ds(2 * p, 2)]).then_inc(six_ready, 1)
                    pool.wait_ge(six_ready, p + 1)
                    if q == 1 and not peeled:
                        add_shared(adds_before(i, q) + 2, i - 1)

            steps(pool, body)
            n = adds_before(NSEQ, 0)
            for q in range(2):
                add_pair(n, PAIRS - 2 + q, q, Q - 2 + q)
                n += 2
            add_shared(n, NSEQ - 1)
            pool.wait_ge(added, 16 * (n + 1))


_INS = ['x', 'txt', 'L0_tok_log_dt', 'L0_tok_B_ri', 'L0_tok_inv_A_real', 'L0_tok_A_imag',
        'L0_attn_Wq', 'L0_attn_Wk', 'L0_attn_Wv', 'L0_attn_Wo', 'L0_ffn_gate_w',
        'L0_ffn_w_gate', 'L0_ffn_w_up', 'L0_ffn_w_down', 'L0_ffn_sw_gate', 'L0_ffn_sw_up', 'L0_ffn_sw_down']


def build(nc, a, out):
    B, S0, _, _ = a["x"].shape
    S1, D = a["txt"].shape[1:]
    SEQ = S0 + S1
    E = a["L0_ffn_gate_w"].shape[0]
    CAP = out.shape[0] - B * SEQ
    KC = D // P
    h = nc.dram_tensor("tokens_h", (B, S0, D), F32).ap()
    xrow = nc.dram_tensor("rows_scores", (B * SEQ + CAP, D + E), F32).ap()
    x2T = nc.dram_tensor("rows_turned", (B, P, KC, SEQ), F32).ap()
    table = nc.dram_tensor("slot_table", (E * CAP, 1), U32).ap()
    with ExitStack() as ctx:
        NX = sum(a["L0_attn_W" + w].shape[0] for w in "qkv")
        WxT = ctx.enter_context(nc.sbuf_tensor("WxT", [P, 2, KC, NX], F32R))
        WoT = ctx.enter_context(nc.sbuf_tensor("WoT", [P, 2, KC, D], F32R))
        gwT = ctx.enter_context(nc.sbuf_tensor("gwT", [P, KC, E], F32))
        transposed_weights_phase(nc, *[a["L0_attn_W" + w] for w in "qkvo"], a["L0_ffn_gate_w"], a["ident"],
                                 WxT, WoT, gwT)
        state_space_phase(nc, a["x"], *[a["L0_tok_" + w] for w in ("log_dt", "B_ri", "inv_A_real", "A_imag")],
                          a["ident"], h)
        attention_phase(nc, h, a["txt"], [a[w] for w in ("cos", "sin", "ident", "upper", "tok", "slot")],
                        WxT, WoT, gwT, out, xrow, x2T, table, a["empty"])
    experts_phase(nc, out, xrow, x2T, table, *[a["L0_ffn_" + w] for w in
                  ("w_gate", "w_up", "w_down", "sw_gate", "sw_up", "sw_down")], a["ident"])


def kernel(**inputs):
    import concourse.bacc as bacc
    from concourse.bass_utils import run_bass_kernel_spmd

    nc = bacc.Bacc("TRN2", target_bir_lowering=False, num_devices=1)
    B, S0 = inputs["x"].shape[:2]
    SEQ = S0 + inputs["txt"].shape[1]
    D = inputs["txt"].shape[2]
    CAP = 64
    arrays = {name: np.ascontiguousarray(inputs[name]) for name in _INS}
    arrays.update(shape_constants(B, SEQ, inputs["L0_ffn_gate_w"].shape[0], CAP))
    arrays = {f"in_{name}": np.ascontiguousarray(a) for name, a in arrays.items()}
    aps = {name[3:]: nc.dram_tensor(name, a.shape, mybir.dt.from_np(a.dtype), kind="ExternalInput").ap()
           for name, a in arrays.items()}
    out = nc.dram_tensor("out_rows", (B * SEQ + CAP, D), F32, kind="ExternalOutput").ap()
    build(nc, aps, out)
    r = run_bass_kernel_spmd(nc, [arrays], core_ids=[0])
    return r.results[0]["out_rows"][:B * SEQ].reshape(B, SEQ, D)
```

```python
from contextlib import ExitStack

import numpy as np

import concourse.bass as bass
from concourse import mybir

F32 = mybir.dt.float32
F32R = mybir.dt.float32r
BF16 = mybir.dt.bfloat16
U32 = mybir.dt.uint32
ALU = mybir.AluOpType
ACT = mybir.ActivationFunctionType
AX = mybir.AxisListType
P = 128


def state_space_phase(nc, x, log_dt, B_ri, inv_A_real, A_imag, ident_in, h_dram):
    CH, H, N, _ = x.shape
    L = h_dram.shape[2]
    STEP = 64
    NA = L // STEP
    HALF = H // 2
    CHUNK = 32
    NCHUNK = HALF // CHUNK
    CA = CH * NA
    with ExitStack() as ctx:
        def sb(name, shape, dt=F32):
            return ctx.enter_context(nc.sbuf_tensor(name, shape, dt))

        def ps(name, shape, dt=F32):
            return ctx.enter_context(nc.psum_tensor(name, shape, dt))

        def sem(name):
            return ctx.enter_context(nc.semaphore(name))

        C = sb("ss_C", [P, CH, 2, N, 2])
        Bn = sb("ss_B", [P, 2, N, 2])
        ar = sb("ss_ar", [P, 2, N])
        ai = sb("ss_ai", [P, 2, N])
        dt = sb("ss_dt", [P, 2])
        ident = sb("ss_ident", [P, P])
        xr = sb("ss_xr", [P, 2, N])
        xi = sb("ss_xi", [P, 2, N])
        dr = sb("ss_dr", [P, 2, N])
        inv = sb("ss_inv", [P, 2, N])
        t1 = sb("ss_t1", [P, 2, N])
        t2 = sb("ss_t2", [P, 2, N])
        t3 = sb("ss_t3", [P, 2, N])
        zg = sb("ss_zg", [P, 4, 2, N])
        zgT = sb("ss_zgT", [P, 4, HALF])
        E = sb("ss_E", [P, 2, CH, HALF])
        e1 = sb("ss_e1", [P, CH, HALF])
        e2 = sb("ss_e2", [P, CH, HALF])
        zp = sb("ss_zp", [P, 2, 7, HALF])
        Za = sb("ss_Za", [P, 2, NA, HALF])
        sq = sb("ss_sq", [P, 2, NA, HALF])
        Pm = sb("ss_P", [P, 2, 2, CHUNK, CA])
        Qm = sb("ss_Q", [P, 2, 2, CHUNK, STEP])
        tp = sb("ss_tp", [P, 2, CHUNK, NA])
        tq = sb("ss_tq", [P, 2, CHUNK * STEP // 2])
        out = sb("ss_out", [P, 2, CHUNK, STEP])
        psT = ps("ss_psT", [P, 5, 4, P])
        psK = ps("ss_psK", [P, 2, 512])

        loaded = sem("ss_loaded")
        exps = sem("ss_exps")
        zg_ready = sem("ss_zg_ready")
        turned = sem("ss_turned")
        powers = sem("ss_powers")
        p_ready = sem("ss_p_ready")
        q_ready = sem("ss_q_ready")
        multiplied = sem("ss_multiplied")
        evacuated = sem("ss_evacuated")
        stored = [sem(f"ss_stored{j}") for j in range(2)]
        dve_step = sem("ss_dve_step")
        pool_step = sem("ss_pool_step")
        block = ctx.enter_context(nc.Block())
        HPB = 512 // STEP
        NBANK = CHUNK // HPB

        @block.sync
        def _(sp):
            sp.dma_start(ar[:], inv_A_real.rearrange("(s p) n -> p s n", p=P)).then_inc(loaded, 16)
            sp.dma_start(ai[:], A_imag.rearrange("(s p) n -> p s n", p=P)).then_inc(loaded, 16)
            with nc.allow_non_contiguous_dma(reason="256 values of log_dt"):
                sp.dma_start(dt[:], log_dt.rearrange("(s p) -> p s", p=P)).then_inc(loaded, 16)
            sp.dma_start(Bn[:].rearrange("p s n r -> p s (n r)"),
                         B_ri.rearrange("(s p) n r -> p s (n r)", p=P)).then_inc(loaded, 16)
            sp.dma_start(ident[:], ident_in).then_inc(loaded, 16)
            for s in range(2):
                sp.dma_start(C[:, :, s].rearrange("p c n r -> p c (n r)"),
                             x[:, s * P:(s + 1) * P].rearrange("c p n r -> p c (n r)")).then_inc(loaded, 16)
            for k in range(NCHUNK):
                sp.wait_ge(evacuated, NBANK * (k + 1))
                for s in range(2):
                    h0 = s * HALF + k * CHUNK
                    for c in range(CH):
                        q0 = s * CA + c * NA
                        sp.dma_start(h_dram[c, h0:h0 + CHUNK, :].rearrange("h (a b) -> a h b", b=STEP),
                                     out[q0:q0 + NA, k % 2]).then_inc(stored[k % 2], 16)
            for j in range(2):
                sp.wait_ge(stored[j], 16 * 2 * CH * NCHUNK // 2)

        @block.scalar
        def _(act):
            act.wait_ge(loaded, 16 * 7)
            nc.scalar.activation(ar[:], ar[:], ACT.Exp).then_inc(exps, 1)
            nc.scalar.activation(dt[:], dt[:], ACT.Exp).then_inc(exps, 1)
            for k in range(NCHUNK):
                if k >= 2:
                    act.wait_ge(stored[k % 2], 16 * 2 * CH * (k // 2))
                for j in range(NBANK):
                    n = k * NBANK + j
                    act.wait_ge(multiplied, n + 1)
                    nc.scalar.activation(out[:, k % 2, j * HPB:(j + 1) * HPB, :].rearrange("p h b -> p (h b)"),
                                         psK[:, n % 2, :], ACT.Copy).then_inc(evacuated, 1)

        @block.vector
        def _(dve):
            chain = [0]

            def link(ins):
                chain[0] += 1
                ins.then_inc(dve_step, 1)
                dve.wait_ge(dve_step, chain[0])

            dve.wait_ge(exps, 2)
            V = nc.vector
            for s in range(2):
                V.tensor_scalar(xr[:, s], ar[:, s], dt[:, s:s + 1], -0.5, ALU.mult, ALU.mult)
                link(V.tensor_scalar(xi[:, s], ai[:, s], dt[:, s:s + 1], 0.5, ALU.mult, ALU.mult))
            V.tensor_scalar(dr[:], xr[:], -1.0, 1.0, ALU.mult, ALU.add)
            V.tensor_tensor(t1[:], xr[:], xr[:], ALU.mult)
            link(V.tensor_tensor(t2[:], xi[:], xi[:], ALU.mult))
            link(V.tensor_tensor(inv[:], dr[:], dr[:], ALU.mult))
            link(V.tensor_tensor(inv[:], inv[:], t2[:], ALU.add))
            link(V.reciprocal(inv[:], inv[:]))
            link(V.tensor_tensor(t1[:], t1[:], t2[:], ALU.add))
            link(V.tensor_scalar(t1[:], t1[:], -1.0, 1.0, ALU.mult, ALU.add))
            V.tensor_tensor(zg[:, 0], t1[:], inv[:], ALU.mult)
            link(V.scalar_tensor_tensor(out=zg[:, 1], in0=xi[:], scalar=2.0, in1=inv[:], op0=ALU.mult, op1=ALU.mult))
            for s in range(2):
                link(V.tensor_scalar(inv[:, s], inv[:, s], dt[:, s:s + 1], 2.0, ALU.mult, ALU.mult))
            V.tensor_tensor(t1[:], Bn[:, :, :, 0], dr[:], ALU.mult)
            V.tensor_tensor(t2[:], Bn[:, :, :, 1], xi[:], ALU.mult)
            V.tensor_tensor(t3[:], Bn[:, :, :, 0], xi[:], ALU.mult)
            link(V.tensor_tensor(xr[:], Bn[:, :, :, 1], dr[:], ALU.mult))
            V.tensor_tensor(t1[:], t1[:], t2[:], ALU.subtract)
            link(V.tensor_tensor(t3[:], t3[:], xr[:], ALU.add))
            V.tensor_tensor(zg[:, 2], t1[:], inv[:], ALU.mult)
            V.tensor_tensor(zg[:, 3], t3[:], inv[:], ALU.mult).then_inc(zg_ready, 1)

            dve.wait_ge(turned, 1)
            link(V.tensor_copy(zgT[:], psT[:, 0]))
            dve.wait_ge(turned, 2)
            Cr = psT[:, 1:3].rearrange("p u v h -> p (u v) h")
            Ci = psT[:, 3:5].rearrange("p u v h -> p (u v) h")
            g = [zgT[:, 2 + r:3 + r, :].to_broadcast([P, CH, HALF]) for r in range(2)]
            V.tensor_tensor(e1[:], Cr, g[0], ALU.mult)
            link(V.tensor_tensor(e2[:], Ci, g[1], ALU.mult))
            link(V.tensor_tensor(E[:, 0], e1[:], e2[:], ALU.subtract))
            V.tensor_tensor(e1[:], Cr, g[1], ALU.mult)
            link(V.tensor_tensor(e2[:], Ci, g[0], ALU.mult))
            V.tensor_tensor(E[:, 1], e1[:], e2[:], ALU.add)

            link(V.tensor_copy(zp[:, :, 0, :], zgT[:, 0:2, :]))
            for k in range(6):
                a, b = zp[:, 0, k], zp[:, 1, k]
                V.tensor_tensor(sq[:, 0, 0], a, a, ALU.mult)
                V.tensor_tensor(sq[:, 0, 1], b, b, ALU.mult)
                link(V.tensor_tensor(sq[:, 0, 2], a, b, ALU.mult))
                V.tensor_tensor(zp[:, 0, k + 1], sq[:, 0, 0], sq[:, 0, 1], ALU.subtract)
                link(V.tensor_scalar(zp[:, 1, k + 1], sq[:, 0, 2], 2.0, None, ALU.mult))
            V.memset(Za[:, 0, 0], 1.0)
            V.memset(Za[:, 1, 0], 0.0)
            link(V.tensor_copy(Za[:, :, 1, :], zp[:, :, 6, :]))
            n = 2
            while n < NA:
                a, b = Za[:, 0, n // 2], Za[:, 1, n // 2]
                V.tensor_tensor(sq[:, 0, 0], a, a, ALU.mult)
                V.tensor_tensor(sq[:, 0, 1], b, b, ALU.mult)
                link(V.tensor_tensor(sq[:, 0, 2], a, b, ALU.mult))
                V.tensor_tensor(Za[:, 0, n], sq[:, 0, 0], sq[:, 0, 1], ALU.subtract)
                link(V.tensor_scalar(Za[:, 1, n], sq[:, 0, 2], 2.0, None, ALU.mult))
                m = n - 1
                u = [Za[:, r, n:n + 1, :].to_broadcast([P, m, HALF]) for r in range(2)]
                v = [Za[:, r, 1:n, :] for r in range(2)]
                V.tensor_tensor(Za[:, 0, n + 1:2 * n], u[0], v[0], ALU.mult)
                link(V.tensor_tensor(sq[:, 0, 0:m], u[1], v[1], ALU.mult))
                V.tensor_tensor(Za[:, 1, n + 1:2 * n], u[0], v[1], ALU.mult)
                link(V.tensor_tensor(sq[:, 1, 0:m], u[1], v[0], ALU.mult))
                V.tensor_tensor(Za[:, 0, n + 1:2 * n], Za[:, 0, n + 1:2 * n], sq[:, 0, 0:m], ALU.subtract)
                link(V.tensor_tensor(Za[:, 1, n + 1:2 * n], Za[:, 1, n + 1:2 * n], sq[:, 1, 0:m], ALU.add))
                n *= 2
            dve.sem_inc(powers, 1)

            for k in range(NCHUNK):
                hs = slice(k * CHUNK, (k + 1) * CHUNK)
                if k >= 2:
                    dve.wait_ge(multiplied, NBANK * (k - 1))
                za = [Za[:, r, :, hs].rearrange("p a h -> p h a") for r in range(2)]
                for c in range(CH):
                    pr = Pm[:, k % 2, 0, :, c * NA:(c + 1) * NA]
                    pi = Pm[:, k % 2, 1, :, c * NA:(c + 1) * NA]
                    er = E[:, 0, c, hs].rearrange("p (h a) -> p h a", a=1).to_broadcast([P, CHUNK, NA])
                    ei = E[:, 1, c, hs].rearrange("p (h a) -> p h a", a=1).to_broadcast([P, CHUNK, NA])
                    V.tensor_tensor(pr, er, za[0], ALU.mult)
                    V.tensor_tensor(tp[:, 0], ei, za[1], ALU.mult)
                    V.tensor_tensor(tp[:, 1], er, za[1], ALU.mult)
                    link(V.scalar_tensor_tensor(out=pi, in0=ei, scalar=-1.0, in1=za[0], op0=ALU.mult, op1=ALU.mult))
                    V.tensor_tensor(pr, pr, tp[:, 0], ALU.subtract)
                    link(V.tensor_tensor(pi, pi, tp[:, 1], ALU.subtract))
                dve.sem_inc(p_ready, 1)

        @block.gpsimd
        def _(pool):
            chain = [0]

            def link(ins):
                chain[0] += 1
                ins.then_inc(pool_step, 1)
                pool.wait_ge(pool_step, chain[0])

            G = nc.gpsimd
            pool.wait_ge(powers, 1)
            for k in range(NCHUNK):
                hs = slice(k * CHUNK, (k + 1) * CHUNK)
                if k >= 2:
                    pool.wait_ge(multiplied, NBANK * (k - 1))
                q = [Qm[:, k % 2, r] for r in range(2)]
                G.memset(q[0][:, :, 0:1], 1.0)
                G.memset(q[1][:, :, 0:1], 0.0)
                for r in range(2):
                    link(G.tensor_copy(q[r][:, :, 1], zp[:, r, 0, hs]))
                n = 2
                lev = 1
                while n < STEP:
                    z = [zp[:, r, lev, hs].rearrange("p (h a) -> p h a", a=1).to_broadcast([P, CHUNK, n]) for r in range(2)]
                    t = [tq[:, r, 0:CHUNK * n].rearrange("p (h a) -> p h a", a=n) for r in range(2)]
                    G.tensor_tensor(q[0][:, :, n:2 * n], q[0][:, :, 0:n], z[0], ALU.mult)
                    G.tensor_tensor(t[0], q[1][:, :, 0:n], z[1], ALU.mult)
                    G.tensor_tensor(q[1][:, :, n:2 * n], q[0][:, :, 0:n], z[1], ALU.mult)
                    link(G.tensor_tensor(t[1], q[1][:, :, 0:n], z[0], ALU.mult))
                    G.tensor_tensor(q[0][:, :, n:2 * n], q[0][:, :, n:2 * n], t[0], ALU.subtract)
                    link(G.tensor_tensor(q[1][:, :, n:2 * n], q[1][:, :, n:2 * n], t[1], ALU.add))
                    n *= 2
                    lev += 1
                pool.sem_inc(q_ready, 1)

        @block.tensor
        def _(pe):
            T = nc.tensor
            pe.wait_ge(loaded, 16 * 7)
            for r in range(2):
                for c in range(CH):
                    T.transpose(psT[:, 1 + 2 * r + c // 4, c % 4, :], C[:, c, :, :, r].rearrange("p s n -> p (s n)"), ident[:])
            pe.wait_ge(zg_ready, 1)
            for j in range(4):
                m = T.transpose(psT[:, 0, j, :], zg[:, j].rearrange("p s n -> p (s n)"), ident[:])
            m.then_inc(turned, 2)
            for k in range(NCHUNK):
                pe.wait_ge(p_ready, k + 1)
                pe.wait_ge(q_ready, k + 1)
                for j in range(NBANK):
                    n = k * NBANK + j
                    if n >= 2:
                        pe.wait_ge(evacuated, n - 1)
                    for i in range(HPB):
                        h = j * HPB + i
                        for r in range(2):
                            for s in range(2):
                                m = T.matmul(psK[64 * s:64 * s + 64, n % 2, i * STEP:(i + 1) * STEP],
                                             Pm[64 * s:64 * s + 64, k % 2, r, h, :],
                                             Qm[64 * s:64 * s + 64, k % 2, r, h, :],
                                             start=(r == 0), stop=(r == 1))
                    m.then_inc(multiplied, 1)
ROUTE_STEPS = 22


def shape_constants(B, SEQ, E, CAP):
    HD = 32
    NT = SEQ // P
    inv = (np.float32(1.0) / np.float32(10000.0) ** (np.arange(0, HD, 2, dtype=np.float32) / np.float32(HD))).astype(np.float32)
    f = np.arange(SEQ, dtype=np.float32)[:, None] * inv[None]
    emb = np.concatenate([f, f], axis=-1)
    sign = np.where(np.arange(HD) < HD // 2, -1.0, 1.0).astype(np.float32)
    tiles = lambda a: np.ascontiguousarray(a.reshape(NT, P, HD).transpose(1, 0, 2))
    t = np.arange(P)
    return {
        "cos": tiles(np.cos(emb).astype(np.float32)),
        "sin": tiles(np.sin(emb).astype(np.float32) * sign),
        "ident": np.eye(P, dtype=np.float32),
        "upper": np.stack([(t[:, None] < t[None]).astype(np.float32), np.ones((P, P), np.float32)], axis=1),
        "tok": (t[:, None] + P * np.arange(NT)[None]).astype(np.float32),
        "slot": np.stack([np.broadcast_to(np.arange(E, dtype=np.float32), (P, E)),
                          np.broadcast_to(CAP * np.arange(E, dtype=np.float32), (P, E))]),
        "empty": (B * SEQ + np.arange(E * CAP) % CAP).astype(np.uint32)[:, None],
    }


def wait(engine, semaphore, value):
    if type(value) is int and value <= 0:
        return
    engine.wait_ge(semaphore, value)


def wait_apart(engine, semaphore, value, carrier):
    if type(value) is int and value <= 0:
        return
    engine.wait_ge(semaphore, value)
    engine.sem_inc(carrier, 1)


def transposed_weights_phase(nc, Wq, Wk, Wv, Wo, gate_w, ident_in, WxT, WoT, gwT):
    D = Wq.shape[1]
    KC = D // P
    OQ, OK = Wq.shape[0] // P, Wk.shape[0] // P
    NE = gate_w.shape[0]
    blocks = [(Wq, o) for o in range(OQ)] + [(Wk, o) for o in range(OK)] + [(Wv, o) for o in range(OK)] \
        + [(Wo, o) for o in range(OQ)]
    NB = len(blocks)
    NX = OQ + 2 * OK
    with ExitStack() as ctx:
        rows = ctx.enter_context(nc.sbuf_tensor("w_rows", [P, NB, D], F32))
        grow = ctx.enter_context(nc.sbuf_tensor("w_gate_rows", [NE, D], F32))
        ident = ctx.enter_context(nc.sbuf_tensor("w_ident", [P, P], F32))
        ps = ctx.enter_context(nc.psum_tensor("w_ps", [P, 8, 512], F32))
        loaded = ctx.enter_context(nc.semaphore("w_loaded"))
        turned = ctx.enter_context(nc.semaphore("w_turned"))
        hi_done = ctx.enter_context(nc.semaphore("w_hi_done"))
        lo_done = ctx.enter_context(nc.semaphore("w_lo_done"))
        block = ctx.enter_context(nc.Block())

        def halves(n):
            if n < NX:
                return [WxT[:, r, :, n * P:(n + 1) * P] for r in range(2)]
            return [WoT[:, r, :, (n - NX) * P:(n - NX + 1) * P] for r in range(2)]

        @block.sync
        def _(sp):
            sp.dma_start(ident[:], ident_in).then_inc(loaded, 16)
            sp.dma_start(grow[:], gate_w).then_inc(loaded, 16)
            for n, (w, o) in enumerate(blocks):
                sp.dma_start(rows[:, n], w[o * P:(o + 1) * P, :]).then_inc(loaded, 16)

        @block.tensor
        def _(pe):
            pe.wait_ge(loaded, 16 * (NB + 2))
            for n in range(NB + 1):
                if n >= 8:
                    pe.wait_ge(lo_done, n - 7)
                for k in range(KC):
                    if n < NB:
                        m = nc.tensor.transpose(ps[:, n % 8, k * P:(k + 1) * P], rows[:, n, k * P:(k + 1) * P], ident[:])
                    else:
                        m = nc.tensor.transpose(ps[:, n % 8, k * NE:(k + 1) * NE], grow[:, k * P:(k + 1) * P],
                                                ident[0:NE, 0:NE])
                m.then_inc(turned, 1)

        @block.scalar
        def _(act):
            for n in range(NB):
                act.wait_ge(turned, n + 1)
                nc.scalar.activation(halves(n)[0], ps[:, n % 8].rearrange("p (k o) -> p k o", k=KC),
                                     ACT.Copy).then_inc(hi_done, 1)

        @block.vector
        def _(dve):
            for n in range(NB):
                dve.wait_ge(hi_done, n + 1)
                hi, lo = halves(n)
                nc.vector.tensor_tensor(lo, ps[:, n % 8].rearrange("p (k o) -> p k o", k=KC),
                                        hi.bitcast(F32), ALU.subtract).then_inc(lo_done, 1)
            dve.wait_ge(turned, NB + 1)
            nc.vector.tensor_copy(gwT[:], ps[:, NB % 8, 0:KC * NE].rearrange("p (k e) -> p k e", k=KC))\
                .then_inc(lo_done, 1)


def attention_phase(nc, h_dram, txt, tabs, WxT, WoT, gwT, acc, xrow, x2T_dram, slot_table, consts):
    (cos_in, sin_in, ident_in, upper_in, tok_in, slot_in) = tabs
    B, S0, D = h_dram.shape
    SEQ = S0 + txt.shape[1]
    NT = SEQ // P
    KC = D // P
    NH, NKV, HD = 16, 4, 32
    HT = NH + NKV
    REP = NH // NKV
    E, TOPK, CAP = 64, 6, 64
    SPLIT = 3 * HD
    QR = SPLIT + 1
    NSLOT = E * CAP
    RING = 2 * REP
    EPS = 1e-5
    with ExitStack() as ctx:
        def sb(name, shape, dt=F32):
            return ctx.enter_context(nc.sbuf_tensor(name, shape, dt))

        def sem(name):
            return ctx.enter_context(nc.semaphore(name))

        ident = sb("at_ident", [P, P])
        identb = sb("at_identb", [P, P], BF16)
        ones = sb("at_ones", [P, HD])
        upper = sb("at_upper", [P, 2, P], BF16)
        cos = sb("at_cos", [P, NT, HD])
        sin = sb("at_sin", [P, NT, HD])
        mhalf = sb("at_mhalf", [P, NT])
        xn = sb("at_xn", [P, NT, D])
        hr = sb("at_hr", [P, NT, D])
        bn = sb("at_bn", [P, NT, 6])
        mv = sb("at_mv", [P, NT, 2])
        ve = sb("at_ve", [P, NT])
        rstd = sb("at_rstd", [P, NT])
        bn2 = sb("at_bn2", [P, NT, 6])
        mv2 = sb("at_mv2", [P, NT, 2])
        ve2 = sb("at_ve2", [P, NT])
        rstd2 = sb("at_rstd2", [P, NT])
        xT = sb("at_xT", [P, 2, KC, SEQ], F32R)
        oTs = sb("at_oTs", [P, 2, KC, SEQ], F32R)
        r1 = sb("at_r1", [P, 2, HT, HD])
        r2 = sb("at_r2", [P, 2, HT, HD])
        Q3 = sb("at_Q3", [P, NT, HT, QR])
        qb = sb("at_qb", [P, NT, 5, P], BF16)
        qbT = sb("at_qbT", [P, NT, 5, P], BF16)
        vn = sb("at_vn", [P, NT, NKV * HD])
        vv = sb("at_v", [P, NT, NKV * HD])
        QT = sb("at_QT", [QR, HT, SEQ], F32R)
        PT = sb("at_PT", [P, RING, NT, SEQ])
        rS = sb("at_rS", [P, SEQ])
        oT = sb("at_oT", [P, 2, SEQ])
        x2 = sb("at_x2", [P, NT, D + E])
        x2T = sb("at_x2T", [P, KC, SEQ])
        lg = sb("at_lg", [P, NT, E])
        mx = sb("at_mx", [P, NT, 8])
        mi = sb("at_mi", [P, NT, 8], U32)
        mf = sb("at_mf", [P, NT, 8])
        nm = sb("at_nm", [P, NT])
        es = sb("at_es", [P, NT, E])
        ssum = sb("at_ssum", [P, NT])
        rsum = sb("at_rsum", [P, NT])
        iota = sb("at_iota", [P, E])
        slot0 = sb("at_slot0", [P, E])
        hot = sb("at_hot", [P, NT * TOPK, E], BF16)
        mask = sb("at_mask", [P, NT, E], BF16)
        base = sb("at_base", [P, E])
        pos = sb("at_pos", [P, NT, E])
        over = sb("at_over", [P, NT, E])
        hv = sb("at_hv", [P, TOPK, E])
        sf = sb("at_sf", [P, NT * TOPK])
        si = sb("at_si", [P, NT * TOPK], U32)
        tokf = sb("at_tokf", [P, NT])
        toki = sb("at_toki", [P, NT], U32)
        upf = PT[:, 0, 0, 0:2 * P].rearrange("p (a t) -> p a t", a=2)
        ps = ctx.enter_context(nc.psum_tensor("at_ps", [P, 8, 512], F32))

        names = """consts_in consts_ok ones_ok a_in r_in var_ready rstd_ready xn_ready x_turned xhi_ready xlo_ready
            q_ready kv_ready rope_mul rope_add v_copied v_moved q_hi q_lo qb_ready qb_turned qbT_ready raw_scores
            max_ready q_turned qT_by_act qT_by_dve scores_ready probs_ready pv_done o_ready ohi_ready olo_ready
            proj_done h2_ready var2_ready rstd2_ready x2_ready x2_turned x2T_by_act x2T_by_dve logits_ready
            gmax_ready gexp_ready mask_ready pos_ready pos_read score_rows slots_ready h2_stored x2_stored
            x2T_stored scattered table_set stats_step divide_step route_step carried_dve carried_pool
            carried_sp""".split()
        (consts_in, consts_ok, ones_ok, a_in, r_in, var_ready, rstd_ready, xn_ready, x_turned, xhi_ready, xlo_ready,
         q_ready, kv_ready, rope_mul, rope_add, v_copied, v_moved, q_hi, q_lo, qb_ready, qb_turned, qbT_ready,
         raw_scores, max_ready, q_turned, qT_by_act, qT_by_dve, scores_ready, probs_ready, pv_done, o_ready,
         ohi_ready, olo_ready, proj_done, h2_ready, var2_ready, rstd2_ready, x2_ready, x2_turned, x2T_by_act,
         x2T_by_dve, logits_ready, gmax_ready, gexp_ready, mask_ready, pos_ready, pos_read, score_rows, slots_ready,
         h2_stored, x2_stored, x2T_stored, scattered, table_set, stats_step, divide_step, route_step, carried_dve,
         carried_pool, carried_sp) = [sem("at_" + n) for n in names]
        block = ctx.enter_context(nc.Block())

        SLOTS = NH + REP
        NMAX = NT * NH
        MAX_FROM = 11
        FREE = 5

        def maxima(n):
            if n < MAX_FROM:
                return range(0)
            left = SLOTS - MAX_FROM
            a, m = n - MAX_FROM, NMAX // left
            more = NMAX % left
            return range(a * m + min(a, more), (a + 1) * m + min(a + 1, more))

        def iterations(engine, body, last_full=B - 1):
            body(-1, True, False, False)
            body(0, True, True, False)
            body(1, True, True, True)
            with engine.Fori(2, last_full) as b:
                body(b, True, True, True)
            for b in range(last_full, B - 1):
                body(b, True, True, True)
            body(B - 1, False, True, True)
            body(B, False, False, True)

        @block.sync
        def _(sp):
            for dst, src in ((ident[:], ident_in), (cos[:], cos_in), (sin[:], sin_in), (upf, upper_in),
                             (tokf[:], tok_in), (iota[:], slot_in[0]), (slot0[:], slot_in[1])):
                sp.dma_start(dst, src).then_inc(consts_in, 16)

            def rows_in(dst, b, done):
                sp.dma_start(dst[:, 0:S0 // P, :], h_dram[b].rearrange("(s p) d -> p s d", p=P)).then_inc(done, 16)
                sp.dma_start(dst[:, S0 // P:NT, :], txt[b].rearrange("(s p) d -> p s d", p=P)).then_inc(done, 16)

            def body(b, nxt, main, prev):
                if prev:
                    c = b - 1
                    wait_apart(sp, h2_stored, 16 * c, carried_sp)
                    wait_apart(sp, x2_ready, NT * c, carried_sp)
                    rows_in(hr, c, r_in)
                if type(b) is not int or b < B - 2:
                    wait_apart(sp, x_turned, KC * (b + 2), carried_sp)
                    rows_in(xn, b + 2, a_in)
                if prev:
                    wait_apart(sp, h2_ready, NT * (c + 1), carried_sp)
                    sp.dma_start(acc[bass.ds(c * SEQ, SEQ), :].rearrange("(s p) d -> p s d", p=P), hr[:])\
                        .then_inc(h2_stored, 16)
                    wait_apart(sp, x2T_by_act, 2 * (c + 1), carried_sp)
                    wait_apart(sp, x2T_by_dve, 2 * (c + 1), carried_sp)
                    sp.dma_start(x2T_dram[c], x2T[:]).then_inc(x2T_stored, 16)
                    wait_apart(sp, score_rows, c + 1, carried_sp)
                    sp.dma_start(xrow[bass.ds(c * SEQ, SEQ), :].rearrange("(s p) d -> p s d", p=P), x2[:])\
                        .then_inc(x2_stored, 16)

            rows_in(xn, 0, a_in)
            iterations(sp, body, last_full=B - 2)
            for done in (h2_stored, x2_stored, x2T_stored):
                sp.wait_ge(done, 16 * B)

        @block.tensor
        def _(pe):
            T = nc.tensor
            pe.wait_ge(consts_in, 16 * 7)
            pe.wait_ge(consts_ok, 1)
            pe.wait_ge(ones_ok, 1)

            def product(out, xs, x_cols, ws, w_cols, chunks):
                n = 0
                for k in range(chunks):
                    for xa, wa in ((0, 0), (0, 1), (1, 0)):
                        m = T.matmul(out, xs[:, xa, k, x_cols], ws[:, wa, k, w_cols],
                                     start=(n == 0), stop=(n == 3 * chunks - 1))
                        n += 1
                return m

            def turned_heads(b):
                wait(pe, max_ready, NMAX * (b + 1))
                wait(pe, q_hi, 3 * NT * (b + 1))
                wait(pe, q_lo, NT * (b + 1))
                wait(pe, o_ready, NKV * b)
                wait(pe, probs_ready, NH * NT * b)
                for n in range(HT):
                    if n >= FREE:
                        e = n - FREE
                        wait(pe, qT_by_act if e % 2 == 0 else qT_by_dve, HT // 2 * b + e // 2 + 1)
                    for s in range(NT):
                        m = T.transpose(ps[0:QR, n % FREE, s * P:(s + 1) * P], Q3[:, s, n, :], ident[:])
                    m.then_inc(q_turned, 1)
                wait(pe, qT_by_act, HT // 2 * (b + 1))
                wait(pe, qT_by_dve, HT // 2 * (b + 1))
                wait(pe, v_moved, b + 1)

            def score(b, h, kt):
                if h >= 1:
                    wait(pe, probs_ready, NT * (NH * b + h - 1) + kt + 1)
                T.matmul(ps[:, kt, 0:SEQ], QT[:, NH + h // REP, kt * P:(kt + 1) * P], QT[:, h, :],
                         start=True, stop=True).then_inc(scores_ready, 1)

            def values(b, n, j):
                g = n // REP - 1
                q = 2 * (n % REP) + j
                if g < 0 or q >= 2 * NT:
                    return
                kt, sums = q % NT, q // NT
                if q == 0:
                    wait(pe, probs_ready, NT * (NH * b + REP * (g + 1)))
                    wait(pe, o_ready, NKV * b + g)
                for jj in range(REP):
                    w = ones[:, :] if sums else vv[:, kt, HD * g:HD * (g + 1)]
                    m = T.matmul(ps[HD * jj:HD * (jj + 1), 3 + sums, 0:SEQ], w, PT[:, (REP * g + jj) % RING, kt, :],
                                 start=(kt == 0), stop=(kt == NT - 1))
                if q == 2 * NT - 1:
                    m.then_inc(pv_done, 1)

            def row_maximum(a, u):
                s, r, g = u // NH, u % NH // NKV, u % NKV
                if u == 0:
                    wait(pe, qbT_ready, NT * (a + 1))
                if u >= 2:
                    wait(pe, max_ready, NMAX * a + u - 1)
                rows = slice(HD * g, HD * (g + 1))
                T.matmul(ps[:, 5 + u % 2, 0:SEQ], qbT[rows, s, r, :], qbT[rows, :, 4, :],
                         start=True, stop=True).then_inc(raw_scores, 1)

            def next_sequence(a, n):
                if n == 1:
                    wait(pe, xn_ready, NT * (a + 1))
                    wait(pe, max_ready, NMAX * a)
                    for k in range(KC):
                        if k >= 2:
                            wait(pe, xlo_ready, KC * a + k - 1)
                        for s in range(NT):
                            m = T.transpose(ps[:, 5 + k % 2, s * P:(s + 1) * P], xn[:, s, k * P:(k + 1) * P], ident[:])
                        m.then_inc(x_turned, 1)
                if n in (2, 4, 6):
                    s = n // 2 - 1
                    if s == 0:
                        wait(pe, xhi_ready, KC * (a + 1))
                        wait(pe, xlo_ready, KC * (a + 1))
                    wait(pe, rope_mul, NT * a + s)
                    product(ps[:, 5, 0:NH * HD], xT, slice(s * P, (s + 1) * P), WxT, slice(0, NH * HD), KC)\
                        .then_inc(q_ready, 1)
                if n in (3, 5, 7):
                    s = n // 2 - 1
                    wait(pe, v_copied, NT * a + s)
                    product(ps[:, 6, 0:2 * NKV * HD], xT, slice(s * P, (s + 1) * P), WxT,
                            slice(NH * HD, (NH + 2 * NKV) * HD), KC).then_inc(kv_ready, 1)
                for s in {9: (0, 1), 10: (2,)}.get(n, ()):
                    wait(pe, qb_ready, NT * a + s + 1)
                    wait(pe, rope_mul, NT * (a + 1))
                    wait(pe, v_copied, NT * (a + 1))
                    if s == 2:
                        wait(pe, qbT_ready, NT * a + 1)
                    for r in range(5):
                        m = T.transpose(ps[:, 5 + s % 2].bitcast(BF16)[:, r * P:(r + 1) * P], qb[:, s, r, :], identb[:])
                    m.then_inc(qb_turned, 1)

            def sequence_before(c, n):
                if n in (0, 3, 5):
                    s = (0, 3, 5).index(n)
                    if s == 0:
                        wait(pe, ohi_ready, NKV * (c + 1))
                        wait(pe, olo_ready, NKV * (c + 1))
                        wait(pe, pos_read, c)
                    wait(pe, h2_ready, NT * c + s)
                    product(ps[:, 7, :], oTs, slice(s * P, (s + 1) * P), WoT, slice(0, D), KC).then_inc(proj_done, 1)
                if n in (8, 9, 10, 11):
                    k = n - 8
                    if k == 0:
                        wait(pe, x2_ready, NT * (c + 1))
                    else:
                        wait(pe, x2T_by_dve if k % 2 == 0 else x2T_by_act, 2 * c + (k - 1) // 2 + 1)
                    for s in range(NT):
                        m = T.transpose(ps[:, 7, s * P:(s + 1) * P], x2[:, s, k * P:(k + 1) * P], ident[:])
                    m.then_inc(x2_turned, 1)
                if n == 12:
                    wait(pe, x2T_by_act, 2 * (c + 1))
                    wait(pe, x2T_by_dve, 2 * (c + 1))
                    for s in range(NT):
                        for k in range(KC):
                            m = T.matmul(ps[:, 7, s * E:(s + 1) * E], x2T[:, k, s * P:(s + 1) * P], gwT[:, k, :],
                                         start=(k == 0), stop=(k == KC - 1))
                    m.then_inc(logits_ready, 1)
                if n == 15:
                    wait(pe, mask_ready, c + 1)
                    for s in range(NT + 1):
                        for q in range(min(s, NT - 1) + 1):
                            m = T.matmul(ps[:, 7, 256 + s * E:256 + (s + 1) * E], upper[:, 0 if q == s else 1, :],
                                         mask[:, q, :], start=(q == 0), stop=(q == min(s, NT - 1)))
                    m.then_inc(pos_ready, 1)

            def body(b, nxt, main, prev):
                if main:
                    turned_heads(b)
                for n in range(SLOTS):
                    units = maxima(n) if nxt else ()
                    for j in range(6):
                        if main and j < NT and n < NH:
                            score(b, n, j)
                        if main and j in (3, 4):
                            values(b, n, j - 3)
                        if j < len(units):
                            row_maximum(b + 1, units[j])
                    if nxt:
                        next_sequence(b + 1, n)
                    if prev:
                        sequence_before(b - 1, n)

            iterations(pe, body)

        @block.scalar
        def _(act):
            A = nc.scalar
            act.wait_ge(consts_in, 16 * 7)
            A.activation(identb[:], ident[:], ACT.Copy)
            A.activation(upper[:], upf, ACT.Copy).then_inc(consts_ok, 1)

            def next_sequence(a, n):
                if n == 1:
                    for k in range(KC):
                        wait(act, x_turned, KC * a + k + 1)
                        wait(act, kv_ready, NT * a)
                        A.activation(xT[:, 0, k, :], ps[:, 5 + k % 2, 0:SEQ], ACT.Copy).then_inc(xhi_ready, 1)
                if n in (4, 6, 8):
                    s = n // 2 - 2
                    wait(act, rope_mul, NT * a + s + 1)
                    wait(act, v_moved, a)
                    A.activation(vn[:, s, :], ps[:, 6, P:2 * P], ACT.Copy).then_inc(v_copied, 1)
                if n in (5, 7, 9):
                    s = (n - 5) // 2
                    wait(act, rope_add, NT * a + s + 1)
                    qk = r1[:, s % 2]
                    A.activation(Q3[:, s, :, 0:HD].bitcast(F32R), qk, ACT.Copy).then_inc(q_hi, 1)
                    A.activation(qb[:, s, 0:4, :].rearrange("p r (g d) -> p g r d", g=NKV),
                                 qk[:, 0:NH, :].rearrange("p (g r) d -> p g r d", g=NKV), ACT.Copy)
                    A.activation(qb[:, s, 4, :].rearrange("p (g d) -> p g d", g=NKV), qk[:, NH:HT, :], ACT.Copy)\
                        .then_inc(qb_ready, 1)
                    wait(act, q_hi, 3 * (NT * a + s) + 1)
                    A.activation(Q3[:, s, 0:NH, 2 * HD:3 * HD], Q3[:, s, 0:NH, 0:HD], ACT.Copy).then_inc(q_hi, 1)
                    A.activation(Q3[:, s, NH:HT, HD:2 * HD], Q3[:, s, NH:HT, 0:HD], ACT.Copy).then_inc(q_hi, 1)
                for s in {9: (0, 1), 10: (2,)}.get(n, ()):
                    wait(act, qb_turned, NT * a + s + 1)
                    A.activation(qbT[:, s], ps[:, 5 + s % 2].bitcast(BF16)[:, 0:5 * P]
                                 .rearrange("p (r t) -> p r t", r=5), ACT.Copy).then_inc(qbT_ready, 1)

            def out_hi(b, g):
                wait(act, o_ready, NKV * b + g + 1)
                wait(act, proj_done, NT * b)
                A.activation(oTs[:, 0, g, :], oT[:, g % 2, :], ACT.Copy).then_inc(ohi_ready, 1)

            def sequence_before(c, n):
                if n in (8, 10):
                    k = n - 8
                    wait(act, x2_turned, KC * c + k + 1)
                    wait(act, x2T_stored, 16 * c)
                    A.activation(x2T[:, k, :], ps[:, 7, 0:SEQ], ACT.Copy).then_inc(x2T_by_act, 1)
                if n == 14:
                    wait(act, gmax_ready, c + 1)
                    for s in range(NT):
                        A.activation(es[:, s, :], lg[:, s, :], ACT.Exp, bias=nm[:, s:s + 1],
                                     accum_out=ssum[:, s:s + 1]).then_inc(gexp_ready, 1)

            def body(b, nxt, main, prev):
                if main:
                    for n in range(0, HT, 2):
                        wait(act, q_turned, HT * b + n + 1)
                        A.activation(QT[:, n, :], ps[0:QR, n % FREE, 0:SEQ], ACT.Copy).then_inc(qT_by_act, 1)
                for n in range(SLOTS):
                    if main and n < NH:
                        if n >= RING:
                            wait(act, pv_done, NKV * b + (n - RING) // REP + 1)
                        for kt in range(NT):
                            wait(act, scores_ready, NT * (NH * b + n) + kt + 1)
                            A.activation(PT[:, n % RING, kt, :], ps[:, kt, 0:SEQ], ACT.Exp, scale=float(HD) ** -0.5)\
                                .then_inc(probs_ready, 1)
                    if nxt:
                        next_sequence(b + 1, n)
                    if prev:
                        sequence_before(b - 1, n)
                    if main and n % REP == REP - 1 and n >= REP:
                        out_hi(b, n // REP - 1)

            iterations(act, body)

        @block.vector
        def _(dve):
            V = nc.vector
            V.memset(mhalf[:], -0.5)
            V.memset(base[:], 0.0)
            V.memset(ones[:], 1.0)
            V.memset(Q3[:, :, NH:HT, SPLIT:QR], 1.0).then_inc(ones_ok, 1)
            dve.wait_ge(consts_in, 16 * 7)
            dve.wait_ge(ones_ok, 1)
            done = {}

            def link(ins, chain, total, seq, apart=False):
                done[chain] = done.get(chain, 0) + 1
                semaphore = {"stats": stats_step, "divide": divide_step, "route": route_step}[chain]
                ins.then_inc(semaphore, 1)
                (wait_apart if apart else wait)(dve, semaphore, seq * total + done[chain],
                                                *((carried_dve,) if apart else ()))

            NSTAT, NDIV, NROUTE = 2, NKV, ROUTE_STEPS

            def row_maxima(a, n):
                for u in maxima(n):
                    s, r, g = u // NH, u % NH // NKV, u % NKV
                    wait(dve, raw_scores, NMAX * a + u + 1)
                    h = REP * g + r
                    V.tensor_reduce(Q3[:, s, h, SPLIT:QR], ps[:, 5 + u % 2, 0:SEQ], AX.X, ALU.max, negate=True)\
                        .then_inc(max_ready, 1)

            def statistics(a):
                wait(dve, a_in, 32 * (a + 1))
                for s in range(NT):
                    ins = V.bn_stats(bn[:, s, :], xn[:, s, :])
                link(ins, "stats", NSTAT, a, apart=True)
                for s in range(NT):
                    ins = V.bn_aggr(mv[:, s, :], bn[:, s, :])
                link(ins, "stats", NSTAT, a)
                V.tensor_scalar(ve[:], mv[:, :, 1], EPS, None, ALU.add).then_inc(var_ready, 1)

            def normalise(a):
                wait(dve, rstd_ready, a + 1)
                for s in range(NT):
                    V.tensor_scalar(xn[:, s, :], xn[:, s, :], mv[:, s, 0:1], rstd[:, s:s + 1],
                                    ALU.subtract, ALU.mult).then_inc(xn_ready, 1)

            def next_sequence(a, n):
                if n == 1:
                    for k in range(KC):
                        wait(dve, xhi_ready, KC * a + k + 1)
                        V.tensor_tensor(xT[:, 1, k, :], ps[:, 5 + k % 2, 0:SEQ], xT[:, 0, k, :].bitcast(F32),
                                        ALU.subtract).then_inc(xlo_ready, 1)
                if n in (3, 5, 7):
                    s = (n - 3) // 2
                    half = HD // 2
                    wait(dve, q_ready, NT * a + s + 1)
                    wait(dve, kv_ready, NT * a + s + 1)
                    wait(dve, qb_ready, NT * a + s - 1)
                    wait(dve, q_lo, NT * a + s - 1)
                    qk = ps[:, 5:7, :].rearrange("p u c -> p (u c)")[:, 0:HT * HD].rearrange("p (h d) -> p h d", d=HD)
                    V.tensor_tensor(r1[:, s % 2], qk, cos[:, s:s + 1, :].to_broadcast([P, HT, HD]), ALU.mult)
                    V.tensor_tensor(r2[:, s % 2, :, 0:half], qk[:, :, half:HD],
                                    sin[:, s:s + 1, 0:half].to_broadcast([P, HT, half]), ALU.mult)
                    V.tensor_tensor(r2[:, s % 2, :, half:HD], qk[:, :, 0:half],
                                    sin[:, s:s + 1, half:HD].to_broadcast([P, HT, half]), ALU.mult)\
                        .then_inc(rope_mul, 1)

            def divide(b, g):
                wait(dve, pv_done, NKV * b + g + 1)
                link(V.reciprocal(rS[:], ps[:, 4, 0:SEQ]), "divide", NDIV, b)
                wait(dve, olo_ready, NKV * b + g - 1)
                V.tensor_tensor(oT[:, g % 2, :], ps[:, 3, 0:SEQ], rS[:], ALU.mult).then_inc(o_ready, 1)

            def sequence_before(c, n):
                def chain(ins, apart=False):
                    link(ins, "route", NROUTE, c, apart)

                wide = lambda t: t[:, :].rearrange("p (a e) -> p a e", a=1).to_broadcast([P, NT, E])
                if n in (0, 3, 5):
                    s = (0, 3, 5).index(n)
                    if s == 0:
                        wait(dve, r_in, 32 * (c + 1))
                    wait(dve, proj_done, NT * c + s + 1)
                    V.tensor_tensor(hr[:, s, :], hr[:, s, :], ps[:, 7, :], ALU.add).then_inc(h2_ready, 1)
                if n == 6:
                    wait(dve, h2_ready, NT * (c + 1))
                    for s in range(NT):
                        ins = V.bn_stats(bn2[:, s, :], hr[:, s, :])
                    chain(ins, apart=True)
                    for s in range(NT):
                        ins = V.bn_aggr(mv2[:, s, :], bn2[:, s, :])
                    chain(ins)
                    V.tensor_scalar(ve2[:], mv2[:, :, 1], EPS, None, ALU.add).then_inc(var2_ready, 1)
                if n == 7:
                    wait(dve, rstd2_ready, c + 1)
                    wait(dve, x2_stored, 16 * c)
                    for s in range(NT):
                        V.tensor_scalar(x2[:, s, 0:D], hr[:, s, :], mv2[:, s, 0:1], rstd2[:, s:s + 1],
                                        ALU.subtract, ALU.mult).then_inc(x2_ready, 1)
                if n in (9, 11):
                    k = n - 8
                    wait(dve, x2_turned, KC * c + k + 1)
                    wait(dve, x2T_stored, 16 * c)
                    V.tensor_copy(x2T[:, k, :], ps[:, 7, 0:SEQ]).then_inc(x2T_by_dve, 1)
                if n == 13:
                    wait(dve, logits_ready, c + 1)
                    chain(V.tensor_copy(lg[:], ps[:, 7, 0:NT * E].rearrange("p (s e) -> p s e", s=NT)), apart=True)
                    for s in range(NT):
                        ins = V.max(mx[:, s, :], lg[:, s, :])
                    chain(ins)
                    V.tensor_scalar(nm[:], mx[:, :, 0], -1.0, None, ALU.mult).then_inc(gmax_ready, 1)
                    for s in range(NT):
                        ins = V.max_index(mi[:, s, :], mx[:, s, :], lg[:, s, :])
                    chain(ins)
                    chain(V.tensor_copy(mf[:], mi[:]))
                    for s in range(NT):
                        ins = V.tensor_tensor(
                            hot[:, s * TOPK:(s + 1) * TOPK, :],
                            iota[:, :].rearrange("p (a e) -> p a e", a=1).to_broadcast([P, TOPK, E]),
                            mf[:, s, 0:TOPK].rearrange("p (k a) -> p k a", a=1).to_broadcast([P, TOPK, E]), ALU.is_equal)
                    chain(ins)
                    chain(V.tensor_reduce(pos[:], hot[:].rearrange("p (s k) e -> p s e k", s=NT), AX.X, ALU.add))
                    V.tensor_copy(mask[:], pos[:]).then_inc(mask_ready, 1)
                if n == 15:
                    wait(dve, gexp_ready, NT * (c + 1))
                    chain(V.reciprocal(rsum[:], ssum[:]))
                    for s in range(NT):
                        ins = V.tensor_scalar(x2[:, s, D:D + E], es[:, s, :], rsum[:, s:s + 1], None, ALU.mult)
                    ins.then_inc(score_rows, 1)
                if n == 16:
                    wait(dve, pos_ready, c + 1)
                    pp = ps[:, 7, 256:256 + NT * E].rearrange("p (s e) -> p s e", s=NT)
                    chain(V.tensor_tensor(pos[:], pp, wide(base), ALU.add))
                    chain(V.tensor_tensor(base[:], base[:], ps[:, 7, 256 + NT * E:256 + (NT + 1) * E], ALU.add))
                    dve.sem_inc(pos_read, 1)
                    chain(V.tensor_scalar(over[:], pos[:], float(CAP), 65536.0, ALU.is_ge, ALU.mult))
                    chain(V.tensor_tensor(pos[:], pos[:], over[:], ALU.add))
                    chain(V.tensor_tensor(pos[:], pos[:], wide(slot0), ALU.add))
                    for s in range(NT):
                        ks = slice(s * TOPK, (s + 1) * TOPK)
                        chain(V.tensor_tensor(hv[:], hot[:, ks, :], pos[:, s:s + 1, :].to_broadcast([P, TOPK, E]),
                                              ALU.mult))
                        chain(V.tensor_reduce(sf[:, ks], hv[:], AX.X, ALU.add))
                    wait(dve, scattered, 16 * NT * TOPK * c)
                    V.tensor_copy(si[:], sf[:])
                    chain(V.tensor_copy(toki[:], tokf[:]))
                    chain(V.tensor_scalar(tokf[:], tokf[:], float(SEQ), None, ALU.add))
                    dve.sem_inc(slots_ready, 1)

            def body(b, nxt, main, prev):
                done.clear()
                if nxt:
                    statistics(b + 1)
                if main:
                    for n in range(1, HT, 2):
                        wait(dve, q_turned, HT * b + n + 1)
                        V.tensor_copy(QT[:, n, :], ps[0:QR, n % FREE, 0:SEQ]).then_inc(qT_by_dve, 1)
                if nxt:
                    normalise(b + 1)
                for n in range(SLOTS):
                    if nxt:
                        row_maxima(b + 1, n)
                        next_sequence(b + 1, n)
                    if prev:
                        sequence_before(b - 1, n)
                    if main and n % REP == REP - 2 and n >= REP:
                        divide(b, n // REP - 1)
                for chain, total, used in (("stats", NSTAT, nxt), ("divide", NDIV, main), ("route", NROUTE, prev)):
                    assert done.get(chain, 0) == (total if used else 0), (chain, done)

            iterations(dve, body)

        @block.gpsimd
        def _(pool):
            G = nc.gpsimd
            G.dma_start(slot_table, consts).then_inc(table_set, 16)
            pool.wait_ge(table_set, 16)
            pool.wait_ge(ones_ok, 1)

            def next_sequence(a, n):
                if n in (3, 5, 7):
                    s = (n - 3) // 2
                    wait(pool, rope_mul, NT * a + s + 1)
                    G.tensor_tensor(r1[:, s % 2], r1[:, s % 2], r2[:, s % 2], ALU.add).then_inc(rope_add, 1)
                if n in (5, 7, 9):
                    s = (n - 5) // 2
                    wait(pool, q_hi, 3 * (NT * a + s) + 1)
                    wait(pool, rope_add, NT * a + s + 1)
                    G.tensor_tensor(Q3[:, s, 0:NH, HD:2 * HD].bitcast(F32R), r1[:, s % 2, 0:NH],
                                    Q3[:, s, 0:NH, 0:HD], ALU.subtract)
                    G.tensor_tensor(Q3[:, s, NH:HT, 2 * HD:3 * HD].bitcast(F32R), r1[:, s % 2, NH:HT],
                                    Q3[:, s, NH:HT, 0:HD], ALU.subtract).then_inc(q_lo, 1)

            def sequence_before(c, n):
                if n == 6:
                    wait(pool, var2_ready, c + 1)
                    G.tensor_tensor(rstd2[:], ve2[:], mhalf[:], ALU.pow).then_inc(rstd2_ready, 1)
                if n == 17:
                    wait_apart(pool, slots_ready, c + 1, carried_pool)
                    for s in range(NT):
                        for k in range(TOPK):
                            m = s * TOPK + k
                            G.indirect_dma_start(slot_table, bass.IndirectOffsetOnAxis(ap=si[:, m:m + 1], axis=0),
                                                 toki[:, s:s + 1], None, bounds_check=NSLOT - 1, oob_is_err=False,
                                                 compute_op=ALU.bypass).then_inc(scattered, 16)

            def body(b, nxt, main, prev):
                if nxt:
                    wait(pool, var_ready, b + 2)
                    G.tensor_tensor(rstd[:], ve[:], mhalf[:], ALU.pow).then_inc(rstd_ready, 1)
                if main:
                    wait_apart(pool, v_copied, NT * (b + 1), carried_pool)
                    wait_apart(pool, pv_done, NKV * b, carried_pool)
                    G.tensor_copy(vv[:], vn[:]).then_inc(v_moved, 1)
                for n in range(SLOTS):
                    if nxt:
                        next_sequence(b + 1, n)
                    if prev:
                        sequence_before(b - 1, n)
                    if main and n % REP == REP - 1 and n >= REP:
                        g = n // REP - 1
                        wait(pool, ohi_ready, NKV * b + g + 1)
                        G.tensor_tensor(oTs[:, 1, g, :], oT[:, g % 2, :], oTs[:, 0, g, :].bitcast(F32),
                                        ALU.subtract).then_inc(olo_ready, 1)

            iterations(pool, body)
            pool.wait_ge(scattered, 16 * NT * TOPK * B)


def experts_phase(nc, acc, xrow, x2T_dram, slot_table, w_gate, w_up, w_down, sw_gate, sw_up, sw_down, ident_in):
    E, D, I = w_gate.shape
    IS = sw_gate.shape[1]
    NSEQ, _, KC, SEQ = x2T_dram.shape
    CAP = slot_table.shape[0] // E
    T = NSEQ * SEQ
    NT = SEQ // P
    PAIRS = E // 2
    Q = PAIRS // NSEQ
    IC = (I + P - 1) // P
    IW = [min(P, I - c * P) for c in range(IC)]
    SC = (IS + P - 1) // P
    SW = [IS // SC + (1 if c < IS % SC else 0) for c in range(SC)]
    SO = [sum(SW[:c]) for c in range(SC)]
    SM = max(SW)
    assert Q == 4 and SC == 2 * (Q - 1) and NT == 3
    with ExitStack() as ctx:
        def sb(name, shape, dt=F32):
            return ctx.enter_context(nc.sbuf_tensor(name, shape, dt))

        def sem(name):
            return ctx.enter_context(nc.semaphore(name))

        ident = sb("mo_ident", [P, P])
        zeros = sb("mo_zeros", [CAP, D + E])
        gather_all = sb("mo_gather_all", [P, PAIRS], U32)
        scatter_all = sb("mo_scatter_all", [CAP, E], U32)
        gather_ix = sb("mo_gather_ix", [P, Q], U32)
        scatter_ix = sb("mo_scatter_ix", [CAP, Q, 2], U32)
        wgu = sb("mo_wgu", [P, 2, 2, 2, KC, I])
        wd = sb("mo_wd", [P, 2, 2, IC, D])
        sgu = sb("mo_sgu", [P, 2, 2, KC, IS], F32R)
        sd = sb("mo_sd", [SM, 2, SC, D], F32R)
        x2 = sb("mo_x2", [P, KC, SEQ])
        x2s = sb("mo_x2s", [P, 2, KC, SEQ], F32R)
        hs = sb("mo_hs", [SM, 2, SC, SEQ], F32R)
        ssil = sb("mo_ssil", [SM, SEQ])
        sh = sb("mo_sh", [SM, 2, SEQ])
        so = sb("mo_so", [P, NT, D])
        xg = sb("mo_xg", [P, 2, D + E])
        xgT = sb("mo_xgT", [P, KC, P])
        wcol = sb("mo_wcol", [P, 2])
        sil = sb("mo_sil", [P, I])
        hm = sb("mo_hm", [P, I])
        hmT = sb("mo_hmT", [P, IC, P])
        y = sb("mo_y", [CAP, 2, 2, D])
        ps = ctx.enter_context(nc.psum_tensor("mo_ps", [P, 8, 512], F32))

        consts_in = sem("mo_consts_in")
        zeros_set = sem("mo_zeros_set")
        pads_in = sem("mo_pads_in")
        table_in = sem("mo_table_in")
        staged = [sem(f"mo_staged{j}") for j in range(2)]
        shi_done = sem("mo_shi_done")
        slo_done = sem("mo_slo_done")
        w_in = [sem(f"mo_w_in{j}") for j in range(2)]
        x2_in = sem("mo_x2_in")
        x2hi_ready = sem("mo_x2hi_ready")
        x2lo_ready = sem("mo_x2lo_ready")
        gix_ready = sem("mo_gix_ready")
        six_ready = sem("mo_six_ready")
        rows_in = [sem(f"mo_rows_in{j}") for j in range(2)]
        rows_turned = sem("mo_rows_turned")
        rowsT_ready = sem("mo_rowsT_ready")
        wcol_ready = sem("mo_wcol_ready")
        gate_up_done = sem("mo_gate_up_done")
        silu_done = sem("mo_silu_done")
        hidden_ready = sem("mo_hidden_ready")
        hidden_turned = sem("mo_hidden_turned")
        hiddenT_ready = sem("mo_hiddenT_ready")
        down_done = sem("mo_down_done")
        ya_ready = sem("mo_ya_ready")
        yb_ready = sem("mo_yb_ready")
        s_gate_done = sem("mo_s_gate_done")
        s_up_done = sem("mo_s_up_done")
        s_silu_done = sem("mo_s_silu_done")
        s_mult_done = sem("mo_s_mult_done")
        s_hi_done = sem("mo_s_hi_done")
        s_lo_done = sem("mo_s_lo_done")
        s_down_done = sem("mo_s_down_done")
        so_ready = sem("mo_so_ready")
        added = sem("mo_added")
        carried = sem("mo_carried")
        block = ctx.enter_context(nc.Block())

        stage = [wgu[:, j].rearrange("p e g k i -> p (e g k i)")[:, 0:KC * IS] for j in range(2)]
        staged_d = wd[:].rearrange("p b e c d -> p (b e c d)")[0:SM, 0:SC * D]

        def adds_before(i, q):
            return (2 * Q + 1) * i - 2 * (Q - 2) - 1 + 2 * q + (1 if q >= 2 else 0)

        def steps(engine, body):
            body(0)
            with engine.Fori(1, NSEQ) as i:
                body(i)

        @block.sync
        def _(sp):
            sp.dma_start(ident[:], ident_in).then_inc(consts_in, 16)
            for j, w in enumerate((sw_gate, sw_up)):
                sp.dma_start(stage[j].rearrange("p (k i) -> p k i", k=KC), w.rearrange("(k p) i -> p k i", p=P))\
                    .then_inc(staged[0], 16)
            for c in range(SC):
                sp.dma_start(staged_d[0:SW[c], c * D:(c + 1) * D], sw_down[SO[c]:SO[c] + SW[c], :])\
                    .then_inc(staged[1], 16)
            sp.wait_ge(zeros_set, 1)
            sp.dma_start(xrow[T:T + CAP, :], zeros[:]).then_inc(pads_in, 16)
            sp.dma_start(acc[T:T + CAP, :], zeros[:, 0:D]).then_inc(pads_in, 16)
            with nc.allow_non_contiguous_dma(reason="one word for each slot"):
                sp.dma_start(gather_all[:], slot_table.rearrange("(q c) a -> c (q a)", c=P)).then_inc(table_in, 16)
                sp.dma_start(scatter_all[:], slot_table.rearrange("(e c) a -> c (e a)", c=CAP)).then_inc(table_in, 16)

            def body(i):
                for q in range(Q):
                    p = Q * i + q
                    j = q % 2
                    if q == 0:
                        wait(sp, x2hi_ready, i)
                        wait(sp, x2lo_ready, i)
                        sp.dma_start(x2[:], x2T_dram[i]).then_inc(x2_in, 16)
                    if type(p) is int and p < 2:
                        sp.wait_ge(slo_done, 3)
                    wait(sp, gate_up_done, p - 1)
                    for e in range(2):
                        for g, w in enumerate((w_gate, w_up)):
                            sp.dma_start(wgu[:, j, e, g], w[2 * p + e].rearrange("(p k) i -> p k i", k=KC))\
                                .then_inc(w_in[j], 16)
                    wait(sp, down_done, p - 1)
                    for e in range(2):
                        sp.dma_start(wd[:, j, e, 0:IC - 1, :],
                                     w_down[2 * p + e][0:(IC - 1) * P, :].rearrange("(c p) d -> p c d", p=P))\
                            .then_inc(w_in[j], 16)
                        sp.dma_start(wd[0:IW[-1], j, e, IC - 1, :], w_down[2 * p + e][(IC - 1) * P:I, :])\
                            .then_inc(w_in[j], 16)

            steps(sp, body)
            sp.wait_ge(pads_in, 32)

        @block.tensor
        def _(pe):
            M = nc.tensor
            pe.wait_ge(consts_in, 16)
            pe.wait_ge(slo_done, 3)

            def shared_in(i, c, g):
                n = SC * i + c
                if c == 0 and g == 0:
                    pe.wait_ge(x2hi_ready, i + 1)
                    pe.wait_ge(x2lo_ready, i + 1)
                wait(pe, s_mult_done, n)
                k3 = 0
                for k in range(KC):
                    for xa, wa in ((0, 0), (0, 1), (1, 0)):
                        m = M.matmul(ps[0:SW[c], 5 + g, 0:SEQ], sgu[:, wa, g, k, SO[c]:SO[c] + SW[c]],
                                     x2s[:, xa, k, :], start=(k3 == 0), stop=(k3 == 3 * KC - 1))
                        k3 += 1
                m.then_inc((s_gate_done, s_up_done)[g], 1)

            def shared_out(i, s):
                wait(pe, so_ready, NT * i + s)
                if s == 0:
                    pe.wait_ge(s_hi_done, SC * (i + 1))
                    pe.wait_ge(s_lo_done, SC * (i + 1))
                k3 = 0
                for c in range(SC):
                    for xa, wa in ((0, 0), (0, 1), (1, 0)):
                        m = M.matmul(ps[:, 7, :], hs[0:SW[c], xa, c, s * P:(s + 1) * P], sd[0:SW[c], wa, c, :],
                                     start=(k3 == 0), stop=(k3 == 3 * SC - 1))
                        k3 += 1
                m.then_inc(s_down_done, 1)

            def body(i):
                for q in range(Q):
                    p = Q * i + q
                    j = q % 2
                    use = 2 * i + q // 2 + 1
                    pe.wait_ge(rows_in[j], 16 * use)
                    wait(pe, rowsT_ready, p)
                    for k in range(KC):
                        m = M.transpose(ps[:, 0, k * P:(k + 1) * P], xg[:, j, k:D:KC], ident[:])
                    m.then_inc(rows_turned, 1)
                    if q < Q - 1:
                        shared_in(i, 2 * q, 0)
                        shared_in(i, 2 * q, 1)
                    else:
                        shared_out(i, 0)
                    pe.wait_ge(rowsT_ready, p + 1)
                    pe.wait_ge(w_in[j], 16 * 8 * use)
                    wait(pe, hidden_ready, p)
                    for g in range(2):
                        for k in range(KC):
                            for e in range(2):
                                m = M.matmul(ps[CAP * e:CAP * (e + 1), 1 + g, 0:I], xgT[:, k, CAP * e:CAP * (e + 1)],
                                             wgu[:, j, e, g, k, :], start=(k == 0), stop=(k == KC - 1))
                    m.then_inc(gate_up_done, 1)
                    if q < Q - 1:
                        shared_in(i, 2 * q + 1, 0)
                    else:
                        shared_out(i, 1)
                    pe.wait_ge(hidden_ready, p + 1)
                    wait(pe, hiddenT_ready, p)
                    for c in range(IC):
                        m = M.transpose(ps[0:IW[c], 3, c * P:(c + 1) * P], hm[:, c * P:c * P + IW[c]], ident[:])
                    m.then_inc(hidden_turned, 1)
                    if q < Q - 1:
                        shared_in(i, 2 * q + 1, 1)
                    else:
                        shared_out(i, 2)
                    pe.wait_ge(hiddenT_ready, p + 1)
                    wait(pe, ya_ready, p)
                    wait(pe, yb_ready, p)
                    for c in range(IC):
                        for e in range(2):
                            m = M.matmul(ps[CAP * e:CAP * (e + 1), 4, :], hmT[0:IW[c], c, CAP * e:CAP * (e + 1)],
                                         wd[0:IW[c], j, e, c, :], start=(c == 0), stop=(c == IC - 1))
                    m.then_inc(down_done, 1)

            steps(pe, body)

        @block.scalar
        def _(act):
            A = nc.scalar
            act.wait_ge(staged[0], 32)
            for g in range(2):
                A.activation(sgu[:, 0, g].rearrange("p k i -> p (k i)"), stage[g], ACT.Copy).then_inc(shi_done, 1)
            act.wait_ge(staged[1], 16 * SC)
            for c in range(SC):
                m = A.activation(sd[0:SW[c], 0, c], staged_d[0:SW[c], c * D:(c + 1) * D], ACT.Copy)
            m.then_inc(shi_done, 1)

            def split_x2(i):
                act.wait_ge(x2_in, 16 * (i + 1))
                wait(act, s_up_done, SC * i)
                A.activation(x2s[:, 0], x2[:], ACT.Copy).then_inc(x2hi_ready, 1)

            def silu_shared(i, c):
                n = SC * i + c
                act.wait_ge(s_gate_done, n + 1)
                wait(act, s_mult_done, n)
                A.activation(ssil[0:SW[c], :], ps[0:SW[c], 5, 0:SEQ], ACT.Silu).then_inc(s_silu_done, 1)

            def hi_shared(i, c):
                n = SC * i + c
                act.wait_ge(s_mult_done, n + 1)
                if c == 0:
                    wait(act, s_down_done, NT * i)
                A.activation(hs[0:SW[c], 0, c, :], sh[0:SW[c], c % 2, :], ACT.Copy).then_inc(s_hi_done, 1)

            def body(i):
                for q in range(Q):
                    p = Q * i + q
                    if q == 0:
                        split_x2(i)
                    if q < Q - 1:
                        silu_shared(i, 2 * q)
                    act.wait_ge(gate_up_done, p + 1)
                    wait(act, hidden_ready, p)
                    A.activation(sil[:], ps[:, 1, 0:I], ACT.Silu).then_inc(silu_done, 1)
                    if q < Q - 1:
                        hi_shared(i, 2 * q)
                        silu_shared(i, 2 * q + 1)
                        hi_shared(i, 2 * q + 1)
                    act.wait_ge(down_done, p + 1)
                    wait(act, added, 16 * (adds_before(i, q) + 1))
                    A.activation(y[:, q % 2, 0, :], ps[0:CAP, 4, :], ACT.Copy).then_inc(ya_ready, 1)

            steps(act, body)

        @block.vector
        def _(dve):
            V = nc.vector
            V.memset(zeros[:], 0.0).then_inc(zeros_set, 1)
            for g in range(2):
                dve.wait_ge(shi_done, g + 1)
                V.tensor_tensor(sgu[:, 1, g].rearrange("p k i -> p (k i)"), stage[g],
                                sgu[:, 0, g].bitcast(F32).rearrange("p k i -> p (k i)"), ALU.subtract)\
                    .then_inc(slo_done, 1)
            dve.wait_ge(shi_done, 3)
            for c in range(SC):
                m = V.tensor_tensor(sd[0:SW[c], 1, c], staged_d[0:SW[c], c * D:(c + 1) * D],
                                    sd[0:SW[c], 0, c].bitcast(F32), ALU.subtract)
            m.then_inc(slo_done, 1)

            def mult_shared(i, c):
                n = SC * i + c
                dve.wait_ge(s_silu_done, n + 1)
                dve.wait_ge(s_up_done, n + 1)
                wait(dve, s_hi_done, n - 1)
                V.tensor_tensor(sh[0:SW[c], c % 2, :], ssil[0:SW[c], :], ps[0:SW[c], 6, 0:SEQ], ALU.mult)\
                    .then_inc(s_mult_done, 1)

            def lo_shared(i, c):
                n = SC * i + c
                dve.wait_ge(s_hi_done, n + 1)
                V.tensor_tensor(hs[0:SW[c], 1, c, :], sh[0:SW[c], c % 2, :], hs[0:SW[c], 0, c, :].bitcast(F32),
                                ALU.subtract).then_inc(s_lo_done, 1)

            def out_shared(i, s):
                dve.wait_ge(s_down_done, NT * i + s + 1)
                wait(dve, added, 16 * adds_before(i, 2) if type(i) is not int or i > 0 else 0)
                V.tensor_copy(so[:, s, :], ps[:, 7, :]).then_inc(so_ready, 1)

            def body(i):
                for q in range(Q):
                    p = Q * i + q
                    j = q % 2
                    if q == 0:
                        dve.wait_ge(x2hi_ready, i + 1)
                        V.tensor_tensor(x2s[:, 1], x2[:], x2s[:, 0].bitcast(F32), ALU.subtract)\
                            .then_inc(x2lo_ready, 1)
                    dve.wait_ge(rows_turned, p + 1)
                    wait(dve, gate_up_done, p)
                    V.tensor_copy(xgT[:].rearrange("p k t -> p (k t)"), ps[:, 0, :]).then_inc(rowsT_ready, 1)
                    V.tensor_copy(wcol[0:CAP, j:j + 1], xg[0:CAP, j, bass.ds(D + 2 * p, 1)])
                    V.tensor_copy(wcol[CAP:P, j:j + 1], xg[CAP:P, j, bass.ds(D + 2 * p + 1, 1)])\
                        .then_inc(wcol_ready, 1)
                    if q < Q - 1:
                        mult_shared(i, 2 * q)
                    else:
                        out_shared(i, 0)
                    dve.wait_ge(silu_done, p + 1)
                    dve.wait_ge(wcol_ready, p + 1)
                    wait(dve, hidden_turned, p)
                    V.scalar_tensor_tensor(out=hm[:], in0=sil[:], scalar=wcol[:, j:j + 1], in1=ps[:, 2, 0:I],
                                           op0=ALU.mult, op1=ALU.mult).then_inc(hidden_ready, 1)
                    if q == Q - 1:
                        out_shared(i, 1)
                    dve.wait_ge(hidden_turned, p + 1)
                    wait(dve, down_done, p)
                    V.tensor_copy(hmT[:, 0:IC - 1, :], ps[:, 3, 0:(IC - 1) * P].rearrange("p (c t) -> p c t", t=P))
                    V.tensor_copy(hmT[0:IW[-1], IC - 1, :], ps[0:IW[-1], 3, (IC - 1) * P:IC * P])\
                        .then_inc(hiddenT_ready, 1)
                    if q < Q - 1:
                        lo_shared(i, 2 * q)
                        mult_shared(i, 2 * q + 1)
                        lo_shared(i, 2 * q + 1)
                    else:
                        out_shared(i, 2)
                    dve.wait_ge(down_done, p + 1)
                    wait(dve, added, 16 * (adds_before(i, q) + 2))
                    V.tensor_copy(y[:, j, 1, :], ps[CAP:P, 4, :]).then_inc(yb_ready, 1)

            steps(dve, body)

        @block.gpsimd
        def _(pool):
            G = nc.gpsimd
            pool.wait_ge(table_in, 32)
            pool.wait_ge(pads_in, 32)

            def add_pair(n, p, jy, qix):
                for e in range(2):
                    wait(pool, added, 16 * (n + e))
                    wait_apart(pool, (ya_ready, yb_ready)[e], p + 1, carried)
                    G.indirect_dma_start(acc, bass.IndirectOffsetOnAxis(ap=scatter_ix[:, qix, e:e + 1], axis=0),
                                         y[:, jy, e, :], None, compute_op=ALU.add).then_inc(added, 16)

            def add_shared(n, i):
                pool.wait_ge(so_ready, NT * (i + 1))
                pool.wait_ge(added, 16 * n)
                G.dma_start(acc[bass.ds(i * SEQ, SEQ), :].rearrange("(s p) d -> p s d", p=P), so[:],
                            accum_op=ALU.add).then_inc(added, 16)

            def body(i):
                peeled = type(i) is int and i == 0
                for q in range(Q):
                    p = Q * i + q
                    j = q % 2
                    wait(pool, rows_in[j], 16 * (2 * i + q // 2))
                    wait(pool, rows_turned, p - 1)
                    wait(pool, wcol_ready, p - 1)
                    G.tensor_copy(gather_ix[:, q:q + 1], gather_all[:, bass.ds(p, 1)]).then_inc(gix_ready, 1)
                    wait_apart(pool, gix_ready, p + 1, carried)
                    G.indirect_dma_start(xg[:, j, :], None, xrow,
                                         bass.IndirectOffsetOnAxis(ap=gather_ix[:, q:q + 1], axis=0))\
                        .then_inc(rows_in[j], 16)
                    if not (peeled and q < 2):
                        add_pair(adds_before(i, q), p - 2, j, (q + 2) % Q)
                    G.tensor_copy(scatter_ix[:, q, :], scatter_all[:, bass.ds(2 * p, 2)]).then_inc(six_ready, 1)
                    pool.wait_ge(six_ready, p + 1)
                    if q == 1 and not peeled:
                        add_shared(adds_before(i, q) + 2, i - 1)

            steps(pool, body)
            n = adds_before(NSEQ, 0)
            for q in range(2):
                add_pair(n, PAIRS - 2 + q, q, Q - 2 + q)
                n += 2
            add_shared(n, NSEQ - 1)
            pool.wait_ge(added, 16 * (n + 1))


_INS = ['x', 'txt', 'L0_tok_log_dt', 'L0_tok_B_ri', 'L0_tok_inv_A_real', 'L0_tok_A_imag',
        'L0_attn_Wq', 'L0_attn_Wk', 'L0_attn_Wv', 'L0_attn_Wo', 'L0_ffn_gate_w',
        'L0_ffn_w_gate', 'L0_ffn_w_up', 'L0_ffn_w_down', 'L0_ffn_sw_gate', 'L0_ffn_sw_up', 'L0_ffn_sw_down']


def build(nc, a, out):
    B, S0, _, _ = a["x"].shape
    S1, D = a["txt"].shape[1:]
    SEQ = S0 + S1
    E = a["L0_ffn_gate_w"].shape[0]
    CAP = out.shape[0] - B * SEQ
    KC = D // P
    h = nc.dram_tensor("tokens_h", (B, S0, D), F32).ap()
    xrow = nc.dram_tensor("rows_scores", (B * SEQ + CAP, D + E), F32).ap()
    x2T = nc.dram_tensor("rows_turned", (B, P, KC, SEQ), F32).ap()
    table = nc.dram_tensor("slot_table", (E * CAP, 1), U32).ap()
    with ExitStack() as ctx:
        NX = sum(a["L0_attn_W" + w].shape[0] for w in "qkv")
        WxT = ctx.enter_context(nc.sbuf_tensor("WxT", [P, 2, KC, NX], F32R))
        WoT = ctx.enter_context(nc.sbuf_tensor("WoT", [P, 2, KC, D], F32R))
        gwT = ctx.enter_context(nc.sbuf_tensor("gwT", [P, KC, E], F32))
        transposed_weights_phase(nc, *[a["L0_attn_W" + w] for w in "qkvo"], a["L0_ffn_gate_w"], a["ident"],
                                 WxT, WoT, gwT)
        state_space_phase(nc, a["x"], *[a["L0_tok_" + w] for w in ("log_dt", "B_ri", "inv_A_real", "A_imag")],
                          a["ident"], h)
        attention_phase(nc, h, a["txt"], [a[w] for w in ("cos", "sin", "ident", "upper", "tok", "slot")],
                        WxT, WoT, gwT, out, xrow, x2T, table, a["empty"])
    experts_phase(nc, out, xrow, x2T, table, *[a["L0_ffn_" + w] for w in
                  ("w_gate", "w_up", "w_down", "sw_gate", "sw_up", "sw_down")], a["ident"])


def kernel(**inputs):
    import concourse.bacc as bacc
    from concourse.bass_utils import run_bass_kernel_spmd

    nc = bacc.Bacc("TRN2", target_bir_lowering=False, num_devices=1, dynamic_dma_scratch_size=8192)
    B, S0 = inputs["x"].shape[:2]
    SEQ = S0 + inputs["txt"].shape[1]
    D = inputs["txt"].shape[2]
    CAP = 64
    arrays = {name: np.ascontiguousarray(inputs[name]) for name in _INS}
    arrays.update(shape_constants(B, SEQ, inputs["L0_ffn_gate_w"].shape[0], CAP))
    arrays = {f"in_{name}": np.ascontiguousarray(a) for name, a in arrays.items()}
    aps = {name[3:]: nc.dram_tensor(name, a.shape, mybir.dt.from_np(a.dtype), kind="ExternalInput").ap()
           for name, a in arrays.items()}
    out = nc.dram_tensor("out_rows", (B * SEQ + CAP, D), F32, kind="ExternalOutput").ap()
    build(nc, aps, out)
    r = run_bass_kernel_spmd(nc, [arrays], core_ids=[0])
    return r.results[0]["out_rows"][:B * SEQ].reshape(B, SEQ, D)
```

```python
from contextlib import ExitStack

import numpy as np

import concourse.bass as bass
from concourse import mybir

F32 = mybir.dt.float32
F32R = mybir.dt.float32r
BF16 = mybir.dt.bfloat16
U32 = mybir.dt.uint32
ALU = mybir.AluOpType
ACT = mybir.ActivationFunctionType
AX = mybir.AxisListType
P = 128


def state_space_phase(nc, x, log_dt, B_ri, inv_A_real, A_imag, ident_in, h_dram, bulk,
                      Wq, Wk, Wv, Wo, gate_w, WxT, WoT, gwT):
    CH, H, N, _ = x.shape
    L = h_dram.shape[2]
    STEP = 64
    NA = L // STEP
    HALF = H // 2
    CHUNK = 32
    NCHUNK = HALF // CHUNK
    CA = CH * NA
    with ExitStack() as ctx:
        def sb(name, shape, dt=F32):
            return ctx.enter_context(nc.sbuf_tensor(name, shape, dt))

        def ps(name, shape, dt=F32):
            return ctx.enter_context(nc.psum_tensor(name, shape, dt))

        def sem(name):
            return ctx.enter_context(nc.semaphore(name))

        C = sb("ss_C", [P, CH, 2, N, 2])
        Bn = sb("ss_B", [P, 2, N, 2])
        ar = sb("ss_ar", [P, 2, N])
        ai = sb("ss_ai", [P, 2, N])
        dt = sb("ss_dt", [P, 2])
        ident = sb("ss_ident", [P, P])
        xr = sb("ss_xr", [P, 2, N])
        xi = sb("ss_xi", [P, 2, N])
        dr = sb("ss_dr", [P, 2, N])
        inv = sb("ss_inv", [P, 2, N])
        t1 = sb("ss_t1", [P, 2, N])
        t2 = sb("ss_t2", [P, 2, N])
        t3 = sb("ss_t3", [P, 2, N])
        zg = sb("ss_zg", [P, 4, 2, N])
        zgT = sb("ss_zgT", [P, 4, HALF])
        E = sb("ss_E", [P, 2, CH, HALF])
        e1 = sb("ss_e1", [P, CH, HALF])
        e2 = sb("ss_e2", [P, CH, HALF])
        zp = sb("ss_zp", [P, 2, 7, HALF])
        Za = sb("ss_Za", [P, 2, NA, HALF])
        sq = sb("ss_sq", [P, 2, NA, HALF])
        Pm = bulk[:, 0:4 * CHUNK * CA].rearrange("p (j r h q) -> p j r h q", j=2, r=2, h=CHUNK)
        Qm = sb("ss_Q", [P, 2, 2, CHUNK, STEP])
        tp = sb("ss_tp", [P, 2, CHUNK, NA])
        tq = sb("ss_tq", [P, 2, CHUNK * STEP // 2])
        out = sb("ss_out", [P, 2, CHUNK, STEP])

        D = Wq.shape[1]
        KC = D // P
        NE = gate_w.shape[0]
        weights = [(w, o) for w in (Wq, Wk, Wv, Wo) for o in range(w.shape[0] // P)]
        NW = len(weights)
        NX = NW - Wo.shape[0] // P
        rows = bulk[:, 0:NW * D].rearrange("p (n d) -> p n d", n=NW)
        grow = bulk[0:NE, NW * D:(NW + 1) * D]
        passing = [out[:, j].rearrange("p h b -> p (h b)")[:, 0:KC * P].rearrange("p (k o) -> p k o", k=KC)
                   for j in range(2)]

        def halves(n):
            if n < NX:
                return [WxT[:, r, :, n * P:(n + 1) * P] for r in range(2)]
            return [WoT[:, r, :, (n - NX) * P:(n - NX + 1) * P] for r in range(2)]
        psT = ps("ss_psT", [P, 5, 4, P])
        psK = ps("ss_psK", [P, 2, 512])

        loaded = sem("ss_loaded")
        exps = sem("ss_exps")
        zg_ready = sem("ss_zg_ready")
        turned = sem("ss_turned")
        powers = sem("ss_powers")
        p_ready = sem("ss_p_ready")
        q_ready = sem("ss_q_ready")
        multiplied = sem("ss_multiplied")
        evacuated = sem("ss_evacuated")
        stored = [sem(f"ss_stored{j}") for j in range(2)]
        dve_step = sem("ss_dve_step")
        pool_step = sem("ss_pool_step")
        q_by_dve = sem("ss_q_by_dve")
        w_loaded = sem("ss_w_loaded")
        w_turned = sem("ss_w_turned")
        w_passed = sem("ss_w_passed")
        w_hi_done = sem("ss_w_hi_done")
        w_lo_done = sem("ss_w_lo_done")
        block = ctx.enter_context(nc.Block())
        HPB = 512 // STEP
        NBANK = CHUNK // HPB

        def z_powers(engine, link, k, temporaries):
            hs = slice(k * CHUNK, (k + 1) * CHUNK)
            q = [Qm[:, k % 2, r] for r in range(2)]
            engine.memset(q[0][:, :, 0:1], 1.0)
            engine.memset(q[1][:, :, 0:1], 0.0)
            for r in range(2):
                link(engine.tensor_copy(q[r][:, :, 1], zp[:, r, 0, hs]))
            n = 2
            level = 1
            while n < STEP:
                z = [zp[:, r, level, hs].rearrange("p (h a) -> p h a", a=1).to_broadcast([P, CHUNK, n])
                     for r in range(2)]
                t = [a[:, 0:CHUNK * n].rearrange("p (h a) -> p h a", a=n) for a in temporaries]
                engine.tensor_tensor(q[0][:, :, n:2 * n], q[0][:, :, 0:n], z[0], ALU.mult)
                engine.tensor_tensor(t[0], q[1][:, :, 0:n], z[1], ALU.mult)
                engine.tensor_tensor(q[1][:, :, n:2 * n], q[0][:, :, 0:n], z[1], ALU.mult)
                link(engine.tensor_tensor(t[1], q[1][:, :, 0:n], z[0], ALU.mult))
                engine.tensor_tensor(q[0][:, :, n:2 * n], q[0][:, :, n:2 * n], t[0], ALU.subtract)
                link(engine.tensor_tensor(q[1][:, :, n:2 * n], q[1][:, :, n:2 * n], t[1], ALU.add))
                n *= 2
                level += 1

        @block.sync
        def _(sp):
            sp.dma_start(ar[:], inv_A_real.rearrange("(s p) n -> p s n", p=P)).then_inc(loaded, 16)
            sp.dma_start(ai[:], A_imag.rearrange("(s p) n -> p s n", p=P)).then_inc(loaded, 16)
            with nc.allow_non_contiguous_dma(reason="256 values of log_dt"):
                sp.dma_start(dt[:], log_dt.rearrange("(s p) -> p s", p=P)).then_inc(loaded, 16)
            sp.dma_start(Bn[:].rearrange("p s n r -> p s (n r)"),
                         B_ri.rearrange("(s p) n r -> p s (n r)", p=P)).then_inc(loaded, 16)
            sp.dma_start(ident[:], ident_in).then_inc(loaded, 16)
            for s in range(2):
                sp.dma_start(C[:, :, s].rearrange("p c n r -> p c (n r)"),
                             x[:, s * P:(s + 1) * P].rearrange("c p n r -> p c (n r)")).then_inc(loaded, 16)
            for n, (w, o) in enumerate(weights):
                sp.dma_start(rows[:, n], w[o * P:(o + 1) * P, :]).then_inc(w_loaded, 16)
            sp.dma_start(grow, gate_w).then_inc(w_loaded, 16)
            for k in range(NCHUNK):
                sp.wait_ge(evacuated, NBANK * (k + 1))
                for s in range(2):
                    h0 = s * HALF + k * CHUNK
                    for c in range(CH):
                        q0 = s * CA + c * NA
                        sp.dma_start(h_dram[c, h0:h0 + CHUNK, :].rearrange("h (a b) -> a h b", b=STEP),
                                     out[q0:q0 + NA, k % 2]).then_inc(stored[k % 2], 16)
            for j in range(2):
                sp.wait_ge(stored[j], 16 * 2 * CH * NCHUNK // 2)

        @block.scalar
        def _(act):
            act.wait_ge(loaded, 16 * 7)
            nc.scalar.activation(ar[:], ar[:], ACT.Exp).then_inc(exps, 1)
            nc.scalar.activation(dt[:], dt[:], ACT.Exp).then_inc(exps, 1)
            for n in range(NW):
                if n >= 2:
                    act.wait_ge(w_lo_done, n - 1)
                act.wait_ge(w_turned, n + 1)
                turned_block = psK[:, n % 2, :].rearrange("p (k o) -> p k o", k=KC)
                nc.scalar.activation(passing[n % 2], turned_block, ACT.Copy).then_inc(w_passed, 1)
                nc.scalar.activation(halves(n)[0], turned_block, ACT.Copy).then_inc(w_hi_done, 1)
            act.wait_ge(w_turned, NW + 1)
            nc.scalar.activation(gwT[:], psK[:, NW % 2, 0:KC * NE].rearrange("p (k e) -> p k e", k=KC), ACT.Copy)\
                .then_inc(w_hi_done, 1)
            act.wait_ge(w_lo_done, NW)
            for k in range(NCHUNK):
                if k >= 2:
                    act.wait_ge(stored[k % 2], 16 * 2 * CH * (k // 2))
                for j in range(NBANK):
                    n = k * NBANK + j
                    act.wait_ge(multiplied, n + 1)
                    nc.scalar.activation(out[:, k % 2, j * HPB:(j + 1) * HPB, :].rearrange("p h b -> p (h b)"),
                                         psK[:, n % 2, :], ACT.Copy).then_inc(evacuated, 1)

        @block.vector
        def _(dve):
            chain = [0]

            def link(ins):
                chain[0] += 1
                ins.then_inc(dve_step, 1)
                dve.wait_ge(dve_step, chain[0])

            dve.wait_ge(exps, 2)
            V = nc.vector
            for s in range(2):
                V.tensor_scalar(xr[:, s], ar[:, s], dt[:, s:s + 1], -0.5, ALU.mult, ALU.mult)
                link(V.tensor_scalar(xi[:, s], ai[:, s], dt[:, s:s + 1], 0.5, ALU.mult, ALU.mult))
            V.tensor_scalar(dr[:], xr[:], -1.0, 1.0, ALU.mult, ALU.add)
            V.tensor_tensor(t1[:], xr[:], xr[:], ALU.mult)
            link(V.tensor_tensor(t2[:], xi[:], xi[:], ALU.mult))
            link(V.tensor_tensor(inv[:], dr[:], dr[:], ALU.mult))
            link(V.tensor_tensor(inv[:], inv[:], t2[:], ALU.add))
            link(V.reciprocal(inv[:], inv[:]))
            link(V.tensor_tensor(t1[:], t1[:], t2[:], ALU.add))
            link(V.tensor_scalar(t1[:], t1[:], -1.0, 1.0, ALU.mult, ALU.add))
            V.tensor_tensor(zg[:, 0], t1[:], inv[:], ALU.mult)
            link(V.scalar_tensor_tensor(out=zg[:, 1], in0=xi[:], scalar=2.0, in1=inv[:], op0=ALU.mult, op1=ALU.mult))
            for s in range(2):
                link(V.tensor_scalar(inv[:, s], inv[:, s], dt[:, s:s + 1], 2.0, ALU.mult, ALU.mult))
            V.tensor_tensor(t1[:], Bn[:, :, :, 0], dr[:], ALU.mult)
            V.tensor_tensor(t2[:], Bn[:, :, :, 1], xi[:], ALU.mult)
            V.tensor_tensor(t3[:], Bn[:, :, :, 0], xi[:], ALU.mult)
            link(V.tensor_tensor(xr[:], Bn[:, :, :, 1], dr[:], ALU.mult))
            V.tensor_tensor(t1[:], t1[:], t2[:], ALU.subtract)
            link(V.tensor_tensor(t3[:], t3[:], xr[:], ALU.add))
            V.tensor_tensor(zg[:, 2], t1[:], inv[:], ALU.mult)
            V.tensor_tensor(zg[:, 3], t3[:], inv[:], ALU.mult).then_inc(zg_ready, 1)

            dve.wait_ge(turned, 1)
            link(V.tensor_copy(zgT[:], psT[:, 0]))
            dve.wait_ge(turned, 2)
            Cr = psT[:, 1:3].rearrange("p u v h -> p (u v) h")
            Ci = psT[:, 3:5].rearrange("p u v h -> p (u v) h")
            g = [zgT[:, 2 + r:3 + r, :].to_broadcast([P, CH, HALF]) for r in range(2)]
            V.tensor_tensor(e1[:], Cr, g[0], ALU.mult)
            link(V.tensor_tensor(e2[:], Ci, g[1], ALU.mult))
            link(V.tensor_tensor(E[:, 0], e1[:], e2[:], ALU.subtract))
            V.tensor_tensor(e1[:], Cr, g[1], ALU.mult)
            link(V.tensor_tensor(e2[:], Ci, g[0], ALU.mult))
            V.tensor_tensor(E[:, 1], e1[:], e2[:], ALU.add)

            link(V.tensor_copy(zp[:, :, 0, :], zgT[:, 0:2, :]))
            for k in range(6):
                a, b = zp[:, 0, k], zp[:, 1, k]
                V.tensor_tensor(sq[:, 0, 0], a, a, ALU.mult)
                V.tensor_tensor(sq[:, 0, 1], b, b, ALU.mult)
                link(V.tensor_tensor(sq[:, 0, 2], a, b, ALU.mult))
                V.tensor_tensor(zp[:, 0, k + 1], sq[:, 0, 0], sq[:, 0, 1], ALU.subtract)
                link(V.tensor_scalar(zp[:, 1, k + 1], sq[:, 0, 2], 2.0, None, ALU.mult))
            V.memset(Za[:, 0, 0], 1.0)
            V.memset(Za[:, 1, 0], 0.0)
            link(V.tensor_copy(Za[:, :, 1, :], zp[:, :, 6, :]))
            n = 2
            while n < NA:
                a, b = Za[:, 0, n // 2], Za[:, 1, n // 2]
                V.tensor_tensor(sq[:, 0, 0], a, a, ALU.mult)
                V.tensor_tensor(sq[:, 0, 1], b, b, ALU.mult)
                link(V.tensor_tensor(sq[:, 0, 2], a, b, ALU.mult))
                V.tensor_tensor(Za[:, 0, n], sq[:, 0, 0], sq[:, 0, 1], ALU.subtract)
                link(V.tensor_scalar(Za[:, 1, n], sq[:, 0, 2], 2.0, None, ALU.mult))
                m = n - 1
                u = [Za[:, r, n:n + 1, :].to_broadcast([P, m, HALF]) for r in range(2)]
                v = [Za[:, r, 1:n, :] for r in range(2)]
                V.tensor_tensor(Za[:, 0, n + 1:2 * n], u[0], v[0], ALU.mult)
                link(V.tensor_tensor(sq[:, 0, 0:m], u[1], v[1], ALU.mult))
                V.tensor_tensor(Za[:, 1, n + 1:2 * n], u[0], v[1], ALU.mult)
                link(V.tensor_tensor(sq[:, 1, 0:m], u[1], v[0], ALU.mult))
                V.tensor_tensor(Za[:, 0, n + 1:2 * n], Za[:, 0, n + 1:2 * n], sq[:, 0, 0:m], ALU.subtract)
                link(V.tensor_tensor(Za[:, 1, n + 1:2 * n], Za[:, 1, n + 1:2 * n], sq[:, 1, 0:m], ALU.add))
                n *= 2
            dve.sem_inc(powers, 1)

            dve.wait_ge(w_turned, NW + 1)
            for k in range(NCHUNK):
                hs = slice(k * CHUNK, (k + 1) * CHUNK)
                if k >= 2:
                    dve.wait_ge(multiplied, NBANK * (k - 1))
                za = [Za[:, r, :, hs].rearrange("p a h -> p h a") for r in range(2)]
                for c in range(CH):
                    pr = Pm[:, k % 2, 0, :, c * NA:(c + 1) * NA]
                    pi = Pm[:, k % 2, 1, :, c * NA:(c + 1) * NA]
                    er = E[:, 0, c, hs].rearrange("p (h a) -> p h a", a=1).to_broadcast([P, CHUNK, NA])
                    ei = E[:, 1, c, hs].rearrange("p (h a) -> p h a", a=1).to_broadcast([P, CHUNK, NA])
                    V.tensor_tensor(pr, er, za[0], ALU.mult)
                    V.tensor_tensor(tp[:, 0], ei, za[1], ALU.mult)
                    V.tensor_tensor(tp[:, 1], er, za[1], ALU.mult)
                    link(V.scalar_tensor_tensor(out=pi, in0=ei, scalar=-1.0, in1=za[0], op0=ALU.mult, op1=ALU.mult))
                    V.tensor_tensor(pr, pr, tp[:, 0], ALU.subtract)
                    link(V.tensor_tensor(pi, pi, tp[:, 1], ALU.subtract))
                dve.sem_inc(p_ready, 1)
                if k % 2 == 1:
                    z_powers(V, link, k, [e[:].rearrange("p c h -> p (c h)") for e in (e1, e2)])
                    dve.sem_inc(q_by_dve, 1)

        @block.gpsimd
        def _(pool):
            chain = [0]

            def link(ins):
                chain[0] += 1
                ins.then_inc(pool_step, 1)
                pool.wait_ge(pool_step, chain[0])

            G = nc.gpsimd
            for n in range(NW):
                pool.wait_ge(w_passed, n + 1)
                pool.wait_ge(w_hi_done, n + 1)
                hi, lo = halves(n)
                G.tensor_tensor(lo, passing[n % 2], hi, ALU.subtract).then_inc(w_lo_done, 1)
            pool.wait_ge(powers, 1)
            for k in range(0, NCHUNK, 2):
                if k >= 2:
                    pool.wait_ge(multiplied, NBANK * (k - 1))
                z_powers(G, link, k, [tq[:, r] for r in range(2)])
                pool.sem_inc(q_ready, 1)

        @block.tensor
        def _(pe):
            T = nc.tensor
            pe.wait_ge(loaded, 16 * 7)
            for r in range(2):
                for c in range(CH):
                    T.transpose(psT[:, 1 + 2 * r + c // 4, c % 4, :], C[:, c, :, :, r].rearrange("p s n -> p (s n)"), ident[:])
            pe.wait_ge(zg_ready, 1)
            for j in range(4):
                m = T.transpose(psT[:, 0, j, :], zg[:, j].rearrange("p s n -> p (s n)"), ident[:])
            m.then_inc(turned, 2)
            pe.wait_ge(w_loaded, 16 * (NW + 1))
            for n in range(NW + 1):
                if n >= 2:
                    pe.wait_ge(w_hi_done, n - 1)
                for k in range(KC):
                    ks = slice(k * P, (k + 1) * P)
                    if n < NW:
                        m = T.transpose(psK[:, n % 2, ks], rows[:, n, ks], ident[:])
                    else:
                        m = T.transpose(psK[:, n % 2, k * NE:(k + 1) * NE], grow[:, ks], ident[0:NE, 0:NE])
                m.then_inc(w_turned, 1)
            pe.wait_ge(w_hi_done, NW + 1)
            for k in range(NCHUNK):
                pe.wait_ge(p_ready, k + 1)
                pe.wait_ge((q_ready, q_by_dve)[k % 2], k // 2 + 1)
                for j in range(NBANK):
                    n = k * NBANK + j
                    if n >= 2:
                        pe.wait_ge(evacuated, n - 1)
                    for i in range(HPB):
                        h = j * HPB + i
                        for r in range(2):
                            for s in range(2):
                                m = T.matmul(psK[64 * s:64 * s + 64, n % 2, i * STEP:(i + 1) * STEP],
                                             Pm[64 * s:64 * s + 64, k % 2, r, h, :],
                                             Qm[64 * s:64 * s + 64, k % 2, r, h, :],
                                             start=(r == 0), stop=(r == 1))
                    m.then_inc(multiplied, 1)
ROUTE_STEPS = 11


def shape_constants(B, SEQ, E, CAP):
    HD = 32
    NT = SEQ // P
    inv = (np.float32(1.0) / np.float32(10000.0) ** (np.arange(0, HD, 2, dtype=np.float32) / np.float32(HD))).astype(np.float32)
    f = np.arange(SEQ, dtype=np.float32)[:, None] * inv[None]
    emb = np.concatenate([f, f], axis=-1)
    sign = np.where(np.arange(HD) < HD // 2, -1.0, 1.0).astype(np.float32)
    tiles = lambda a: np.ascontiguousarray(a.reshape(NT, P, HD).transpose(1, 0, 2))
    t = np.arange(P)
    return {
        "cos": tiles(np.cos(emb).astype(np.float32)),
        "sin": tiles(np.sin(emb).astype(np.float32) * sign),
        "ident": np.eye(P, dtype=np.float32),
        "upper": np.stack([(t[:, None] < t[None]).astype(np.float32), np.ones((P, P), np.float32)], axis=1),
        "tok": (t[:, None] + P * np.arange(NT)[None]).astype(np.float32),
        "slot": np.stack([np.broadcast_to(np.arange(E, dtype=np.float32), (P, E)),
                          np.broadcast_to(CAP * np.arange(E, dtype=np.float32), (P, E))]),
        "empty": (B * SEQ + np.arange(E * CAP) % CAP).astype(np.uint32)[:, None],
    }


def wait(engine, semaphore, value):
    if type(value) is int and value <= 0:
        return
    engine.wait_ge(semaphore, value)


def wait_apart(engine, semaphore, value, carrier):
    if type(value) is int and value <= 0:
        return
    engine.wait_ge(semaphore, value)
    engine.sem_inc(carrier, 1)
def attention_phase(nc, h_dram, txt, tabs, WxT, WoT, gwT, acc, xrow, x2T_dram, slot_table, consts, bulk,
                    load_ahead):
    (cos_in, sin_in, ident_in, upper_in, tok_in, slot_in) = tabs
    B, S0, D = h_dram.shape
    SEQ = S0 + txt.shape[1]
    NT = SEQ // P
    KC = D // P
    NH, NKV, HD = 16, 4, 32
    HT = NH + NKV
    REP = NH // NKV
    E, TOPK, CAP = 64, 6, 64
    SPLIT = 3 * HD
    QR = SPLIT + 1
    NSLOT = E * CAP
    RING = 2 * REP
    EPS = 1e-5
    with ExitStack() as ctx:
        def sb(name, shape, dt=F32):
            return ctx.enter_context(nc.sbuf_tensor(name, shape, dt))

        def sem(name):
            return ctx.enter_context(nc.semaphore(name))

        ident = sb("at_ident", [P, P])
        identb = sb("at_identb", [P, P], BF16)
        ones = sb("at_ones", [P, HD])
        upper = sb("at_upper", [P, 2, P], BF16)
        cos = sb("at_cos", [P, NT, HD])
        sin = sb("at_sin", [P, NT, HD])
        mhalf = sb("at_mhalf", [P, NT])
        xn = sb("at_xn", [P, NT, D])
        hr = sb("at_hr", [P, NT, D])
        bn = sb("at_bn", [P, NT, 6])
        mv = sb("at_mv", [P, NT, 2])
        ve = sb("at_ve", [P, NT])
        rstd = sb("at_rstd", [P, NT])
        shift = sb("at_shift", [P, NT])
        bn2 = sb("at_bn2", [P, NT, 6])
        mv2 = sb("at_mv2", [P, NT, 2])
        ve2 = sb("at_ve2", [P, NT])
        rstd2 = sb("at_rstd2", [P, NT])
        shift2 = sb("at_shift2", [P, NT])
        xT = sb("at_xT", [P, 2, KC, SEQ], F32R)
        oTs = sb("at_oTs", [P, 2, KC, SEQ], F32R)
        r1 = sb("at_r1", [P, 2, HT, HD])
        r2 = sb("at_r2", [P, 2, HT, HD])
        Q3 = sb("at_Q3", [P, NT, HT, QR])
        qb = sb("at_qb", [P, NT, 5, P], BF16)
        qbT = sb("at_qbT", [P, NT, 5, P], BF16)
        vn = sb("at_vn", [P, NT, NKV * HD])
        vv = sb("at_v", [P, NT, NKV * HD])
        QT = sb("at_QT", [QR, HT, SEQ], F32R)
        PT = bulk[:].rearrange("p (r t q) -> p r t q", r=RING, t=NT)
        rsums = sb("at_rsums", [P, SEQ])
        oT = sb("at_oT", [P, 2, SEQ])
        x2 = sb("at_x2", [P, NT, D + E])
        x2T = sb("at_x2T", [P, KC, SEQ])
        lg = sb("at_lg", [P, NT, E])
        mx = sb("at_mx", [P, NT, 8])
        mi = sb("at_mi", [P, NT, 8], U32)
        mf = sb("at_mf", [P, NT, 8])
        nm = sb("at_nm", [P, NT])
        es = sb("at_es", [P, NT, E])
        ssum = sb("at_ssum", [P, NT])
        rsum = sb("at_rsum", [P, NT])
        iota = sb("at_iota", [P, E])
        slot0 = sb("at_slot0", [P, E])
        hot = sb("at_hot", [P, NT * TOPK, E], BF16)
        mask = sb("at_mask", [P, NT, E], BF16)
        base = sb("at_base", [P, E])
        pos = sb("at_pos", [P, NT, E])
        over = sb("at_over", [P, NT, E])
        hv = r2[:].rearrange("p u h d -> p (u h d)")[:, 0:NT * TOPK * E].rearrange("p (k e) -> p k e", e=E)
        sf = sb("at_sf", [P, NT * TOPK])
        si = sb("at_si", [P, NT * TOPK], U32)
        tokf = sb("at_tokf", [P, NT])
        toki = sb("at_toki", [P, NT], U32)
        upf = PT[:, 0, 0, 0:2 * P].rearrange("p (a t) -> p a t", a=2)
        ps = ctx.enter_context(nc.psum_tensor("at_ps", [P, 8, 512], F32))

        names = """consts_in consts_ok ones_ok a_in r_in var_ready rstd_ready xn_ready x_turned xhi_ready
            xlo_ready q_ready kv_ready rope_q rope_mul rope_add v_copied v_moved q_hi q_lo qb_ready
            qb_turned qbT_ready raw_scores max_ready q_turned qT_by_act qT_by_dve scores_ready probs_ready
            pv_done o_ready ohi_ready olo_ready proj_done h2_ready var2_ready rstd2_ready x2_ready x2_turned
            x2T_ready logits_ready lg_copied place_ready slot_rows_ready gmax_ready gexp_ready mask_ready
            pos_ready pos_read score_rows slots_ready h2_stored x2_stored x2T_stored scattered table_set
            stats_step divide_step row_step rstd_step rstd_step2 slot_step route_step carried_dve
            carried_pool carried_sp""".split()
        (consts_in, consts_ok, ones_ok, a_in, r_in, var_ready, rstd_ready, xn_ready, x_turned, xhi_ready,
         xlo_ready, q_ready, kv_ready, rope_q, rope_mul, rope_add, v_copied, v_moved, q_hi, q_lo, qb_ready,
         qb_turned, qbT_ready, raw_scores, max_ready, q_turned, qT_by_act, qT_by_dve, scores_ready, probs_ready,
         pv_done, o_ready, ohi_ready, olo_ready, proj_done, h2_ready, var2_ready, rstd2_ready, x2_ready,
         x2_turned, x2T_ready, logits_ready, lg_copied, place_ready, slot_rows_ready, gmax_ready, gexp_ready,
         mask_ready, pos_ready, pos_read, score_rows, slots_ready, h2_stored, x2_stored, x2T_stored, scattered,
         table_set, stats_step, divide_step, row_step, rstd_step, rstd_step2, slot_step, route_step,
         carried_dve, carried_pool, carried_sp) = [sem("at_" + n) for n in names]
        block = ctx.enter_context(nc.Block())

        def wide(t):
            return t[:, :].rearrange("p (a e) -> p a e", a=1).to_broadcast([P, NT, E])

        SLOTS = NH + REP
        NMAX = NT * NH
        MAX_FROM = 10
        SPLIT_SLOTS = (12, 13, 15, 19)
        FREE = 5

        def maxima(n):
            if n < MAX_FROM:
                return range(0)
            left = SLOTS - MAX_FROM
            a, m = n - MAX_FROM, NMAX // left
            more = NMAX % left
            return range(a * m + min(a, more), (a + 1) * m + min(a + 1, more))

        def iterations(engine, body, last_full=B - 1):
            body(-1, True, False, False, False)
            body(0, True, True, False, False)
            body(1, True, True, True, False)
            body(2, True, True, True, True)
            with engine.Fori(3, last_full) as b:
                body(b, True, True, True, True)
            for b in range(last_full, B - 1):
                body(b, True, True, True, True)
            body(B - 1, False, True, True, True)
            body(B, False, False, True, True)
            body(B + 1, False, False, False, True)

        @block.sync
        def _(sp):
            for dst, src in ((ident[:], ident_in), (cos[:], cos_in), (sin[:], sin_in), (upf, upper_in),
                             (tokf[:], tok_in), (iota[:], slot_in[0]), (slot0[:], slot_in[1])):
                sp.dma_start(dst, src).then_inc(consts_in, 16)

            def rows_in(dst, b, done):
                sp.dma_start(dst[:, 0:S0 // P, :], h_dram[b].rearrange("(s p) d -> p s d", p=P)).then_inc(done, 16)
                sp.dma_start(dst[:, S0 // P:NT, :], txt[b].rearrange("(s p) d -> p s d", p=P)).then_inc(done, 16)

            def body(b, nxt, main, prev, prev2):
                if prev:
                    c = b - 1
                    wait_apart(sp, h2_stored, 16 * c, carried_sp)
                    wait_apart(sp, x2_ready, NT * c, carried_sp)
                    rows_in(hr, c, r_in)
                if prev and not main:
                    sp.wait_ge(pv_done, NKV * B)
                    load_ahead(sp)
                if type(b) is not int or b < B - 2:
                    wait_apart(sp, x_turned, KC * (b + 2), carried_sp)
                    rows_in(xn, b + 2, a_in)
                if prev2:
                    d = b - 2
                    wait_apart(sp, score_rows, d + 1, carried_sp)
                    sp.dma_start(xrow[bass.ds(d * SEQ, SEQ), :].rearrange("(s p) d -> p s d", p=P), x2[:])\
                        .then_inc(x2_stored, 16)
                if prev:
                    wait_apart(sp, h2_ready, NT * (c + 1), carried_sp)
                    sp.dma_start(acc[bass.ds(c * SEQ, SEQ), :].rearrange("(s p) d -> p s d", p=P), hr[:])\
                        .then_inc(h2_stored, 16)
                    wait_apart(sp, x2T_ready, KC * (c + 1), carried_sp)
                    sp.dma_start(x2T_dram[c], x2T[:]).then_inc(x2T_stored, 16)

            rows_in(xn, 0, a_in)
            iterations(sp, body, last_full=B - 2)
            for done in (h2_stored, x2_stored, x2T_stored):
                sp.wait_ge(done, 16 * B)

        @block.tensor
        def _(pe):
            T = nc.tensor
            pe.wait_ge(consts_in, 16 * 7)
            pe.wait_ge(consts_ok, 1)
            pe.wait_ge(ones_ok, 1)

            def product(out, xs, x_cols, ws, w_cols, chunks):
                n = 0
                for k in range(chunks):
                    for xa, wa in ((0, 0), (0, 1), (1, 0)):
                        m = T.matmul(out, xs[:, xa, k, x_cols], ws[:, wa, k, w_cols],
                                     start=(n == 0), stop=(n == 3 * chunks - 1))
                        n += 1
                return m

            def turned_heads(b):
                wait(pe, max_ready, NMAX * (b + 1))
                wait(pe, q_hi, 3 * NT * (b + 1))
                wait(pe, q_lo, NT * (b + 1))
                wait(pe, o_ready, NKV * b)
                wait(pe, probs_ready, NH * NT * b)
                for n in range(HT):
                    if n >= FREE:
                        e = n - FREE
                        wait(pe, qT_by_act if e % 2 == 0 else qT_by_dve, HT // 2 * b + e // 2 + 1)
                    for s in range(NT):
                        m = T.transpose(ps[0:QR, n % FREE, s * P:(s + 1) * P], Q3[:, s, n, :], ident[:])
                    m.then_inc(q_turned, 1)
                wait(pe, qT_by_act, HT // 2 * (b + 1))
                wait(pe, qT_by_dve, HT // 2 * (b + 1))
                wait(pe, v_moved, b + 1)

            def score(b, h, kt):
                if h >= 1:
                    wait(pe, probs_ready, NT * (NH * b + h - 1) + kt + 1)
                T.matmul(ps[:, kt, 0:SEQ], QT[:, NH + h // REP, kt * P:(kt + 1) * P], QT[:, h, :],
                         start=True, stop=True).then_inc(scores_ready, 1)

            def values(b, n, j):
                g = n // REP - 1
                q = 2 * (n % REP) + j
                if g < 0 or q >= 2 * NT:
                    return
                kt, sums = q % NT, q // NT
                if q == 0:
                    wait(pe, probs_ready, NT * (NH * b + REP * (g + 1)))
                    wait(pe, o_ready, NKV * b + g)
                for jj in range(REP):
                    w = ones[:, :] if sums else vv[:, kt, HD * g:HD * (g + 1)]
                    m = T.matmul(ps[HD * jj:HD * (jj + 1), 3 + sums, 0:SEQ], w, PT[:, (REP * g + jj) % RING, kt, :],
                                 start=(kt == 0), stop=(kt == NT - 1))
                if q == 2 * NT - 1:
                    m.then_inc(pv_done, 1)

            def row_maximum(a, u):
                s, r, g = u // NH, u % NH // NKV, u % NKV
                if u == 0:
                    wait(pe, qbT_ready, NT * (a + 1))
                if u >= 2:
                    wait(pe, max_ready, NMAX * a + u - 1)
                rows = slice(HD * g, HD * (g + 1))
                T.matmul(ps[:, 5 + u % 2, 0:SEQ], qbT[rows, s, r, :], qbT[rows, :, 4, :],
                         start=True, stop=True).then_inc(raw_scores, 1)

            def next_sequence(a, n):
                if n == 0:
                    wait(pe, xn_ready, NT * (a + 1))
                    wait(pe, max_ready, NMAX * a)
                    for k in range(KC):
                        if k >= 2:
                            wait(pe, xlo_ready, KC * a + k - 1)
                        for s in range(NT):
                            m = T.transpose(ps[:, 5 + k % 2, s * P:(s + 1) * P], xn[:, s, k * P:(k + 1) * P], ident[:])
                        m.then_inc(x_turned, 1)
                if n in (1, 3, 5):
                    s = n // 2
                    if s == 0:
                        wait(pe, xhi_ready, KC * (a + 1))
                        wait(pe, xlo_ready, KC * (a + 1))
                    wait(pe, rope_q, NT * a + s)
                    product(ps[:, 5, 0:NH * HD], xT, slice(s * P, (s + 1) * P), WxT, slice(0, NH * HD), KC)\
                        .then_inc(q_ready, 1)
                if n in (2, 4, 6):
                    s = n // 2 - 1
                    wait(pe, rope_mul, NT * a + s)
                    wait(pe, v_copied, NT * a + s)
                    product(ps[:, 6, 0:2 * NKV * HD], xT, slice(s * P, (s + 1) * P), WxT,
                            slice(NH * HD, (NH + 2 * NKV) * HD), KC).then_inc(kv_ready, 1)
                for s in {8: (0, 1), 9: (2,)}.get(n, ()):
                    wait(pe, qb_ready, NT * a + s + 1)
                    wait(pe, rope_mul, NT * (a + 1))
                    wait(pe, v_copied, NT * (a + 1))
                    if s == 2:
                        wait(pe, qbT_ready, NT * a + 1)
                    for r in range(5):
                        m = T.transpose(ps[:, 5 + s % 2].bitcast(BF16)[:, r * P:(r + 1) * P], qb[:, s, r, :], identb[:])
                    m.then_inc(qb_turned, 1)

            def sequence_before(c, n):
                if n in (7, 9, 11):
                    s = (n - 7) // 2
                    if s == 0:
                        wait(pe, ohi_ready, NKV * (c + 1))
                        wait(pe, olo_ready, NKV * (c + 1))
                        wait(pe, pos_read, c)
                    wait(pe, h2_ready, NT * c + s)
                    product(ps[:, 7, :], oTs, slice(s * P, (s + 1) * P), WoT, slice(0, D), KC).then_inc(proj_done, 1)
                if n in (14, 15, 16, 17):
                    k = n - 14
                    if k == 0:
                        wait(pe, x2_ready, NT * (c + 1))
                    else:
                        wait(pe, x2T_ready, KC * c + k)
                    for s in range(NT):
                        m = T.transpose(ps[:, 7, s * P:(s + 1) * P], x2[:, s, k * P:(k + 1) * P], ident[:])
                    m.then_inc(x2_turned, 1)

            def routing(c, n):
                if n == 0:
                    wait(pe, x2T_ready, KC * (c + 1))
                    for s in range(NT):
                        for k in range(KC):
                            m = T.matmul(ps[:, 7, s * E:(s + 1) * E], x2T[:, k, s * P:(s + 1) * P], gwT[:, k, :],
                                         start=(k == 0), stop=(k == KC - 1))
                    m.then_inc(logits_ready, 1)
                if n == 5:
                    wait(pe, mask_ready, c + 1)
                    for s in range(NT + 1):
                        for q in range(min(s, NT - 1) + 1):
                            m = T.matmul(ps[:, 7, 256 + s * E:256 + (s + 1) * E], upper[:, 0 if q == s else 1, :],
                                         mask[:, q, :], start=(q == 0), stop=(q == min(s, NT - 1)))
                    m.then_inc(pos_ready, 1)

            def body(b, nxt, main, prev, prev2):
                if main:
                    turned_heads(b)
                for n in range(SLOTS):
                    units = maxima(n) if nxt else ()
                    for j in range(6):
                        if main and j < NT and n < NH:
                            score(b, n, j)
                        if main and j in (3, 4):
                            values(b, n, j - 3)
                        if j < len(units):
                            row_maximum(b + 1, units[j])
                    if nxt:
                        next_sequence(b + 1, n)
                    if prev:
                        sequence_before(b - 1, n)
                    if prev2:
                        routing(b - 2, n)

            iterations(pe, body)

        @block.scalar
        def _(act):
            A = nc.scalar
            act.wait_ge(consts_in, 16 * 7)
            A.activation(identb[:], ident[:], ACT.Copy)
            A.activation(upper[:], upf, ACT.Copy).then_inc(consts_ok, 1)

            def next_sequence(a, n):
                if n == 0:
                    for k in range(KC):
                        wait(act, x_turned, KC * a + k + 1)
                        wait(act, kv_ready, NT * a)
                        A.activation(xT[:, 0, k, :], ps[:, 5 + k % 2, 0:SEQ], ACT.Copy).then_inc(xhi_ready, 1)
                if n in (3, 5, 7):
                    s = n // 2 - 1
                    wait(act, rope_mul, NT * a + s + 1)
                    wait(act, v_moved, a)
                    A.activation(vn[:, s, :], ps[:, 6, P:2 * P], ACT.Copy).then_inc(v_copied, 1)
                if n in (4, 6, 8):
                    s = n // 2 - 2
                    wait(act, rope_add, NT * a + s + 1)
                    qk = r1[:, s % 2]
                    A.activation(Q3[:, s, :, 0:HD].bitcast(F32R), qk, ACT.Copy).then_inc(q_hi, 1)
                    A.activation(qb[:, s, 0:4, :].rearrange("p r (g d) -> p g r d", g=NKV),
                                 qk[:, 0:NH, :].rearrange("p (g r) d -> p g r d", g=NKV), ACT.Copy)
                    A.activation(qb[:, s, 4, :].rearrange("p (g d) -> p g d", g=NKV), qk[:, NH:HT, :], ACT.Copy)\
                        .then_inc(qb_ready, 1)
                    wait(act, q_hi, 3 * (NT * a + s) + 1)
                    A.activation(Q3[:, s, 0:NH, 2 * HD:3 * HD], Q3[:, s, 0:NH, 0:HD], ACT.Copy).then_inc(q_hi, 1)
                    A.activation(Q3[:, s, NH:HT, HD:2 * HD], Q3[:, s, NH:HT, 0:HD], ACT.Copy).then_inc(q_hi, 1)
                for s in {8: (0, 1), 9: (2,)}.get(n, ()):
                    wait(act, qb_turned, NT * a + s + 1)
                    A.activation(qbT[:, s], ps[:, 5 + s % 2].bitcast(BF16)[:, 0:5 * P]
                                 .rearrange("p (r t) -> p r t", r=5), ACT.Copy).then_inc(qbT_ready, 1)

            def out_hi(b, g):
                wait(act, o_ready, NKV * b + g + 1)
                wait(act, proj_done, NT * b)
                A.activation(oTs[:, 0, g, :], oT[:, g % 2, :], ACT.Copy).then_inc(ohi_ready, 1)

            def sequence_before(c, n):
                if n == 13:
                    wait(act, rstd2_ready, c + 1)
                    wait(act, x2_stored, 16 * c)
                    for s in range(NT):
                        A.activation(x2[:, s, 0:D], hr[:, s, :], ACT.Identity, bias=shift2[:, s:s + 1],
                                     scale=rstd2[:, s:s + 1]).then_inc(x2_ready, 1)
                if n in (14, 15, 16, 17):
                    k = n - 14
                    wait(act, x2_turned, KC * c + k + 1)
                    wait(act, x2T_stored, 16 * c)
                    A.activation(x2T[:, k, :], ps[:, 7, 0:SEQ], ACT.Copy).then_inc(x2T_ready, 1)

            def routing(c, n):
                if n == 1:
                    wait(act, logits_ready, c + 1)
                    A.activation(lg[:], ps[:, 7, 0:NT * E].rearrange("p (s e) -> p s e", s=NT), ACT.Copy)\
                        .then_inc(lg_copied, 1)
                if n == 3:
                    wait(act, gmax_ready, c + 1)
                    for s in range(NT):
                        A.activation(es[:, s, :], lg[:, s, :], ACT.Exp, bias=nm[:, s:s + 1],
                                     accum_out=ssum[:, s:s + 1]).then_inc(gexp_ready, 1)

            def body(b, nxt, main, prev, prev2):
                if main:
                    for n in range(0, HT, 2):
                        wait(act, q_turned, HT * b + n + 1)
                        A.activation(QT[:, n, :], ps[0:QR, n % FREE, 0:SEQ], ACT.Copy).then_inc(qT_by_act, 1)
                if nxt:
                    wait(act, rstd_ready, b + 2)
                    for s in range(NT):
                        A.activation(xn[:, s, :], xn[:, s, :], ACT.Identity, bias=shift[:, s:s + 1],
                                     scale=rstd[:, s:s + 1]).then_inc(xn_ready, 1)
                for n in range(SLOTS):
                    if main and n < NH:
                        if n >= RING:
                            wait(act, pv_done, NKV * b + (n - RING) // REP + 1)
                        for kt in range(NT):
                            wait(act, scores_ready, NT * (NH * b + n) + kt + 1)
                            A.activation(PT[:, n % RING, kt, :], ps[:, kt, 0:SEQ], ACT.Exp, scale=float(HD) ** -0.5)\
                                .then_inc(probs_ready, 1)
                    if nxt:
                        next_sequence(b + 1, n)
                    if prev:
                        sequence_before(b - 1, n)
                    if prev2:
                        routing(b - 2, n)
                    if main and n in SPLIT_SLOTS:
                        out_hi(b, SPLIT_SLOTS.index(n))

            iterations(act, body)

        @block.vector
        def _(dve):
            V = nc.vector
            V.memset(mhalf[:], -0.5)
            V.memset(base[:], 0.0)
            V.memset(ones[:], 1.0)
            V.memset(Q3[:, :, NH:HT, SPLIT:QR], 1.0).then_inc(ones_ok, 1)
            dve.wait_ge(consts_in, 16 * 7)
            dve.wait_ge(ones_ok, 1)
            done = {}

            def link(ins, chain, total, seq, apart=False):
                done[chain] = done.get(chain, 0) + 1
                semaphore = {"stats": stats_step, "rows": row_step, "route": route_step}[chain]
                ins.then_inc(semaphore, 1)
                (wait_apart if apart else wait)(dve, semaphore, seq * total + done[chain],
                                                *((carried_dve,) if apart else ()))

            NSTAT, NROW, NROUTE = 2, 2, ROUTE_STEPS

            def row_maxima(a, units):
                for u in units:
                    s, r, g = u // NH, u % NH // NKV, u % NKV
                    wait(dve, raw_scores, NMAX * a + u + 1)
                    h = REP * g + r
                    V.tensor_reduce(Q3[:, s, h, SPLIT:QR], ps[:, 5 + u % 2, 0:SEQ], AX.X, ALU.max, negate=True)\
                        .then_inc(max_ready, 1)

            def statistics(a):
                wait(dve, a_in, 32 * (a + 1))
                for s in range(NT):
                    ins = V.bn_stats(bn[:, s, :], xn[:, s, :])
                link(ins, "stats", NSTAT, a, apart=True)
                for s in range(NT):
                    ins = V.bn_aggr(mv[:, s, :], bn[:, s, :])
                link(ins, "stats", NSTAT, a)
                V.tensor_scalar(shift[:], mv[:, :, 0], -1.0, None, ALU.mult)
                V.tensor_scalar(ve[:], mv[:, :, 1], EPS, None, ALU.add).then_inc(var_ready, 1)

            def next_sequence(a, n):
                if n == 0:
                    for k in range(KC):
                        wait(dve, xhi_ready, KC * a + k + 1)
                        V.tensor_tensor(xT[:, 1, k, :], ps[:, 5 + k % 2, 0:SEQ], xT[:, 0, k, :].bitcast(F32),
                                        ALU.subtract).then_inc(xlo_ready, 1)
                if n in (2, 4, 6):
                    s = n // 2 - 1
                    half = HD // 2
                    wait(dve, qb_ready, NT * a + s - 1)
                    wait(dve, q_lo, NT * a + s - 1)
                    for bank, h0, heads, ready, used in ((5, 0, NH, q_ready, rope_q), (6, NH, NKV, kv_ready, rope_mul)):
                        wait(dve, ready, NT * a + s + 1)
                        x = ps[:, bank, 0:heads * HD].rearrange("p (h d) -> p h d", d=HD)
                        h = slice(h0, h0 + heads)
                        V.tensor_tensor(r1[:, s % 2, h], x, cos[:, s:s + 1, :].to_broadcast([P, heads, HD]), ALU.mult)
                        V.tensor_tensor(r2[:, s % 2, h, 0:half], x[:, :, half:HD],
                                        sin[:, s:s + 1, 0:half].to_broadcast([P, heads, half]), ALU.mult)
                        V.tensor_tensor(r2[:, s % 2, h, half:HD], x[:, :, 0:half],
                                        sin[:, s:s + 1, half:HD].to_broadcast([P, heads, half]), ALU.mult)\
                            .then_inc(used, 1)

            def reciprocal(b, g, piece):
                if piece == 0:
                    wait(dve, pv_done, NKV * b + g + 1)
                q = slice(piece * P, (piece + 1) * P)
                V.reciprocal(rsums[:, q], ps[:, 4, q]).then_inc(divide_step, 1)

            def divide(b, g):
                wait(dve, divide_step, NT * (NKV * b + g + 1))
                wait(dve, olo_ready, NKV * b + g - 1)
                V.tensor_tensor(oT[:, g % 2, :], ps[:, 3, 0:SEQ], rsums[:], ALU.mult).then_inc(o_ready, 1)

            def sequence_before(c, n):
                if n in (8, 10, 12):
                    s = (n - 8) // 2
                    if s == 0:
                        wait(dve, r_in, 32 * (c + 1))
                    wait(dve, proj_done, NT * c + s + 1)
                    V.tensor_tensor(hr[:, s, :], hr[:, s, :], ps[:, 7, :], ALU.add).then_inc(h2_ready, 1)
                if n == 12:
                    wait(dve, h2_ready, NT * (c + 1))
                    for s in range(NT):
                        ins = V.bn_stats(bn2[:, s, :], hr[:, s, :])
                    link(ins, "rows", NROW, c, apart=True)
                    for s in range(NT):
                        ins = V.bn_aggr(mv2[:, s, :], bn2[:, s, :])
                    link(ins, "rows", NROW, c)
                    V.tensor_scalar(shift2[:], mv2[:, :, 0], -1.0, None, ALU.mult)
                    V.tensor_scalar(ve2[:], mv2[:, :, 1], EPS, None, ALU.add).then_inc(var2_ready, 1)

            def routing(c, n):
                def chain(ins, apart=False):
                    link(ins, "route", NROUTE, c, apart)

                if n == 1:
                    wait_apart(dve, lg_copied, c + 1, carried_dve)
                    for s in range(NT):
                        ins = V.max(mx[:, s, :], lg[:, s, :])
                    chain(ins)
                    V.tensor_scalar(nm[:], mx[:, :, 0], -1.0, None, ALU.mult).then_inc(gmax_ready, 1)
                    for s in range(NT):
                        ins = V.max_index(mi[:, s, :], mx[:, s, :], lg[:, s, :])
                    chain(ins)
                    chain(V.tensor_copy(mf[:], mi[:]))
                if n == 2:
                    for s in range(NT):
                        ins = V.tensor_tensor(
                            hot[:, s * TOPK:(s + 1) * TOPK, :],
                            iota[:, :].rearrange("p (a e) -> p a e", a=1).to_broadcast([P, TOPK, E]),
                            mf[:, s, 0:TOPK].rearrange("p (k a) -> p k a", a=1).to_broadcast([P, TOPK, E]), ALU.is_equal)
                    chain(ins)
                if n == 4:
                    chain(V.tensor_reduce(pos[:], hot[:].rearrange("p (s k) e -> p s e k", s=NT), AX.X, ALU.add))
                    V.tensor_copy(mask[:], pos[:]).then_inc(mask_ready, 1)
                if n == 4:
                    wait(dve, gexp_ready, NT * (c + 1))
                    chain(V.reciprocal(rsum[:], ssum[:]))
                    for s in range(NT):
                        ins = V.tensor_scalar(x2[:, s, D:D + E], es[:, s, :], rsum[:, s:s + 1], None, ALU.mult)
                    ins.then_inc(score_rows, 1)
                if n == 6:
                    wait(dve, pos_ready, c + 1)
                    pp = ps[:, 7, 256:256 + NT * E].rearrange("p (s e) -> p s e", s=NT)
                    chain(V.tensor_tensor(pos[:], pp, wide(base), ALU.add))
                    V.tensor_scalar(over[:], pos[:], float(CAP), 65536.0, ALU.is_ge, ALU.mult)\
                        .then_inc(place_ready, 1)
                    chain(V.tensor_tensor(base[:], base[:], ps[:, 7, 256 + NT * E:256 + (NT + 1) * E], ALU.add))
                    dve.sem_inc(pos_read, 1)
                if n == 9:
                    wait(dve, slot_rows_ready, c + 1)
                    chain(V.tensor_reduce(sf[:], hv[:], AX.X, ALU.add))
                    wait(dve, scattered, 16 * NT * TOPK * c)
                    V.tensor_copy(si[:], sf[:])
                    chain(V.tensor_copy(toki[:], tokf[:]))
                    chain(V.tensor_scalar(tokf[:], tokf[:], float(SEQ), None, ALU.add))
                    dve.sem_inc(slots_ready, 1)

            def body(b, nxt, main, prev, prev2):
                done.clear()
                if nxt:
                    statistics(b + 1)
                if main:
                    for n in range(1, HT, 2):
                        wait(dve, q_turned, HT * b + n + 1)
                        V.tensor_copy(QT[:, n, :], ps[0:QR, n % FREE, 0:SEQ]).then_inc(qT_by_dve, 1)
                for n in range(SLOTS):
                    units = list(maxima(n)) if nxt else []
                    dividing = main and n % REP == REP - 1 and n >= REP
                    g = n // REP - 1
                    for piece in range(NT):
                        if nxt:
                            row_maxima(b + 1, units[piece:piece + 1])
                        if dividing:
                            reciprocal(b, g, piece)
                    if nxt:
                        row_maxima(b + 1, units[NT:])
                    if dividing:
                        divide(b, g)
                    if nxt:
                        next_sequence(b + 1, n)
                    if prev:
                        sequence_before(b - 1, n)
                    if prev2:
                        routing(b - 2, n)
                for chain, total, used in (("stats", NSTAT, nxt), ("rows", NROW, prev),
                                           ("route", NROUTE, prev2)):
                    assert done.get(chain, 0) == (total if used else 0), (chain, done)

            iterations(dve, body)

        @block.gpsimd
        def _(pool):
            G = nc.gpsimd
            G.dma_start(slot_table, consts).then_inc(table_set, 16)
            pool.wait_ge(table_set, 16)
            pool.wait_ge(ones_ok, 1)

            def next_sequence(a, n):
                if n in (2, 4, 6):
                    s = n // 2 - 1
                    wait(pool, rope_mul, NT * a + s + 1)
                    G.tensor_tensor(r1[:, s % 2], r1[:, s % 2], r2[:, s % 2], ALU.add).then_inc(rope_add, 1)
                if n in (4, 6, 8):
                    s = n // 2 - 2
                    wait(pool, q_hi, 3 * (NT * a + s) + 1)
                    wait(pool, rope_add, NT * a + s + 1)
                    G.tensor_tensor(Q3[:, s, 0:NH, HD:2 * HD].bitcast(F32R), r1[:, s % 2, 0:NH],
                                    Q3[:, s, 0:NH, 0:HD], ALU.subtract)
                    G.tensor_tensor(Q3[:, s, NH:HT, 2 * HD:3 * HD].bitcast(F32R), r1[:, s % 2, NH:HT],
                                    Q3[:, s, NH:HT, 0:HD], ALU.subtract).then_inc(q_lo, 1)

            def sequence_before(c, n):
                if n == 12:
                    wait(pool, var2_ready, c + 1)
                    G.tensor_tensor(rstd2[:], ve2[:], mhalf[:], ALU.pow).then_inc(rstd_step2, 1)
                    wait(pool, rstd_step2, c + 1)
                    G.tensor_tensor(shift2[:], shift2[:], rstd2[:], ALU.mult).then_inc(rstd2_ready, 1)

            def routing(c, n):
                if n == 6:
                    wait(pool, place_ready, c + 1)
                    G.tensor_tensor(pos[:], pos[:], wide(slot0), ALU.add).then_inc(slot_step, 1)
                    wait(pool, slot_step, 2 * c + 1)
                    G.tensor_tensor(pos[:], pos[:], over[:], ALU.add).then_inc(slot_step, 1)
                    wait(pool, slot_step, 2 * c + 2)
                    for s in range(NT):
                        ks = slice(s * TOPK, (s + 1) * TOPK)
                        ins = G.tensor_tensor(hv[:, ks, :], hot[:, ks, :],
                                              pos[:, s:s + 1, :].to_broadcast([P, TOPK, E]), ALU.mult)
                    ins.then_inc(slot_rows_ready, 1)
                if n == 10:
                    wait_apart(pool, slots_ready, c + 1, carried_pool)
                    for s in range(NT):
                        for k in range(TOPK):
                            m = s * TOPK + k
                            G.indirect_dma_start(slot_table, bass.IndirectOffsetOnAxis(ap=si[:, m:m + 1], axis=0),
                                                 toki[:, s:s + 1], None, bounds_check=NSLOT - 1, oob_is_err=False,
                                                 compute_op=ALU.bypass).then_inc(scattered, 16)

            def body(b, nxt, main, prev, prev2):
                if nxt:
                    wait(pool, var_ready, b + 2)
                    G.tensor_tensor(rstd[:], ve[:], mhalf[:], ALU.pow).then_inc(rstd_step, 1)
                    wait(pool, rstd_step, b + 2)
                    G.tensor_tensor(shift[:], shift[:], rstd[:], ALU.mult).then_inc(rstd_ready, 1)
                if main:
                    wait_apart(pool, v_copied, NT * (b + 1), carried_pool)
                    wait_apart(pool, pv_done, NKV * b, carried_pool)
                    G.tensor_copy(vv[:], vn[:]).then_inc(v_moved, 1)
                for n in range(SLOTS):
                    if nxt:
                        next_sequence(b + 1, n)
                    if prev:
                        sequence_before(b - 1, n)
                    if prev2:
                        routing(b - 2, n)
                    if main and n in SPLIT_SLOTS:
                        g = SPLIT_SLOTS.index(n)
                        wait(pool, ohi_ready, NKV * b + g + 1)
                        G.tensor_tensor(oTs[:, 1, g, :], oT[:, g % 2, :], oTs[:, 0, g, :].bitcast(F32),
                                        ALU.subtract).then_inc(olo_ready, 1)

            iterations(pool, body)
            pool.wait_ge(scattered, 16 * NT * TOPK * B)


def shared_chunks(IS):
    SC = (IS + P - 1) // P
    SW = [IS // SC + (1 if c < IS % SC else 0) for c in range(SC)]
    return SC, SW, [sum(SW[:c]) for c in range(SC)]


def shared_weights_places(bulk, KC, IS, SM, SC, D):
    n = KC * IS
    return [bulk[:, j * n:(j + 1) * n] for j in range(2)], bulk[0:SM, 2 * n:2 * n + SC * D]


def load_shared_weights(sp, bulk, staged, sw_gate, sw_up, sw_down):
    D, IS = sw_gate.shape
    KC = D // P
    SC, SW, SO = shared_chunks(IS)
    stage, staged_d = shared_weights_places(bulk, KC, IS, max(SW), SC, D)
    for j, w in enumerate((sw_gate, sw_up)):
        sp.dma_start(stage[j].rearrange("p (k i) -> p k i", k=KC), w.rearrange("(k p) i -> p k i", p=P))\
            .then_inc(staged[0], 16)
    for c in range(SC):
        sp.dma_start(staged_d[0:SW[c], c * D:(c + 1) * D], sw_down[SO[c]:SO[c] + SW[c], :])\
            .then_inc(staged[1], 16)


def experts_phase(nc, acc, xrow, x2T_dram, slot_table, w_gate, w_up, w_down, sw_gate, sw_up, sw_down, ident_in, bulk,
                  staged):
    E, D, I = w_gate.shape
    IS = sw_gate.shape[1]
    NSEQ, _, KC, SEQ = x2T_dram.shape
    CAP = slot_table.shape[0] // E
    T = NSEQ * SEQ
    NT = SEQ // P
    PAIRS = E // 2
    Q = PAIRS // NSEQ
    IC = (I + P - 1) // P
    IW = [min(P, I - c * P) for c in range(IC)]
    SC, SW, SO = shared_chunks(IS)
    SM = max(SW)
    assert Q == 4 and SC == 2 * (Q - 1) and NT == 3
    with ExitStack() as ctx:
        def sb(name, shape, dt=F32):
            return ctx.enter_context(nc.sbuf_tensor(name, shape, dt))

        def sem(name):
            return ctx.enter_context(nc.semaphore(name))

        ident = sb("mo_ident", [P, P])
        zeros = sb("mo_zeros", [CAP, D + E])
        gather_all = sb("mo_gather_all", [P, PAIRS], U32)
        scatter_all = sb("mo_scatter_all", [CAP, E], U32)
        gather_ix = sb("mo_gather_ix", [P, Q], U32)
        scatter_ix = sb("mo_scatter_ix", [CAP, Q, 2], U32)
        NW = 4 * KC * I
        wgu = [sb("mo_wgu", [P, 2, 2, KC, I])[:],
               bulk[:, 0:NW].rearrange("p (e g k i) -> p e g k i", e=2, g=2, k=KC)]
        wd = [sb("mo_wd", [P, 2, IC, D])[:],
              bulk[:, NW:NW + 2 * IC * D].rearrange("p (e c d) -> p e c d", e=2, c=IC)]
        sgu = sb("mo_sgu", [P, 2, 2, KC, IS], F32R)
        sd = sb("mo_sd", [SM, 2, SC, D], F32R)
        x2 = sb("mo_x2", [P, KC, SEQ])
        x2s = sb("mo_x2s", [P, 2, KC, SEQ], F32R)
        hs = sb("mo_hs", [SM, 2, SC, SEQ], F32R)
        ssil = sb("mo_ssil", [SM, SEQ])
        sh = sb("mo_sh", [SM, 2, SEQ])
        so = sb("mo_so", [P, NT, D])
        xg = sb("mo_xg", [P, 2, D + E])
        xgT = sb("mo_xgT", [P, KC, P])
        wcol = sb("mo_wcol", [P, 2])
        sil = sb("mo_sil", [P, I])
        hm = sb("mo_hm", [P, I])
        hmT = sb("mo_hmT", [P, IC, P])
        y = sb("mo_y", [CAP, 2, 2, D])
        ps = ctx.enter_context(nc.psum_tensor("mo_ps", [P, 8, 512], F32))

        consts_in = sem("mo_consts_in")
        zeros_set = sem("mo_zeros_set")
        pads_in = sem("mo_pads_in")
        table_in = sem("mo_table_in")
        shi_done = sem("mo_shi_done")
        slo_done = sem("mo_slo_done")
        w_in = [sem(f"mo_w_in{j}") for j in range(2)]
        x2_in = sem("mo_x2_in")
        x2hi_ready = sem("mo_x2hi_ready")
        x2lo_ready = sem("mo_x2lo_ready")
        gix_ready = sem("mo_gix_ready")
        six_ready = sem("mo_six_ready")
        rows_in = [sem(f"mo_rows_in{j}") for j in range(2)]
        rows_turned = sem("mo_rows_turned")
        rowsT_ready = sem("mo_rowsT_ready")
        wcol_ready = sem("mo_wcol_ready")
        gate_up_done = sem("mo_gate_up_done")
        silu_done = sem("mo_silu_done")
        hidden_ready = sem("mo_hidden_ready")
        hidden_turned = sem("mo_hidden_turned")
        hiddenT_ready = sem("mo_hiddenT_ready")
        down_done = sem("mo_down_done")
        ya_ready = sem("mo_ya_ready")
        yb_ready = sem("mo_yb_ready")
        s_gate_done = sem("mo_s_gate_done")
        s_up_done = sem("mo_s_up_done")
        s_silu_done = sem("mo_s_silu_done")
        s_mult_done = sem("mo_s_mult_done")
        s_hi_done = sem("mo_s_hi_done")
        s_lo_done = sem("mo_s_lo_done")
        s_down_done = sem("mo_s_down_done")
        so_ready = sem("mo_so_ready")
        added = sem("mo_added")
        carried = sem("mo_carried")
        block = ctx.enter_context(nc.Block())

        stage, staged_d = shared_weights_places(bulk, KC, IS, SM, SC, D)

        def adds_before(i, q):
            return (2 * Q + 1) * i - 2 * (Q - 2) - 1 + 2 * q + (1 if q >= 2 else 0)

        def steps(engine, body):
            body(0)
            with engine.Fori(1, NSEQ - 1) as i:
                body(i)
            body(NSEQ - 1)

        def first(i):
            return type(i) is int and i == 0

        def last(i):
            return type(i) is int and i == NSEQ - 1

        @block.sync
        def _(sp):
            sp.dma_start(ident[:], ident_in).then_inc(consts_in, 16)
            sp.wait_ge(zeros_set, 1)
            sp.dma_start(xrow[T:T + CAP, :], zeros[:]).then_inc(pads_in, 16)
            sp.dma_start(acc[T:T + CAP, :], zeros[:, 0:D]).then_inc(pads_in, 16)
            with nc.allow_non_contiguous_dma(reason="one word for each slot"):
                sp.dma_start(gather_all[:], slot_table.rearrange("(q c) a -> c (q a)", c=P)).then_inc(table_in, 16)
                sp.dma_start(scatter_all[:], slot_table.rearrange("(e c) a -> c (e a)", c=CAP)).then_inc(table_in, 16)

            def body(i):
                for q in range(Q):
                    p = Q * i + q
                    j = q % 2
                    if q == 0:
                        wait(sp, x2hi_ready, i)
                        wait(sp, x2lo_ready, i)
                        sp.dma_start(x2[:], x2T_dram[i]).then_inc(x2_in, 16)
                    if type(p) is int and p == 0:
                        sp.wait_ge(rows_in[0], 16)
                    if type(p) is int and p == 1:
                        sp.wait_ge(slo_done, 3)
                    wait(sp, gate_up_done, p - 1)
                    for e in range(2):
                        for g, w in enumerate((w_gate, w_up)):
                            sp.dma_start(wgu[j][:, e, g], w[2 * p + e].rearrange("(p k) i -> p k i", k=KC))\
                                .then_inc(w_in[j], 16)
                    wait(sp, down_done, p - 1)
                    for e in range(2):
                        sp.dma_start(wd[j][:, e, 0:IC - 1, :],
                                     w_down[2 * p + e][0:(IC - 1) * P, :].rearrange("(c p) d -> p c d", p=P))\
                            .then_inc(w_in[j], 16)
                        sp.dma_start(wd[j][0:IW[-1], e, IC - 1, :], w_down[2 * p + e][(IC - 1) * P:I, :])\
                            .then_inc(w_in[j], 16)

            steps(sp, body)
            sp.wait_ge(pads_in, 32)

        @block.tensor
        def _(pe):
            M = nc.tensor
            pe.wait_ge(consts_in, 16)
            pe.wait_ge(slo_done, 3)

            def shared_in(i, c, g):
                n = SC * i + c
                if c == 0 and g == 0:
                    pe.wait_ge(x2hi_ready, i + 1)
                    pe.wait_ge(x2lo_ready, i + 1)
                wait(pe, s_mult_done, n)
                k3 = 0
                for k in range(KC):
                    for xa, wa in ((0, 0), (0, 1), (1, 0)):
                        m = M.matmul(ps[0:SW[c], 5 + g, 0:SEQ], sgu[:, wa, g, k, SO[c]:SO[c] + SW[c]],
                                     x2s[:, xa, k, :], start=(k3 == 0), stop=(k3 == 3 * KC - 1))
                        k3 += 1
                m.then_inc((s_gate_done, s_up_done)[g], 1)

            def shared_out(i, s):
                wait(pe, so_ready, NT * i + s)
                if s == 0:
                    pe.wait_ge(s_hi_done, SC * (i + 1))
                    pe.wait_ge(s_lo_done, SC * (i + 1))
                k3 = 0
                for c in range(SC):
                    for xa, wa in ((0, 0), (0, 1), (1, 0)):
                        m = M.matmul(ps[:, 7, :], hs[0:SW[c], xa, c, s * P:(s + 1) * P], sd[0:SW[c], wa, c, :],
                                     start=(k3 == 0), stop=(k3 == 3 * SC - 1))
                        k3 += 1
                m.then_inc(s_down_done, 1)

            def body(i):
                for q in range(Q):
                    p = Q * i + q
                    j = q % 2
                    use = 2 * i + q // 2 + 1
                    pe.wait_ge(rows_in[j], 16 * use)
                    wait(pe, rowsT_ready, p)
                    for k in range(KC):
                        m = M.transpose(ps[:, 0, k * P:(k + 1) * P], xg[:, j, k:D:KC], ident[:])
                    m.then_inc(rows_turned, 1)
                    if q < Q - 1:
                        shared_in(i, 2 * q, 0)
                        shared_in(i, 2 * q, 1)
                    else:
                        shared_out(i, 0)
                    pe.wait_ge(rowsT_ready, p + 1)
                    pe.wait_ge(w_in[j], 16 * 8 * use)
                    wait(pe, hidden_ready, p)
                    for g in range(2):
                        for k in range(KC):
                            for e in range(2):
                                m = M.matmul(ps[CAP * e:CAP * (e + 1), 1 + g, 0:I], xgT[:, k, CAP * e:CAP * (e + 1)],
                                             wgu[j][:, e, g, k, :], start=(k == 0), stop=(k == KC - 1))
                    m.then_inc(gate_up_done, 1)
                    if q < Q - 1:
                        shared_in(i, 2 * q + 1, 0)
                    else:
                        shared_out(i, 1)
                    pe.wait_ge(hidden_ready, p + 1)
                    wait(pe, hiddenT_ready, p)
                    for c in range(IC):
                        m = M.transpose(ps[0:IW[c], 3, c * P:(c + 1) * P], hm[:, c * P:c * P + IW[c]], ident[:])
                    m.then_inc(hidden_turned, 1)
                    if q < Q - 1:
                        shared_in(i, 2 * q + 1, 1)
                    else:
                        shared_out(i, 2)
                    pe.wait_ge(hiddenT_ready, p + 1)
                    wait(pe, ya_ready, p)
                    wait(pe, yb_ready, p)
                    for c in range(IC):
                        for e in range(2):
                            m = M.matmul(ps[CAP * e:CAP * (e + 1), 4, :], hmT[0:IW[c], c, CAP * e:CAP * (e + 1)],
                                         wd[j][0:IW[c], e, c, :], start=(c == 0), stop=(c == IC - 1))
                    m.then_inc(down_done, 1)

            steps(pe, body)

        @block.scalar
        def _(act):
            A = nc.scalar
            act.wait_ge(staged[0], 32)
            for g in range(2):
                A.activation(sgu[:, 0, g].rearrange("p k i -> p (k i)"), stage[g], ACT.Copy).then_inc(shi_done, 1)
            act.wait_ge(staged[1], 16 * SC)
            for c in range(SC):
                m = A.activation(sd[0:SW[c], 0, c], staged_d[0:SW[c], c * D:(c + 1) * D], ACT.Copy)
            m.then_inc(shi_done, 1)

            def split_x2(i):
                act.wait_ge(x2_in, 16 * (i + 1))
                wait(act, s_up_done, SC * i)
                A.activation(x2s[:, 0], x2[:], ACT.Copy).then_inc(x2hi_ready, 1)

            def silu_shared(i, c):
                n = SC * i + c
                act.wait_ge(s_gate_done, n + 1)
                wait(act, s_mult_done, n)
                A.activation(ssil[0:SW[c], :], ps[0:SW[c], 5, 0:SEQ], ACT.Silu).then_inc(s_silu_done, 1)

            def hi_shared(i, c):
                n = SC * i + c
                act.wait_ge(s_mult_done, n + 1)
                if c == 0:
                    wait(act, s_down_done, NT * i)
                A.activation(hs[0:SW[c], 0, c, :], sh[0:SW[c], c % 2, :], ACT.Copy).then_inc(s_hi_done, 1)

            def body(i):
                for q in range(Q):
                    p = Q * i + q
                    if q == 0 and first(i):
                        split_x2(i)
                    if q == Q - 1 and not last(i):
                        split_x2(i + 1)
                    if q < Q - 1:
                        silu_shared(i, 2 * q)
                    act.wait_ge(gate_up_done, p + 1)
                    wait(act, hidden_ready, p)
                    A.activation(sil[:], ps[:, 1, 0:I], ACT.Silu).then_inc(silu_done, 1)
                    if q < Q - 1:
                        hi_shared(i, 2 * q)
                        silu_shared(i, 2 * q + 1)
                        hi_shared(i, 2 * q + 1)
                    act.wait_ge(down_done, p + 1)
                    wait(act, added, 16 * (adds_before(i, q) + 1))
                    A.activation(y[:, q % 2, 0, :], ps[0:CAP, 4, :], ACT.Copy).then_inc(ya_ready, 1)

            steps(act, body)

        @block.vector
        def _(dve):
            V = nc.vector
            V.memset(zeros[:], 0.0).then_inc(zeros_set, 1)
            for g in range(2):
                dve.wait_ge(shi_done, g + 1)
                V.tensor_tensor(sgu[:, 1, g].rearrange("p k i -> p (k i)"), stage[g],
                                sgu[:, 0, g].bitcast(F32).rearrange("p k i -> p (k i)"), ALU.subtract)\
                    .then_inc(slo_done, 1)
            dve.wait_ge(shi_done, 3)
            for c in range(SC):
                m = V.tensor_tensor(sd[0:SW[c], 1, c], staged_d[0:SW[c], c * D:(c + 1) * D],
                                    sd[0:SW[c], 0, c].bitcast(F32), ALU.subtract)
            m.then_inc(slo_done, 1)

            def split_x2(i):
                dve.wait_ge(x2hi_ready, i + 1)
                V.tensor_tensor(x2s[:, 1], x2[:], x2s[:, 0].bitcast(F32), ALU.subtract).then_inc(x2lo_ready, 1)

            def mult_shared(i, c):
                n = SC * i + c
                dve.wait_ge(s_silu_done, n + 1)
                dve.wait_ge(s_up_done, n + 1)
                wait(dve, s_hi_done, n - 1)
                V.tensor_tensor(sh[0:SW[c], c % 2, :], ssil[0:SW[c], :], ps[0:SW[c], 6, 0:SEQ], ALU.mult)\
                    .then_inc(s_mult_done, 1)

            def lo_shared(i, c):
                n = SC * i + c
                dve.wait_ge(s_hi_done, n + 1)
                V.tensor_tensor(hs[0:SW[c], 1, c, :], sh[0:SW[c], c % 2, :], hs[0:SW[c], 0, c, :].bitcast(F32),
                                ALU.subtract).then_inc(s_lo_done, 1)

            def out_shared(i, s):
                dve.wait_ge(s_down_done, NT * i + s + 1)
                wait(dve, added, 16 * adds_before(i, 2) if type(i) is not int or i > 0 else 0)
                V.tensor_copy(so[:, s, :], ps[:, 7, :]).then_inc(so_ready, 1)

            def body(i):
                for q in range(Q):
                    p = Q * i + q
                    j = q % 2
                    if q == 0 and first(i):
                        split_x2(i)
                    dve.wait_ge(rows_turned, p + 1)
                    wait(dve, gate_up_done, p)
                    V.tensor_copy(xgT[:].rearrange("p k t -> p (k t)"), ps[:, 0, :]).then_inc(rowsT_ready, 1)
                    V.tensor_copy(wcol[0:CAP, j:j + 1], xg[0:CAP, j, bass.ds(D + 2 * p, 1)])
                    V.tensor_copy(wcol[CAP:P, j:j + 1], xg[CAP:P, j, bass.ds(D + 2 * p + 1, 1)])\
                        .then_inc(wcol_ready, 1)
                    if q < Q - 1:
                        mult_shared(i, 2 * q)
                    else:
                        out_shared(i, 0)
                    dve.wait_ge(silu_done, p + 1)
                    dve.wait_ge(wcol_ready, p + 1)
                    wait(dve, hidden_turned, p)
                    V.scalar_tensor_tensor(out=hm[:], in0=sil[:], scalar=wcol[:, j:j + 1], in1=ps[:, 2, 0:I],
                                           op0=ALU.mult, op1=ALU.mult).then_inc(hidden_ready, 1)
                    if q == Q - 1:
                        out_shared(i, 1)
                        if not last(i):
                            split_x2(i + 1)
                    dve.wait_ge(hidden_turned, p + 1)
                    wait(dve, down_done, p)
                    V.tensor_copy(hmT[:, 0:IC - 1, :], ps[:, 3, 0:(IC - 1) * P].rearrange("p (c t) -> p c t", t=P))
                    V.tensor_copy(hmT[0:IW[-1], IC - 1, :], ps[0:IW[-1], 3, (IC - 1) * P:IC * P])\
                        .then_inc(hiddenT_ready, 1)
                    if q < Q - 1:
                        lo_shared(i, 2 * q)
                        mult_shared(i, 2 * q + 1)
                        lo_shared(i, 2 * q + 1)
                    else:
                        out_shared(i, 2)
                    dve.wait_ge(down_done, p + 1)
                    wait(dve, added, 16 * (adds_before(i, q) + 2))
                    V.tensor_copy(y[:, j, 1, :], ps[CAP:P, 4, :]).then_inc(yb_ready, 1)

            steps(dve, body)

        @block.gpsimd
        def _(pool):
            G = nc.gpsimd
            pool.wait_ge(table_in, 32)
            pool.wait_ge(pads_in, 32)

            def add_pair(n, p, jy, qix):
                for e in range(2):
                    wait(pool, added, 16 * (n + e))
                    wait_apart(pool, (ya_ready, yb_ready)[e], p + 1, carried)
                    G.indirect_dma_start(acc, bass.IndirectOffsetOnAxis(ap=scatter_ix[:, qix, e:e + 1], axis=0),
                                         y[:, jy, e, :], None, compute_op=ALU.add).then_inc(added, 16)

            def add_shared(n, i):
                pool.wait_ge(so_ready, NT * (i + 1))
                pool.wait_ge(added, 16 * n)
                G.dma_start(acc[bass.ds(i * SEQ, SEQ), :].rearrange("(s p) d -> p s d", p=P), so[:],
                            accum_op=ALU.add).then_inc(added, 16)

            def body(i):
                peeled = type(i) is int and i == 0
                for q in range(Q):
                    p = Q * i + q
                    j = q % 2
                    wait(pool, rows_in[j], 16 * (2 * i + q // 2))
                    wait(pool, rows_turned, p - 1)
                    wait(pool, wcol_ready, p - 1)
                    G.tensor_copy(gather_ix[:, q:q + 1], gather_all[:, bass.ds(p, 1)]).then_inc(gix_ready, 1)
                    wait_apart(pool, gix_ready, p + 1, carried)
                    G.indirect_dma_start(xg[:, j, :], None, xrow,
                                         bass.IndirectOffsetOnAxis(ap=gather_ix[:, q:q + 1], axis=0))\
                        .then_inc(rows_in[j], 16)
                    if not (peeled and q < 2):
                        add_pair(adds_before(i, q), p - 2, j, (q + 2) % Q)
                    G.tensor_copy(scatter_ix[:, q, :], scatter_all[:, bass.ds(2 * p, 2)]).then_inc(six_ready, 1)
                    pool.wait_ge(six_ready, p + 1)
                    if q == 1 and not peeled:
                        add_shared(adds_before(i, q) + 2, i - 1)

            steps(pool, body)
            n = adds_before(NSEQ, 0)
            for q in range(2):
                add_pair(n, PAIRS - 2 + q, q, Q - 2 + q)
                n += 2
            add_shared(n, NSEQ - 1)
            pool.wait_ge(added, 16 * (n + 1))


_INS = ['x', 'txt', 'L0_tok_log_dt', 'L0_tok_B_ri', 'L0_tok_inv_A_real', 'L0_tok_A_imag',
        'L0_attn_Wq', 'L0_attn_Wk', 'L0_attn_Wv', 'L0_attn_Wo', 'L0_ffn_gate_w',
        'L0_ffn_w_gate', 'L0_ffn_w_up', 'L0_ffn_w_down', 'L0_ffn_sw_gate', 'L0_ffn_sw_up', 'L0_ffn_sw_down']


def build(nc, a, out):
    B, S0, _, _ = a["x"].shape
    S1, D = a["txt"].shape[1:]
    SEQ = S0 + S1
    E = a["L0_ffn_gate_w"].shape[0]
    CAP = out.shape[0] - B * SEQ
    KC = D // P
    h = nc.dram_tensor("tokens_h", (B, S0, D), F32).ap()
    xrow = nc.dram_tensor("rows_scores", (B * SEQ + CAP, D + E), F32).ap()
    x2T = nc.dram_tensor("rows_turned", (B, P, KC, SEQ), F32).ap()
    table = nc.dram_tensor("slot_table", (E * CAP, 1), U32).ap()
    shared = [a["L0_ffn_sw_" + w] for w in ("gate", "up", "down")]
    with ExitStack() as outer:
        bulk = outer.enter_context(nc.sbuf_tensor("bulk", [P, 2 * 4 * (SEQ // P) * SEQ], F32))
        staged = [outer.enter_context(nc.semaphore("staged_" + w)) for w in ("gate_up", "down")]
        with ExitStack() as ctx:
            NX = sum(a["L0_attn_W" + w].shape[0] for w in "qkv")
            WxT = ctx.enter_context(nc.sbuf_tensor("WxT", [P, 2, KC, NX], F32R))
            WoT = ctx.enter_context(nc.sbuf_tensor("WoT", [P, 2, KC, D], F32R))
            gwT = ctx.enter_context(nc.sbuf_tensor("gwT", [P, KC, E], F32))
            state_space_phase(nc, a["x"], *[a["L0_tok_" + w] for w in ("log_dt", "B_ri", "inv_A_real", "A_imag")],
                              a["ident"], h, bulk, *[a["L0_attn_W" + w] for w in "qkvo"], a["L0_ffn_gate_w"],
                              WxT, WoT, gwT)
            attention_phase(nc, h, a["txt"], [a[w] for w in ("cos", "sin", "ident", "upper", "tok", "slot")],
                            WxT, WoT, gwT, out, xrow, x2T, table, a["empty"], bulk,
                            lambda sp: load_shared_weights(sp, bulk, staged, *shared))
        experts_phase(nc, out, xrow, x2T, table, *[a["L0_ffn_w_" + w] for w in ("gate", "up", "down")],
                      *shared, a["ident"], bulk, staged)


def kernel(**inputs):
    import concourse.bacc as bacc
    from concourse.bass_utils import run_bass_kernel_spmd

    nc = bacc.Bacc("TRN2", target_bir_lowering=False, num_devices=1, dynamic_dma_scratch_size=8192)
    B, S0 = inputs["x"].shape[:2]
    SEQ = S0 + inputs["txt"].shape[1]
    D = inputs["txt"].shape[2]
    CAP = 64
    arrays = {name: np.ascontiguousarray(inputs[name]) for name in _INS}
    arrays.update(shape_constants(B, SEQ, inputs["L0_ffn_gate_w"].shape[0], CAP))
    arrays = {f"in_{name}": np.ascontiguousarray(a) for name, a in arrays.items()}
    aps = {name[3:]: nc.dram_tensor(name, a.shape, mybir.dt.from_np(a.dtype), kind="ExternalInput").ap()
           for name, a in arrays.items()}
    out = nc.dram_tensor("out_rows", (B * SEQ + CAP, D), F32, kind="ExternalOutput").ap()
    build(nc, aps, out)
    r = run_bass_kernel_spmd(nc, [arrays], core_ids=[0])
    return r.results[0]["out_rows"][:B * SEQ].reshape(B, SEQ, D)
```
